# Optimizing a Trainium2 kernel written in Bass

```python
import numpy as np
import jax
import jax.numpy as jnp

def _softmax(x, axis=-1):
    return jax.nn.softmax(x, axis=axis)

def _gelu(x):
    return jax.nn.gelu(x, approximate=True)

def _silu(x):
    return jax.nn.silu(x)

def _sigmoid(x):
    return jax.nn.sigmoid(x)

def _layernorm(x, axis=-1, eps=1e-05):
    m = jnp.mean(x, axis=axis, keepdims=True)
    v = jnp.var(x, axis=axis, keepdims=True)
    return (x - m) / jnp.sqrt(v + eps)

def _scatter_add(tgt, idx, src, axis=0):
    return tgt.at[idx].add(src)

def _segment_sum(src, seg, n):
    return jax.ops.segment_sum(src, seg, n)
kernel_name = 'mk_perceiver_d1_seqx_r2_49ff15'

def setup_inputs(seed: int=0):
    np.random.seed(seed)
    _w = jnp.asarray

    def _rec_inputs():
        import jax
        import jax.numpy as jnp
        _rk = jax.random.key(seed)
        x = -0.000125 + 0.9999 * jax.random.normal(jax.random.fold_in(_rk, 1), (1, 512, 512), jnp.float32)
        _lenS = 512 - jax.random.randint(jax.random.fold_in(_rk, 7), (1,), 0, max(1, 512 // 4) + 1, jnp.int32)
        _lenS2 = 8192 - jax.random.randint(jax.random.fold_in(_rk, 8), (1,), 0, max(1, 8192 // 4) + 1, jnp.int32)
        _ctx_768P = jax.random.normal(jax.random.fold_in(_rk, 11), (1, 16, 384), jnp.float32)
        _ctx_768c = jax.random.dirichlet(jax.random.fold_in(_rk, 511), 0.3 * jnp.ones((16,), jnp.float32), (1, 8192))
        _ctx_768t = jnp.einsum('bsk,bkd->bsd', _ctx_768c, _ctx_768P)
        _ctx_768t = _ctx_768t * jax.lax.rsqrt(jnp.mean(jnp.square(_ctx_768t)) + 1e-12) * 0.953939
        ctx_768 = 0.00272024 + 0.999456 * (_ctx_768t + 0.3 * jax.random.normal(jax.random.fold_in(_rk, 611), (1, 8192, 384), jnp.float32))
        return (x, ctx_768)
    x, ctx_768 = _rec_inputs()

    def _L0_xattn_setup():
        import jax, jax.numpy as jnp
        import numpy as np
        HEADS = 16
        DIM_HEAD = 64
        SCALE = DIM_HEAD ** (-0.5)
        QUERY_DIM = 512
        CONTEXT_DIM = 384
        INNER_DIM = HEADS * DIM_HEAD
        key = jax.random.key(seed)
        ks = jax.random.split(key, 7)
        B, Nq, Nk = (8, 2048, 77)
        x = jax.random.normal(ks[0], (B, Nq, QUERY_DIM), dtype=jnp.float32)
        context = jax.random.normal(ks[1], (B, Nk, CONTEXT_DIM), dtype=jnp.float32)
        Wq = jax.random.normal(ks[2], (QUERY_DIM, INNER_DIM), dtype=jnp.float32) * QUERY_DIM ** (-0.5)
        Wk = jax.random.normal(ks[3], (CONTEXT_DIM, INNER_DIM), dtype=jnp.float32) * CONTEXT_DIM ** (-0.5)
        Wv = jax.random.normal(ks[4], (CONTEXT_DIM, INNER_DIM), dtype=jnp.float32) * CONTEXT_DIM ** (-0.5)
        Wo = jax.random.normal(ks[5], (INNER_DIM, QUERY_DIM), dtype=jnp.float32) * INNER_DIM ** (-0.5)
        bo = jnp.zeros((QUERY_DIM,), dtype=jnp.float32)
        return {'x': x, 'context': context, 'Wq': Wq, 'Wk': Wk, 'Wv': Wv, 'Wo': Wo, 'bo': bo}
    _L0_xattn_all = _L0_xattn_setup()
    _L0_xattn_in = {k: v for k, v in _L0_xattn_all.items() if k in ('Wq', 'Wk', 'Wv', 'Wo', 'bo')}
    del _L0_xattn_all

    def _L0_attn_setup():
        import jax, jax.numpy as jnp
        import numpy as np
        MODEL_DIM = 512
        NUM_HEADS = 16
        HEAD_DIM = MODEL_DIM // NUM_HEADS
        ROPE_PERIOD = 10000.0

        def _rope_cos_sin(seq_len, dim, dtype):
            inv_freq = 1.0 / ROPE_PERIOD ** (jnp.arange(0, dim, 2, dtype=jnp.float32) / dim)
            t = jnp.arange(seq_len, dtype=jnp.float32)
            freqs = jnp.outer(t, inv_freq)
            emb = jnp.concatenate([freqs, freqs], axis=-1)
            return (jnp.cos(emb).astype(dtype), jnp.sin(emb).astype(dtype))

        def _rope_embed(x):
            S, D = (x.shape[-2], x.shape[-1])
            cos, sin = _rope_cos_sin(S, D, x.dtype)
            x1 = x[..., :D // 2]
            x2 = x[..., D // 2:]
            rotated = jnp.concatenate([-x2, x1], axis=-1)
            return x * cos + rotated * sin
        key = jax.random.key(seed)
        kx, kq, kk, kv, ko = jax.random.split(key, 5)
        std = 0.02
        return {'x': jax.random.normal(kx, (2, 1024, MODEL_DIM), dtype=jnp.float32), 'Wq': std * jax.random.normal(kq, (MODEL_DIM, MODEL_DIM), dtype=jnp.float32), 'Wk': std * jax.random.normal(kk, (MODEL_DIM, MODEL_DIM), dtype=jnp.float32), 'Wv': std * jax.random.normal(kv, (MODEL_DIM, MODEL_DIM), dtype=jnp.float32), 'Wo': std * jax.random.normal(ko, (MODEL_DIM, MODEL_DIM), dtype=jnp.float32)}
    _L0_attn_all = _L0_attn_setup()
    _L0_attn_in = {k: v for k, v in _L0_attn_all.items() if k in ('Wq', 'Wk', 'Wv', 'Wo')}
    del _L0_attn_all

    def _L0_ffn_setup():
        import jax, jax.numpy as jnp
        import numpy as np
        D, H, E, K = (512, 512, 8, 2)

        def _moe(x, router_w, w_in, b_in, w_out, b_out):
            B, S, Dm = x.shape
            T = B * S
            x2 = x.reshape(T, Dm)
            logits = x2 @ router_w
            probs = jax.nn.softmax(logits, axis=-1)
            top_p, top_e = jax.lax.top_k(probs, K)
            flat_e = top_e.reshape(-1)
            flat_p = top_p.reshape(-1)
            tok = jnp.repeat(jnp.arange(T), K)
            order = jnp.argsort(flat_e)
            se, sp, st = (flat_e[order], flat_p[order], tok[order])
            xd = x2[st]
            N = xd.shape[0]
            h = jnp.zeros((N, H), x.dtype)
            for e in range(E):
                m = (se == e)[:, None]
                h = h + jnp.where(m, jax.nn.gelu(xd @ w_in[e] + b_in[e]), 0.0)
            y = jnp.zeros((N, Dm), x.dtype)
            for e in range(E):
                m = (se == e)[:, None]
                y = y + jnp.where(m, h @ w_out[e] + b_out[e], 0.0)
            y = y * sp[:, None]
            out = jnp.zeros((T, Dm), x.dtype).at[st].add(y)
            return out.reshape(B, S, Dm)
        key = jax.random.key(seed)
        ks = jax.random.split(key, 5)
        s = lambda k, shape, scale: jax.random.normal(k, shape, dtype=jnp.float32) * scale
        return {'input_batch': s(ks[0], (2, 256, D), 1.0), 'router_w': s(ks[1], (D, E), D ** (-0.5)), 'w_in': s(ks[2], (E, D, H), D ** (-0.5)), 'b_in': jnp.zeros((E, H), jnp.float32), 'w_out': s(ks[3], (E, H, D), H ** (-0.5)), 'b_out': jnp.zeros((E, D), jnp.float32)}
    _L0_ffn_all = _L0_ffn_setup()
    _L0_ffn_in = {k: v for k, v in _L0_ffn_all.items() if k in ('router_w', 'w_in', 'b_in', 'w_out', 'b_out')}
    del _L0_ffn_all
    return {'x': x, 'ctx_768': ctx_768, 'L0_xattn_Wq': _L0_xattn_in['Wq'], 'L0_xattn_Wk': _L0_xattn_in['Wk'], 'L0_xattn_Wv': _L0_xattn_in['Wv'], 'L0_xattn_Wo': _L0_xattn_in['Wo'], 'L0_xattn_bo': _L0_xattn_in['bo'], 'L0_attn_Wq': _L0_attn_in['Wq'], 'L0_attn_Wk': _L0_attn_in['Wk'], 'L0_attn_Wv': _L0_attn_in['Wv'], 'L0_attn_Wo': _L0_attn_in['Wo'], 'L0_ffn_router_w': _L0_ffn_in['router_w'], 'L0_ffn_w_in': _L0_ffn_in['w_in'], 'L0_ffn_b_in': _L0_ffn_in['b_in'], 'L0_ffn_w_out': _L0_ffn_in['w_out'], 'L0_ffn_b_out': _L0_ffn_in['b_out']}

def reference(x, ctx_768, L0_xattn_Wq, L0_xattn_Wk, L0_xattn_Wv, L0_xattn_Wo, L0_xattn_bo, L0_attn_Wq, L0_attn_Wk, L0_attn_Wv, L0_attn_Wo, L0_ffn_router_w, L0_ffn_w_in, L0_ffn_b_in, L0_ffn_w_out, L0_ffn_b_out):
    import jax
    import jax.numpy as jnp

    def _L0_xattn_ref(x, context, Wq, Wk, Wv, Wo, bo):
        import jax, jax.numpy as jnp
        import numpy as np
        HEADS = 16
        DIM_HEAD = 64
        SCALE = DIM_HEAD ** (-0.5)
        QUERY_DIM = 512
        CONTEXT_DIM = 384
        INNER_DIM = HEADS * DIM_HEAD
        B, Nq, _ = x.shape
        Nk = context.shape[1]
        q = x @ Wq
        k = context @ Wk
        v = context @ Wv
        q = q.reshape(B, Nq, HEADS, DIM_HEAD).transpose(0, 2, 1, 3)
        k = k.reshape(B, Nk, HEADS, DIM_HEAD).transpose(0, 2, 1, 3)
        v = v.reshape(B, Nk, HEADS, DIM_HEAD).transpose(0, 2, 1, 3)
        sim = jnp.einsum('bhid,bhjd->bhij', q, k) * SCALE
        attn = jax.nn.softmax(sim, axis=-1)
        out = jnp.einsum('bhij,bhjd->bhid', attn, v)
        out = out.transpose(0, 2, 1, 3).reshape(B, Nq, INNER_DIM)
        return out @ Wo + bo

    def _L0_attn_ref(x, Wq, Wk, Wv, Wo):
        import jax, jax.numpy as jnp
        import numpy as np
        MODEL_DIM = 512
        NUM_HEADS = 16
        HEAD_DIM = MODEL_DIM // NUM_HEADS
        ROPE_PERIOD = 10000.0

        def _rope_cos_sin(seq_len, dim, dtype):
            inv_freq = 1.0 / ROPE_PERIOD ** (jnp.arange(0, dim, 2, dtype=jnp.float32) / dim)
            t = jnp.arange(seq_len, dtype=jnp.float32)
            freqs = jnp.outer(t, inv_freq)
            emb = jnp.concatenate([freqs, freqs], axis=-1)
            return (jnp.cos(emb).astype(dtype), jnp.sin(emb).astype(dtype))

        def _rope_embed(x):
            S, D = (x.shape[-2], x.shape[-1])
            cos, sin = _rope_cos_sin(S, D, x.dtype)
            x1 = x[..., :D // 2]
            x2 = x[..., D // 2:]
            rotated = jnp.concatenate([-x2, x1], axis=-1)
            return x * cos + rotated * sin
        B, S, Dm = x.shape
        H, Dh = (NUM_HEADS, HEAD_DIM)
        q = (x @ Wq.T).reshape(B, S, H, Dh).transpose(0, 2, 1, 3)
        k = (x @ Wk.T).reshape(B, S, H, Dh).transpose(0, 2, 1, 3)
        v = (x @ Wv.T).reshape(B, S, H, Dh).transpose(0, 2, 1, 3)
        q = _rope_embed(q)
        k = _rope_embed(k)
        scores = jnp.einsum('bhqd,bhkd->bhqk', q, k) / jnp.sqrt(jnp.asarray(Dh, x.dtype))
        neg_inf = jnp.finfo(x.dtype).min
        causal = jnp.triu(jnp.full((S, S), neg_inf, dtype=x.dtype), k=1)
        scores = scores + causal
        attn = jax.nn.softmax(scores, axis=-1)
        out = jnp.einsum('bhqk,bhkd->bhqd', attn, v)
        out = out.transpose(0, 2, 1, 3).reshape(B, S, Dm)
        return out @ Wo.T

    def _L0_ffn_ref(input_batch, router_w, w_in, b_in, w_out, b_out):
        import jax, jax.numpy as jnp
        import numpy as np
        D, H, E, K = (512, 512, 8, 2)

        def _moe(x, router_w, w_in, b_in, w_out, b_out):
            B, S, Dm = x.shape
            T = B * S
            x2 = x.reshape(T, Dm)
            logits = x2 @ router_w
            probs = jax.nn.softmax(logits, axis=-1)
            top_p, top_e = jax.lax.top_k(probs, K)
            flat_e = top_e.reshape(-1)
            flat_p = top_p.reshape(-1)
            tok = jnp.repeat(jnp.arange(T), K)
            order = jnp.argsort(flat_e)
            se, sp, st = (flat_e[order], flat_p[order], tok[order])
            xd = x2[st]
            N = xd.shape[0]
            h = jnp.zeros((N, H), x.dtype)
            for e in range(E):
                m = (se == e)[:, None]
                h = h + jnp.where(m, jax.nn.gelu(xd @ w_in[e] + b_in[e]), 0.0)
            y = jnp.zeros((N, Dm), x.dtype)
            for e in range(E):
                m = (se == e)[:, None]
                y = y + jnp.where(m, h @ w_out[e] + b_out[e], 0.0)
            y = y * sp[:, None]
            out = jnp.zeros((T, Dm), x.dtype).at[st].add(y)
            return out.reshape(B, S, Dm)
        return _moe(input_batch, router_w, w_in, b_in, w_out, b_out)
    x = x + _L0_xattn_ref(_layernorm(x, axis=-1), ctx_768, L0_xattn_Wq, L0_xattn_Wk, L0_xattn_Wv, L0_xattn_Wo, L0_xattn_bo)
    x = x + _L0_attn_ref(_layernorm(x, axis=-1), L0_attn_Wq, L0_attn_Wk, L0_attn_Wv, L0_attn_Wo)
    x = x + _L0_ffn_ref(_layernorm(x, axis=-1), L0_ffn_router_w, L0_ffn_w_in, L0_ffn_b_in, L0_ffn_w_out, L0_ffn_b_out)
    return x

_drawn_inputs = setup_inputs


def setup_inputs(seed=0):
    import zlib

    import numpy as np

    out = dict(_drawn_inputs(seed))
    spreads = {'L0_xattn_bo': (0.0, 0.1), 'L0_ffn_b_in': (0.0, 0.316), 'L0_ffn_b_out': (0.0, 0.1)}
    factors = {'L0_attn_Wq': 8.0, 'L0_attn_Wk': 7.905}
    for name, (base, spread) in spreads.items():
        noise = np.random.default_rng([zlib.crc32(name.encode()), seed]).standard_normal(out[name].shape)
        drawn = base * np.exp(spread * noise) if base else spread * noise
        out[name] = jnp.asarray(drawn.astype(out[name].dtype))
    for name, factor in factors.items():
        out[name] = (out[name] * factor).astype(out[name].dtype)
    return out
```

```python
import math
from contextlib import ExitStack

import concourse.bass as bass
import numpy as np
from concourse import mybir

F32 = mybir.dt.float32
F16 = mybir.dt.float16
ALU = mybir.AluOpType
ACT = mybir.ActivationFunctionType
X_AXIS = mybir.AxisListType.X

P = 128
D = 512
T = 512
QT = T // P
DT = D // P
EPS = 1e-5

NKEY = 8192
CTX = 384
CT = CTX // P
HX = 16
DH = 64
PAIRS = HX // 2
CHUNK = 2048
NCHUNK = NKEY // CHUNK
KB = CHUNK // P
DUOS = KB // 2
STEPS = 2 * DUOS
KT = CHUNK // 512
VW = 2 * DH + 1

CTX_SCALE = 16.0
W_SCALE = 256.0
KV_SCALE = 16.0
Q_SCALE = 16.0
P_SCALE = 256.0
M_UNIT = 64.0
KV_EVAC = KV_SCALE / (CTX_SCALE * W_SCALE)
EXP_SCALE = 1.0 / (Q_SCALE * KV_SCALE * math.sqrt(DH))

HS = 16
DS = D // HS

E = 8
H = 512

RING = 4
HEAD = 4


def job_plan():
    maxes = [[("M", h, q, k) for q in range(QT) for k in range(KT)] for h in range(2)]
    a, b = maxes
    steps = [[("K", k)] for k in range(KT)]
    for v, n in zip(range(KT), (2, 2, 2, 1)):
        steps.append([("V", v)] + [a.pop(0) for _ in range(n)])
        if v < KT - 1:
            steps.append([a.pop(0) for _ in range(3)])
    steps[-1] += [b.pop(0)]
    steps.append([b.pop(0) for _ in range(3)])
    steps.append([("R", 0)] + [b.pop(0) for _ in range(2)])
    steps += [[b.pop(0) for _ in range(3)] for _ in range(2)]
    steps.append([b.pop(0) for _ in range(4)])
    assert not a and not b and len(steps) == STEPS
    return steps


PLAN = job_plan()
JOBS = sum(map(len, PLAN)) + 1
JOB_AT = {}
for _step in PLAN:
    for _job in _step:
        JOB_AT[_job] = len(JOB_AT)
JOB_AT[("R", 1)] = JOBS - 1
LAST_MAX = [("M", h, QT - 1, KT - 1) for h in range(2)]
W_SPLIT_STEP = 12


def one_of(n):
    return slice(n, n + 1) if isinstance(n, int) else bass.ds(n, 1)


def layer_norm_rows(nc, dve, x, xn, stats, mv, rs, ln_step, root):
    for t in range(QT):
        i = nc.vector.bn_stats(stats[:, t, :], x[:, t, :])
    i.then_inc(ln_step, 1)
    dve.wait_ge(ln_step, 1)
    for t in range(QT):
        i = nc.vector.bn_aggr(mv[:, t, :], stats[:, t, :])
    i.then_inc(ln_step, 1)
    dve.wait_ge(ln_step, 2)
    nc.vector.tensor_scalar(rs[:, 0, :], mv[:, :, 1], EPS, None, ALU.add).then_inc(ln_step, 1)
    dve.wait_ge(root, 1)
    nc.vector.reciprocal(rs[:, 2, :], rs[:, 1, :]).then_inc(ln_step, 1)
    dve.wait_ge(ln_step, 4)
    nc.vector.tensor_tensor(rs[:, 3, :], rs[:, 2, :], rs[:, 2, :], ALU.mult).then_inc(ln_step, 1)
    dve.wait_ge(ln_step, 5)
    nc.vector.tensor_tensor(rs[:, 4, :], rs[:, 3, :], rs[:, 0, :], ALU.mult).then_inc(ln_step, 1)
    dve.wait_ge(ln_step, 6)
    nc.vector.tensor_scalar(rs[:, 5, :], rs[:, 4, :], -0.5, 1.5, ALU.mult, ALU.add).then_inc(ln_step, 1)
    dve.wait_ge(ln_step, 7)
    nc.vector.tensor_tensor(rs[:, 6, :], rs[:, 5, :], rs[:, 2, :], ALU.mult).then_inc(ln_step, 1)
    dve.wait_ge(ln_step, 8)
    for t in range(QT):
        i = nc.vector.tensor_scalar(xn[:, t, :], x[:, t, :], mv[:, t, 0:1], rs[:, 6, t:t + 1],
                                    ALU.subtract, ALU.mult)
    i.then_inc(ln_step, 1)


LN_VAR = 3
LN_DONE = 9


def prologue(nc, a, dram, keep):
    with ExitStack() as ctx:
        sb = lambda name, shape, dt=F32: ctx.enter_context(nc.sbuf_tensor(name, shape, dt))
        sem = lambda name: ctx.enter_context(nc.semaphore(name))
        PIECE = 512
        NPIECE = NKEY // PIECE
        raw = sb("ctx_raw", [P, 2, CT, PIECE])
        x = sb("x_in", [P, QT, D])
        xn = sb("xn", [P, QT, D])
        xnT = sb("xnT", [P, DT, T])
        wq = sb("wq", [P, DT, HX * DH])
        qout = sb("qout", [P, 2, T])
        stats = sb("stats", [P, QT, 6])
        mv = sb("mv", [P, QT, 2])
        rs = sb("rs", [P, 7, QT])
        ps = [ctx.enter_context(nc.psum_tensor(f"pp{i}", [P, 512], F32)) for i in range(4)]
        x_loaded, wq_loaded = sem("x_loaded"), sem("wq_loaded")
        q_stored = [sem("q_stored0"), sem("q_stored1")]
        raw_loaded = [sem("raw_loaded0"), sem("raw_loaded1")]
        ctx_hi, ctx_lo = sem("ctx_hi"), sem("ctx_lo")
        ln_step, root = sem("ln_step"), sem("root")
        turned, turned_out = sem("turned"), sem("turned_out")
        q_ready, q_out = sem("q_ready"), sem("q_out")
        ident_set = sem("ident_set")
        with nc.Block() as block:

            @block.sync
            def _(sp):
                sp.dma_start(x[:], a["x"][0].rearrange("(t p) d -> p t d", p=P)).then_inc(x_loaded, 16)
                sp.dma_start(wq[:], a["L0_xattn_Wq"].rearrange("(k p) n -> p k n", p=P)).then_inc(wq_loaded, 16)
                for n in range(NPIECE):
                    if n >= 2:
                        sp.wait_ge(ctx_lo, n - 1)
                    sp.dma_start(raw[:, n % 2], a["ctxT"].rearrange("(k p) n -> p k n", p=P)[
                        :, :, n * PIECE:(n + 1) * PIECE]).then_inc(raw_loaded[n % 2], 16)

            @block.gpsimd
            def _(pool):
                nc.gpsimd.memset(keep.ident[:], 0.0).then_inc(ident_set, 1)
                nc.gpsimd.memset(keep.ident16[:], 0.0).then_inc(ident_set, 1)
                pool.wait_ge(ident_set, 2)
                for m in (keep.ident, keep.ident16):
                    nc.gpsimd.affine_select(out=m[:], in_=m[:], compare_op=ALU.not_equal, fill=1.0, base=0,
                                            pattern=[[-1, P]], channel_multiplier=1).then_inc(ident_set, 1)

            @block.scalar
            def _(act):
                act.wait_ge(ln_step, LN_VAR)
                nc.scalar.activation(rs[:, 1, :], rs[:, 0, :], ACT.Sqrt).then_inc(root, 1)
                for n in range(NPIECE):
                    act.wait_ge(raw_loaded[n % 2], 16 * (n // 2 + 1))
                    nc.scalar.activation(keep.ctx[:, 0, :, n * PIECE:(n + 1) * PIECE], raw[:, n % 2], ACT.Copy,
                                         scale=CTX_SCALE).then_inc(ctx_hi, 1)
                for n in range(PAIRS):
                    act.wait_ge(q_ready, n + 1)
                    if n >= 2:
                        act.wait_ge(q_stored[n % 2], 16 * (n // 2))
                    nc.scalar.activation(qout[:, n % 2, :], ps[n % 4][:], ACT.Copy).then_inc(q_out, 1)
                    act.wait_ge(q_out, n + 1)
                    act.dma_start(dram.q[n], qout[:, n % 2, :]).then_inc(q_stored[n % 2], 16)
                for s in q_stored:
                    act.wait_ge(s, 16 * PAIRS // 2)

            @block.vector
            def _(dve):
                dve.wait_ge(x_loaded, 16)
                layer_norm_rows(nc, dve, x, xn, stats, mv, rs, ln_step, root)
                for t in range(DT):
                    dve.wait_ge(turned, t + 1)
                    nc.vector.tensor_copy(xnT[:, t, :], ps[t][:]).then_inc(turned_out, 1)
                for n in range(NPIECE):
                    dve.wait_ge(ctx_hi, n + 1)
                    nc.vector.scalar_tensor_tensor(
                        out=keep.ctx[:, 1, :, n * PIECE:(n + 1) * PIECE], in0=raw[:, n % 2], scalar=CTX_SCALE,
                        in1=keep.ctx[:, 0, :, n * PIECE:(n + 1) * PIECE], op0=ALU.mult,
                        op1=ALU.subtract).then_inc(ctx_lo, 1)

            @block.tensor
            def _(pe):
                pe.wait_ge(ident_set, 4)
                pe.wait_ge(ln_step, LN_DONE)
                for d in range(DT):
                    for t in range(QT):
                        i = nc.tensor.transpose(ps[d][:, t * P:(t + 1) * P], xn[:, t, d * P:(d + 1) * P],
                                                keep.ident[:])
                    i.then_inc(turned, 1)
                pe.wait_ge(wq_loaded, 16)
                pe.wait_ge(turned_out, DT)
                for n in range(PAIRS):
                    if n >= 4:
                        pe.wait_ge(q_out, n - 3)
                    for k in range(DT):
                        i = nc.tensor.matmul(ps[n % 4][:], wq[:, k, n * P:(n + 1) * P], xnT[:, k, :],
                                             start=(k == 0), stop=(k == DT - 1))
                    i.then_inc(q_ready, 1)


def cross_attention(nc, a, dram, keep):
    with ExitStack() as ctx:
        sb = lambda name, shape, dt=F32: ctx.enter_context(nc.sbuf_tensor(name, shape, dt))
        sem = lambda name: ctx.enter_context(nc.semaphore(name))
        C = keep.ctx
        SA = sb("sa", [P, 2, 2, CHUNK], F16)
        SB = sb("sb", [P, 2, 2, CHUNK], F16)
        VT = sb("vt", [P, 2, KB, 2, VW], F16)
        QA = sb("qa", [P, 2, 2, T], F16)
        MB = sb("mb", [P, 2, 2, T], F16)
        w_raw = sb("w_raw", [P, 2, CT, P])
        w_hl = sb("w_hl", [P, 2, 2, CT, P], F16)
        q_raw = sb("q_raw", [P, T])
        p32 = sb("p32", [P, 2, 1024])
        ph = sb("ph", [P, RING, 1024], F16)
        pl = sb("pl", [P, RING, 1024], F16)
        acc = sb("acc", [P, 2, 2, 2, DH + 1])
        out = sb("out", [P, QT, 2, DH])
        rec = sb("rec", [P, 2, 2, 2])
        cmx = sb("cmx", [P, 2, QT, KT])
        cm = sb("cm", [P, 2, QT])
        m16 = sb("m16", [P, 2, 2, QT], F16)
        md = sb("md", [P, 2, QT])
        corr = sb("corr", [P, 2, 2, QT])
        ln_p = sb("ln_p", [P, 1])
        spair = [ctx.enter_context(nc.psum_tensor(f"scores{i}", [P, 2, 512], F32)) for i in range(2)]
        work = [ctx.enter_context(nc.psum_tensor(f"work{i}", [P, 512], F32)) for i in range(2)]
        O = ctx.enter_context(nc.psum_tensor("pv", [P, 2, 512], F32))
        O_view = O[:, :, 0:2 * VW].rearrange("p b (t n) -> p b t n", n=VW)

        scores_ready, exp_done, ph_ready = sem("scores_ready"), sem("exp_done"), sem("ph_ready")
        pl_ready, av_done, o_free = sem("pl_ready"), sem("av_done"), sem("o_free")
        job_filled, job_free, out_stored = sem("job_filled"), sem("job_free"), sem("out_stored")
        hi_ready, corr_ready = sem("hi_ready"), sem("corr_ready")
        cm_ready, m_ready, md_ready = sem("cm_ready"), sem("m_ready"), sem("md_ready")
        w_loaded, w_hi, w_split = sem("w_loaded"), sem("w_hi"), sem("w_split")
        q_loaded, q_hi, q_set = sem("q_loaded"), sem("q_hi"), sem("q_set")
        o_part, out_rec, out_norm = sem("o_part"), sem("out_rec"), sem("out_norm")
        consts_set = sem("consts_set")

        def after(n):
            return n + 1 + HEAD

        def k_rows(h):
            return (slice(0, DH), slice(DH, P)) if h == 0 else (slice(DH, P), slice(0, DH))

        def chunk_steps(p, last):
            for c in range(NCHUNK):
                for d in range(STEPS):
                    none = last and c == NCHUNK - 1
                    yield c, d, p * NCHUNK + c, None if none else (c + 1) % NCHUNK

        def corr_count(item_pair, c, h):
            return (item_pair * (NCHUNK - 1) + c - 1) * 2 + h + 1

        with nc.Block() as block:

            @block.sync
            def _(sp):
                def load_w(p):
                    for n, w in enumerate(("wk_pairs", "wv_pairs")):
                        sp.dma_start(w_raw[:, n].rearrange("p k n -> p (k n)"),
                                     a[w][one_of(p)].rearrange("a p n -> (a p) n")).then_inc(w_loaded, 16)

                def load_q(p):
                    sp.dma_start(q_raw[:], dram.q[one_of(p)].rearrange("a p n -> (a p) n")).then_inc(q_loaded, 16)

                def pair(p, last):
                    if not last:
                        sp.wait_ge(w_split, p + 1)
                        load_w(p + 1)
                        sp.wait_ge(q_set, 2 * p + 2)
                        load_q(p + 1)
                    sp.wait_ge(out_norm, p + 1)
                    sp.dma_start(dram.o[one_of(p)].rearrange("a p n -> (a p) n"),
                                 out[:].rearrange("p t h d -> p (t h d)")).then_inc(out_stored, 16)

                sp.sem_inc(out_stored, HEAD)
                load_w(0)
                load_q(0)
                with sp.Fori(0, PAIRS - 1) as p:
                    pair(p, False)
                pair(PAIRS - 1, True)
                sp.wait_ge(out_stored, 16 * PAIRS + HEAD)

            @block.gpsimd
            def _(pool):
                nc.gpsimd.memset(ln_p[:], math.log(P_SCALE)).then_inc(consts_set, 1)
                nc.gpsimd.memset(VT[:, :, :, :, DH:DH + 1], 1.0).then_inc(consts_set, 1)
                pool.wait_ge(consts_set, 2)
                nc.gpsimd.memset(SB[DH:DH + 1], M_UNIT).then_inc(consts_set, 1)

            @block.tensor
            def _(pe):
                def job(item, c, job):
                    n = JOB_AT[job]
                    W = work[n % 2]
                    par = c % 2
                    pe.wait_ge(job_free, after(item * JOBS + n - 2))
                    if job[0] == "K":
                        keys = slice(c * CHUNK + job[1] * 512, c * CHUNK + (job[1] + 1) * 512)
                        for k in range(CT):
                            for w, x in [(0, 0), (0, 1), (1, 0)]:
                                i = nc.tensor.matmul(W[:], w_hl[:, 0, w, k, :], C[:, x, k, keys],
                                                     start=(k == 0 and (w, x) == (0, 0)),
                                                     stop=(k == CT - 1 and (w, x) == (1, 0)))
                    elif job[0] == "V":
                        for b in range(4):
                            k0 = c * CHUNK + (job[1] * 4 + b) * P
                            for k in range(CT):
                                for x, w in [(0, 0), (0, 1), (1, 0)]:
                                    i = nc.tensor.matmul(W[:, b * P:(b + 1) * P], C[:, x, k, k0:k0 + P],
                                                         w_hl[:, 1, w, k, :],
                                                         start=(k == 0 and (x, w) == (0, 0)),
                                                         stop=(k == CT - 1 and (x, w) == (1, 0)))
                    elif job[0] == "M":
                        _, h, q, kt = job
                        if (q, kt) == (0, 0):
                            pe.wait_ge(job_free, after(item * JOBS + JOB_AT[("K", KT - 1)]))
                        i = nc.tensor.matmul(W[:], QA[:, par, h, q * P:(q + 1) * P],
                                             SA[:, par, h, kt * 512:(kt + 1) * 512], start=True, stop=True)
                    else:
                        h = job[1]
                        pe.wait_ge(m_ready, 2 * item + h + 1)
                        for q in range(QT):
                            i = nc.tensor.matmul(W[0:1, q * P:(q + 1) * P], m16[:, par, h, q:q + 1],
                                                 keep.ident16[:], start=True, stop=True)
                    i.then_inc(job_filled, 1)

                def scores(item, c, d):
                    g = item * STEPS + d
                    h, par = d // DUOS, c % 2
                    if d % DUOS == 0:
                        pe.wait_ge(job_free, after(item * JOBS + JOB_AT[("R", h)]))
                    pe.wait_ge(exp_done, after(g - 2))
                    for b in range(2):
                        kb = (d % DUOS) * 2 + b
                        nc.tensor.matmul(spair[d % 2][:, b, :], SA[:, par, h, kb * P:(kb + 1) * P],
                                         QA[:, par, h, :], start=True, stop=False)
                        i = nc.tensor.matmul(spair[d % 2][:, b, :], SB[0:DH + 1, par, h, kb * P:(kb + 1) * P],
                                             MB[0:DH + 1, par, h, :], start=False, stop=True)
                    i.then_inc(scores_ready, 1)

                def weigh(item, c, d):
                    g = item * STEPS + d
                    h, par, at = d // DUOS, c % 2, d % RING
                    if d % DUOS == 0:
                        pe.wait_ge(o_free, after(2 * item + h - 1))
                    pe.wait_ge(pl_ready, after(g))
                    for b in range(2):
                        kb = (d % DUOS) * 2 + b
                        for q in range(QT):
                            o = (q % 2) * VW
                            cols = slice(b * T + q * P, b * T + (q + 1) * P)
                            nc.tensor.matmul(O[:, q // 2, o:o + VW], ph[:, at, cols], VT[:, par, kb, h, :],
                                             start=(kb == 0 and q % 2 == 0), stop=False, skip_group_check=True)
                            i = nc.tensor.matmul(O[:, q // 2, o:o + DH + 1], pl[:, at, cols],
                                                 VT[:, par, kb, h, 0:DH + 1], start=False,
                                                 stop=(kb == KB - 1), skip_group_check=True)
                    i.then_inc(av_done, 1)

                def pair(p, last):
                    for c, d, item, nxt in chunk_steps(p, last):
                        if d == 0:
                            job(item, c, ("R", 1))
                        scores(item, c, d)
                        if nxt is not None:
                            if nxt == 0 and d == 0:
                                pe.wait_ge(w_split, p + 2)
                            if nxt < 2 and d == KT:
                                pe.wait_ge(q_set, 2 * p + (3 if nxt == 0 else 2))
                            for j in PLAN[d]:
                                job(item + 1, nxt, j)
                        s = c * STEPS + d - 2
                        if s >= 0:
                            weigh(p * NCHUNK + s // STEPS, s // STEPS, s % STEPS)
                    for d in (STEPS - 2, STEPS - 1):
                        weigh(p * NCHUNK + NCHUNK - 1, NCHUNK - 1, d)

                for s in (scores_ready, av_done, job_filled):
                    pe.sem_inc(s, HEAD)
                pe.wait_ge(consts_set, 3)
                pe.wait_ge(w_split, 1)
                pe.wait_ge(q_set, 1)
                for step in PLAN:
                    for j in step:
                        job(0, 0, j)
                with pe.Fori(0, PAIRS - 1) as p:
                    pair(p, False)
                pair(PAIRS - 1, True)

            @block.scalar
            def _(act):
                def w_high(p, first=False):
                    act.wait_ge(w_loaded, 32 * p + 32)
                    if not first:
                        act.wait_ge(job_filled, after((p * NCHUNK - 1) * JOBS + JOB_AT[("V", KT - 1)]))
                    for n in range(2):
                        i = nc.scalar.activation(w_hl[:, n, 0], w_raw[:, n], ACT.Copy, scale=W_SCALE)
                    i.then_inc(w_hi, 1)

                def q_high(p, par):
                    act.wait_ge(q_loaded, 16 * p + 16)
                    for h in range(2):
                        for rows in (slice(0, DH), slice(DH, P)):
                            i = nc.scalar.activation(QA[rows, par, h, :], q_raw[h * DH:(h + 1) * DH, :], ACT.Copy,
                                                     scale=Q_SCALE)
                    i.then_inc(q_hi, 1)

                def job(p, item, c, job):
                    n = JOB_AT[job]
                    W = work[n % 2]
                    par = c % 2
                    if job[0] == "K":
                        keys = slice(job[1] * 512, (job[1] + 1) * 512)
                        act.wait_ge(job_filled, after(item * JOBS + n))
                        nc.scalar.activation(SA[0:DH, par, 0, keys], W[0:DH, :], ACT.Copy, scale=KV_EVAC)
                        nc.scalar.activation(SB[0:DH, par, 0, keys], W[0:DH, :], ACT.Copy,
                                             scale=KV_EVAC).then_inc(hi_ready, 1)
                        nc.scalar.activation(SB[0:DH, par, 1, keys], W[DH:P, :], ACT.Copy, scale=KV_EVAC)
                        nc.scalar.activation(SA[DH:P, par, 1, keys], W[DH:P, :], ACT.Copy,
                                             scale=KV_EVAC).then_inc(hi_ready, 1)
                    elif job[0] == "V":
                        act.wait_ge(job_filled, after(item * JOBS + n))
                        v = VT[:, par, job[1] * 4:(job[1] + 1) * 4].rearrange("p k h n -> p (k h) n")
                        nc.scalar.activation(v[:, :, 0:DH], W[:].rearrange("p (k n) -> p k n", n=DH), ACT.Copy,
                                             scale=KV_EVAC).then_inc(hi_ready, 1)
                    elif job[0] == "R" and c > 0:
                        h = job[1]
                        act.wait_ge(md_ready, corr_count(p, c, h))
                        nc.scalar.activation(corr[:, par, h, :], md[:, h, :], ACT.Exp,
                                             scale=M_UNIT * EXP_SCALE).then_inc(corr_ready, 1)

                def step(g, d):
                    act.wait_ge(scores_ready, after(g))
                    act.wait_ge(pl_ready, after(g - 2))
                    nc.scalar.activation(p32[:, d % 2, :], spair[d % 2][:].rearrange("p b n -> p (b n)"), ACT.Exp,
                                         bias=ln_p[:], scale=EXP_SCALE).then_inc(exp_done, 1)

                def high(g, d):
                    act.wait_ge(av_done, after(g - RING))
                    act.wait_ge(exp_done, after(g))
                    nc.scalar.activation(ph[:, d % RING, :], p32[:, d % 2, :], ACT.Copy).then_inc(ph_ready, 1)

                def pair(p, last):
                    for c, d, item, nxt in chunk_steps(p, last):
                        g = item * STEPS + d
                        step(g, d)
                        if d == 0:
                            job(p, item, c, ("R", 1))
                        if nxt is not None:
                            if nxt < 2 and d == 0:
                                act.wait_ge(scores_ready, after(item * STEPS - 1))
                                q_high(p + 1 if nxt == 0 else p, nxt)
                            for j in PLAN[d]:
                                job(p + 1 if nxt == 0 else p, item + 1, nxt, j)
                            if nxt == NCHUNK - 1 and d == W_SPLIT_STEP and not last:
                                w_high(p + 1)
                        high(g, d)

                for s in (exp_done, ph_ready):
                    act.sem_inc(s, HEAD)
                act.wait_ge(consts_set, 3)
                w_high(0, first=True)
                q_high(0, 0)
                for s in PLAN:
                    for j in s:
                        job(0, 0, 0, j)
                with act.Fori(0, PAIRS - 1) as p:
                    pair(p, False)
                pair(PAIRS - 1, True)

            @block.vector
            def _(dve):
                def w_low(p):
                    dve.wait_ge(w_hi, p + 1)
                    for n in range(2):
                        i = nc.vector.scalar_tensor_tensor(out=w_hl[:, n, 1], in0=w_raw[:, n], scalar=W_SCALE,
                                                           in1=w_hl[:, n, 0], op0=ALU.mult, op1=ALU.subtract)
                    i.then_inc(w_split, 1)

                def q_low(n, par):
                    dve.wait_ge(q_hi, n)
                    for h in range(2):
                        rows = slice(h * DH, (h + 1) * DH)
                        i = nc.vector.scalar_tensor_tensor(out=MB[0:DH, par, h, :], in0=q_raw[rows, :], scalar=Q_SCALE,
                                                           in1=QA[rows, par, h, :], op0=ALU.mult, op1=ALU.subtract)
                    i.then_inc(q_set, 1)

                def new_maximum(p, item, c, h):
                    par = c % 2
                    dve.wait_ge(job_free, after(item * JOBS + JOB_AT[LAST_MAX[h]]))
                    nc.vector.tensor_reduce(cm[:, h, :], cmx[:, h], X_AXIS, ALU.max).then_inc(cm_ready, 1)
                    dve.wait_ge(cm_ready, 2 * item + h + 1)
                    if c == 0:
                        nc.vector.tensor_scalar(m16[:, par, h, :], cm[:, h, :], 1.0 / M_UNIT, None,
                                                ALU.mult).then_inc(m_ready, 1)
                        return
                    nc.vector.scalar_tensor_tensor(out=m16[:, par, h, :], in0=cm[:, h, :], scalar=1.0 / M_UNIT,
                                                   in1=m16[:, 1 - par, h, :], op0=ALU.mult,
                                                   op1=ALU.max).then_inc(m_ready, 1)
                    dve.wait_ge(m_ready, 2 * item + h + 1)
                    nc.vector.tensor_tensor(md[:, h, :], m16[:, 1 - par, h, :], m16[:, par, h, :],
                                            ALU.subtract).then_inc(md_ready, 1)

                def job(p, item, c, job):
                    n = JOB_AT[job]
                    W = work[n % 2]
                    par = c % 2
                    if job[0] == "K":
                        keys = slice(job[1] * 512, (job[1] + 1) * 512)
                        for h in range(2):
                            hi, lo = k_rows(h)
                            dve.wait_ge(hi_ready, item * 3 * KT + 2 * job[1] + h + 1)
                            i = nc.vector.scalar_tensor_tensor(
                                out=SA[lo, par, h, keys], in0=W[hi, :], scalar=KV_EVAC, in1=SA[hi, par, h, keys],
                                op0=ALU.mult, op1=ALU.subtract)
                        i.then_inc(job_free, 1)
                    elif job[0] == "V":
                        dve.wait_ge(hi_ready, item * 3 * KT + 2 * KT + job[1] + 1)
                        v = VT[:, par, job[1] * 4:(job[1] + 1) * 4].rearrange("p k h n -> p (k h) n")
                        nc.vector.scalar_tensor_tensor(
                            out=v[:, :, DH + 1:VW], in0=W[:].rearrange("p (k n) -> p k n", n=DH), scalar=KV_EVAC,
                            in1=v[:, :, 0:DH], op0=ALU.mult, op1=ALU.subtract).then_inc(job_free, 1)
                    elif job[0] == "M":
                        _, h, q, kt = job
                        dve.wait_ge(job_filled, after(item * JOBS + n))
                        nc.vector.tensor_reduce(cmx[:, h, q, kt:kt + 1], W[:], X_AXIS, ALU.max).then_inc(job_free, 1)
                        if job == LAST_MAX[h]:
                            new_maximum(p, item, c, h)
                    else:
                        h = job[1]
                        dve.wait_ge(job_filled, after(item * JOBS + n))
                        nc.vector.tensor_scalar(MB[DH:DH + 1, par, h, :], W[0:1, :], -1.0, None,
                                                ALU.mult).then_inc(job_free, 1)

                def low(g, d):
                    dve.wait_ge(ph_ready, after(g))
                    nc.vector.tensor_tensor(pl[:, d % RING, :], p32[:, d % 2, :], ph[:, d % RING, :],
                                            ALU.subtract).then_inc(pl_ready, 1)

                def gather(p, item, c, h):
                    unit = 2 * item + h
                    par = c % 2
                    dve.wait_ge(av_done, after(unit * DUOS + DUOS - 1))
                    if c == 0:
                        for b in range(2):
                            i = nc.vector.tensor_copy(acc[:, h, b], O_view[:, b, :, 0:DH + 1])
                    else:
                        dve.wait_ge(corr_ready, corr_count(p, c, h))
                        for q in range(QT):
                            i = nc.vector.scalar_tensor_tensor(
                                out=acc[:, h, q // 2, q % 2, :], in0=acc[:, h, q // 2, q % 2, :],
                                scalar=corr[:, par, h, q:q + 1], in1=O_view[:, q // 2, q % 2, 0:DH + 1],
                                op0=ALU.mult, op1=ALU.add)
                    i.then_inc(o_part, 1)
                    dve.wait_ge(o_part, unit + 1)
                    for b in range(2):
                        i = nc.vector.tensor_tensor(acc[:, h, b, :, 0:DH], acc[:, h, b, :, 0:DH],
                                                    O_view[:, b, :, DH + 1:VW], ALU.add)
                    i.then_inc(o_free, 1)

                def finish_pair(p, item):
                    dve.wait_ge(o_free, after(2 * item + 1))
                    nc.vector.reciprocal(rec[:], acc[:, :, :, :, DH]).then_inc(out_rec, 1)
                    dve.wait_ge(out_rec, p + 1)
                    dve.wait_ge(out_stored, 16 * p + HEAD)
                    for h in range(2):
                        for q in range(QT):
                            i = nc.vector.tensor_scalar(
                                out[:, q, h, :], acc[:, h, q // 2, q % 2, 0:DH], rec[:, h, q // 2, q % 2:q % 2 + 1],
                                1.0 / KV_SCALE, ALU.mult, ALU.mult)
                    i.then_inc(out_norm, 1)

                def pair(p, last):
                    for c, d, item, nxt in chunk_steps(p, last):
                        if d == 0:
                            job(p, item, c, ("R", 1))
                        if nxt is not None:
                            if nxt < 2 and d == 0:
                                q_low(2 * p + (3 if nxt == 0 else 2), nxt)
                            for j in PLAN[d]:
                                job(p + 1 if nxt == 0 else p, item + 1, nxt, j)
                            if nxt == NCHUNK - 1 and d == W_SPLIT_STEP and not last:
                                w_low(p + 1)
                        low(item * STEPS + d, d)
                        if d == DUOS + 1:
                            gather(p, item, c, 0)
                        if d == 1 and c > 0:
                            gather(p, item - 1, c - 1, 1)
                    item = p * NCHUNK + NCHUNK - 1
                    gather(p, item, NCHUNK - 1, 1)
                    finish_pair(p, item)

                for s in (pl_ready, o_free, job_free):
                    dve.sem_inc(s, HEAD)
                w_low(0)
                q_low(1, 0)
                for s in PLAN:
                    for j in s:
                        job(0, 0, 0, j)
                with dve.Fori(0, PAIRS - 1) as p:
                    pair(p, False)
                pair(PAIRS - 1, True)


def rope_constants():
    inv = (np.float32(1.0) / np.float32(10000.0) ** (np.arange(0, DS, 2, dtype=np.float32) / np.float32(DS)))
    angle = np.outer(np.arange(T, dtype=np.float32), inv.astype(np.float32)).astype(np.float32)
    angle = np.concatenate([angle, angle], axis=-1).T
    turn = np.zeros((P, P), np.float32)
    for n in range(P):
        d = n % DS
        if d < DS // 2:
            turn[n + DS // 2, n] = -1.0
        else:
            turn[n - DS // 2, n] = 1.0
    tile4 = lambda t: np.ascontiguousarray(np.tile(t, (P // DS, 1)).astype(np.float32))
    return tile4(np.cos(angle)), tile4(np.sin(angle)), turn


def self_attention(nc, a, dram, keep, x):
    with ExitStack() as ctx:
        sb = lambda name, shape, dt=F32: ctx.enter_context(nc.sbuf_tensor(name, shape, dt))
        sem = lambda name: ctx.enter_context(nc.semaphore(name))
        ident = keep.ident
        big = sb("big", [P, PAIRS, T])
        o_all = sb("o_all", [P, PAIRS, QT, P])
        wo_x = sb("wo_x", [P, PAIRS, D])
        bo = sb("bo", [P, D])
        xn = sb("xn_t", [P, QT, D])
        xT = sb("xT", [P, DT, T])
        w_at = {n: sb(f"w_{n}", [P, DT, D]) for n in ("Wq", "Wk", "Wv", "Wo")}
        cos, sin, turn, causal = sb("cos", [P, T]), sb("sin", [P, T]), sb("turn", [P, P]), sb("causal", [P, P])
        qk = sb("qk", [P, 2 * DT, T])
        v = sb("v", [P, QT, D])
        r0, r1, r2 = sb("r0", [P, T]), sb("r1", [P, T]), sb("r2", [P, T])
        pr = sb("pr", [P, 2, QT, T])
        pT = sb("pT", [P, 2, QT, T])
        mx, nb = sb("mx", [P, HS, QT]), sb("nb", [P, HS, QT])
        rsum, rrec = sb("rsum", [P, HS, QT]), sb("rrec", [P, HS, QT])
        stats, mv = sb("stats_t", [P, QT, 6]), sb("mv_t", [P, QT, 2])
        rs = sb("rs_t", [P, 7, QT])
        bank = [ctx.enter_context(nc.psum_tensor(f"bank{i}", [P, 512], F32)) for i in range(8)]
        oT = big

        loaded = {n: sem(f"loaded_{n}") for n in ("o", "wo_x", "x", "bo", "Wq", "Wk", "Wv", "Wo", "rope")}
        o_turned, o_turned_out, y_ready, x1_ready = sem("o_turned"), sem("o_turned_out"), sem("y_ready"), sem("x1_ready")
        ln_step, root = sem("ln_step1"), sem("root1")
        x_turned, x_turned_out = sem("x_turned"), sem("x_turned_out")
        proj, proj_out, rotated, rope_step, rope_done = (sem("proj"), sem("proj_out"), sem("rotated"),
                                                         sem("rope_step"), sem("rope_done"))
        v_ready, v_out = sem("v_ready"), sem("v_out")
        s_ready, s_masked, s_max, s_bias, s_exp, s_rec, s_norm = (sem("s_ready"), sem("s_masked"), sem("s_max"), sem(
            "s_bias"), sem("s_exp"), sem("s_rec"), sem("s_norm"))
        p_turned, p_turned_out, av_ready, av_out = sem("p_turned"), sem("p_turned_out"), sem("av_ready"), sem("av_out")
        z_ready, x2_ready = sem("z_ready"), sem("x2_ready")

        S_AT = {3: (0, 0), 2: (1, 0), 0: (1, 384), 1: (2, 0)}
        T_AT = {0: (3, 0), 1: (4, 0), 3: (4, 384), 2: (5, 0)}

        with nc.Block() as block:

            @block.sync
            def _(sp):
                for t in range(QT):
                    sp.dma_start(o_all[:, :, t, :], dram.o.rearrange("a p (t n) -> p a t n", t=QT)[:, :, t, :]
                                 ).then_inc(loaded["o"], 16)
                sp.dma_start(wo_x[:], a["L0_xattn_Wo"].rearrange("(k p) n -> p k n", p=P)).then_inc(loaded["wo_x"], 16)
                sp.dma_start(x[:], a["x"][0].rearrange("(t p) d -> p t d", p=P)).then_inc(loaded["x"], 16)
                sp.dma_start(bo[:], a["L0_xattn_bo"].rearrange("(o n) -> o n", o=1).broadcast_to([P, D])
                             ).then_inc(loaded["bo"], 16)
                for n in ("Wq", "Wk", "Wv", "Wo"):
                    sp.dma_start(w_at[n][:], a[f"attn_{n}T"].rearrange("(k p) n -> p k n", p=P)).then_inc(loaded[n], 16)
                for t, n in ((cos, "rope_cos"), (sin, "rope_sin"), (turn, "rope_turn"), (causal, "causal")):
                    sp.dma_start(t[:], a[n]).then_inc(loaded["rope"], 16)

            @block.tensor
            def _(pe):
                pe.wait_ge(loaded["o"], 16 * QT)
                for n in range(PAIRS):
                    if n >= 4:
                        pe.wait_ge(o_turned_out, n - 3)
                    for t in range(QT):
                        i = nc.tensor.transpose(bank[n % 4][:, t * P:(t + 1) * P], o_all[:, n, t, :], ident[:])
                    i.then_inc(o_turned, 1)
                pe.wait_ge(loaded["wo_x"], 16)
                pe.wait_ge(o_turned_out, PAIRS)
                for t in range(QT):
                    for k in range(PAIRS):
                        i = nc.tensor.matmul(bank[4 + t][:], oT[:, k, t * P:(t + 1) * P], wo_x[:, k, :],
                                             start=(k == 0), stop=(k == PAIRS - 1))
                    i.then_inc(y_ready, 1)
                pe.wait_ge(ln_step, LN_DONE)
                for d in range(DT):
                    for t in range(QT):
                        i = nc.tensor.transpose(bank[d][:, t * P:(t + 1) * P], xn[:, t, d * P:(d + 1) * P], ident[:])
                    i.then_inc(x_turned, 1)
                pe.wait_ge(x_turned_out, DT)
                for n in range(2 * DT):
                    name, m = ("Wq", n) if n < DT else ("Wk", n - DT)
                    if m == 0:
                        pe.wait_ge(loaded[name], 16)
                        pe.wait_ge(loaded["rope"], 64)
                    if n >= 4:
                        pe.wait_ge(rope_done, n - 3)
                    for k in range(DT):
                        i = nc.tensor.matmul(bank[4 + n % 4][:], w_at[name][:, k, m * P:(m + 1) * P], xT[:, k, :],
                                             start=(k == 0), stop=(k == DT - 1))
                    i.then_inc(proj, 1)
                    if n >= 1:
                        pe.wait_ge(proj_out, n)
                        nc.tensor.matmul(bank[(n - 1) % 4][:], turn[:], qk[:, n - 1, :], start=True,
                                         stop=True).then_inc(rotated, 1)
                pe.wait_ge(proj_out, 2 * DT)
                nc.tensor.matmul(bank[(2 * DT - 1) % 4][:], turn[:], qk[:, 2 * DT - 1, :], start=True,
                                 stop=True).then_inc(rotated, 1)
                pe.wait_ge(loaded["Wv"], 16)
                pe.wait_ge(rope_done, 2 * DT)
                for t in range(QT):
                    for k in range(DT):
                        i = nc.tensor.matmul(bank[4 + t][:], xT[:, k, t * P:(t + 1) * P], w_at["Wv"][:, k, :],
                                             start=(k == 0), stop=(k == DT - 1))
                    i.then_inc(v_ready, 1)
                pe.wait_ge(v_out, QT)

                def head_scores(n):
                    rows, tile = slice(n % 4 * DS, n % 4 * DS + DS), n // 4
                    if n >= 1:
                        pe.wait_ge(s_exp, n)
                    for t in (3, 2, 0, 1):
                        b, o = S_AT[t]
                        i = nc.tensor.matmul(bank[b][:, o:o + (t + 1) * P], qk[rows, tile, t * P:(t + 1) * P],
                                             qk[rows, DT + tile, 0:(t + 1) * P], start=True, stop=True)
                    i.then_inc(s_ready, 1)

                head_scores(0)
                for n in range(HS):
                    if n + 1 < HS:
                        head_scores(n + 1)
                    pe.wait_ge(s_norm, n + 1)
                    if n >= 1:
                        pe.wait_ge(p_turned_out, n)
                    for k in (0, 1, 3, 2):
                        b, o = T_AT[k]
                        for t in range(k, QT):
                            i = nc.tensor.transpose(bank[b][:, o + (t - k) * P:o + (t - k + 1) * P],
                                                    pr[:, n % 2, t, k * P:(k + 1) * P], ident[:])
                    i.then_inc(p_turned, 1)
                    pe.wait_ge(p_turned_out, n + 1)
                    rows, out_bank = slice(n % 4 * DS, n % 4 * DS + DS), bank[6 + n // 4 % 2]
                    if n % 4 == 0 and n >= 8:
                        pe.wait_ge(av_out, n // 4 - 1)
                    for k in range(QT):
                        i = nc.tensor.matmul(out_bank[rows, k * P:T], v[:, k, n * DS:(n + 1) * DS],
                                             pT[:, n % 2, k, k * P:T], start=(k == 0), stop=(k == QT - 1))
                    if n % 4 == 3:
                        i.then_inc(av_ready, 1)
                pe.wait_ge(loaded["Wo"], 16)
                pe.wait_ge(av_out, DT)
                for t in range(QT):
                    for k in range(DT):
                        i = nc.tensor.matmul(bank[t][:], oT[:, k, t * P:(t + 1) * P], w_at["Wo"][:, k, :],
                                             start=(k == 0), stop=(k == DT - 1))
                    i.then_inc(z_ready, 1)

            @block.scalar
            def _(act):
                act.wait_ge(ln_step, LN_VAR)
                nc.scalar.activation(rs[:, 1, :], rs[:, 0, :], ACT.Sqrt).then_inc(root, 1)
                for n in range(2 * DT):
                    act.wait_ge(proj, n + 1)
                    nc.scalar.activation(qk[:, n, :], bank[4 + n % 4][:], ACT.Copy).then_inc(proj_out, 1)
                for t in range(QT):
                    act.wait_ge(v_ready, t + 1)
                    nc.scalar.activation(v[:, t, :], bank[4 + t][:], ACT.Copy).then_inc(v_out, 1)

                def exps(n):
                    act.wait_ge(s_bias, n + 1)
                    if n >= 2:
                        act.wait_ge(p_turned, n - 1)
                    for t in range(QT):
                        b, o = S_AT[t]
                        i = nc.scalar.activation(pr[:, n % 2, t, 0:(t + 1) * P], bank[b][:, o:o + (t + 1) * P], ACT.Exp,
                                                 bias=nb[:, n, t:t + 1], scale=1.0 / math.sqrt(DS),
                                                 accum_out=rsum[:, n, t:t + 1])
                    i.then_inc(s_exp, 1)

                exps(0)
                for n in range(HS):
                    if n + 1 < HS:
                        exps(n + 1)
                    act.wait_ge(p_turned, n + 1)
                    for k in range(QT):
                        b, o = T_AT[k]
                        i = nc.scalar.activation(pT[:, n % 2, k, k * P:T], bank[b][:, o:o + (QT - k) * P], ACT.Copy)
                    i.then_inc(p_turned_out, 1)
                    if n % 4 == 3:
                        act.wait_ge(av_ready, n // 4 + 1)
                        nc.scalar.activation(oT[:, n // 4, :], bank[6 + n // 4 % 2][:], ACT.Copy).then_inc(av_out, 1)

            @block.vector
            def _(dve):
                for n in range(PAIRS):
                    dve.wait_ge(o_turned, n + 1)
                    nc.vector.tensor_copy(oT[:, n, :], bank[n % 4][:]).then_inc(o_turned_out, 1)
                dve.wait_ge(loaded["x"], 16)
                dve.wait_ge(loaded["bo"], 16)
                for t in range(QT):
                    i = nc.vector.tensor_tensor(x[:, t, :], x[:, t, :], bo[:], ALU.add)
                i.then_inc(x1_ready, 1)
                dve.wait_ge(x1_ready, 1)
                for t in range(QT):
                    dve.wait_ge(y_ready, t + 1)
                    nc.vector.tensor_tensor(x[:, t, :], x[:, t, :], bank[4 + t][:], ALU.add).then_inc(x1_ready, 1)
                dve.wait_ge(x1_ready, 1 + QT)
                layer_norm_rows(nc, dve, x, xn, stats, mv, rs, ln_step, root)
                for d in range(DT):
                    dve.wait_ge(x_turned, d + 1)
                    nc.vector.tensor_copy(xT[:, d, :], bank[d][:]).then_inc(x_turned_out, 1)
                for n in range(2 * DT):
                    dve.wait_ge(rotated, n + 1)
                    if n >= 1:
                        dve.wait_ge(rope_done, n)
                    nc.vector.tensor_tensor(r0[:], bank[n % 4][:], sin[:], ALU.mult).then_inc(rope_step, 1)
                    nc.vector.tensor_tensor(r1[:], qk[:, n, :], cos[:], ALU.mult).then_inc(rope_step, 1)
                    dve.wait_ge(rope_step, 2 * n + 2)
                    nc.vector.tensor_tensor(qk[:, n, :], r0[:], r1[:], ALU.add).then_inc(rope_done, 1)

                def soft(n):
                    dve.wait_ge(s_ready, n + 1)
                    for t in range(QT):
                        b, o = S_AT[t]
                        diag = bank[b][:, o + t * P:o + (t + 1) * P]
                        i = nc.vector.tensor_tensor(diag, diag, causal[:], ALU.add)
                    i.then_inc(s_masked, 1)
                    dve.wait_ge(s_masked, n + 1)
                    for t in range(QT):
                        b, o = S_AT[t]
                        i = nc.vector.tensor_reduce(mx[:, n, t:t + 1], bank[b][:, o:o + (t + 1) * P], X_AXIS, ALU.max)
                    i.then_inc(s_max, 1)
                    dve.wait_ge(s_max, n + 1)
                    nc.vector.tensor_scalar(nb[:, n, :], mx[:, n, :], -1.0 / math.sqrt(DS), None,
                                            ALU.mult).then_inc(s_bias, 1)

                def norm(n):
                    dve.wait_ge(s_exp, n + 1)
                    nc.vector.reciprocal(rrec[:, n, :], rsum[:, n, :]).then_inc(s_rec, 1)
                    dve.wait_ge(s_rec, n + 1)
                    for t in range(QT):
                        i = nc.vector.tensor_scalar(pr[:, n % 2, t, 0:(t + 1) * P], pr[:, n % 2, t, 0:(t + 1) * P],
                                                    rrec[:, n, t:t + 1], None, ALU.mult)
                    i.then_inc(s_norm, 1)

                soft(0)
                for n in range(HS):
                    norm(n)
                    if n + 1 < HS:
                        soft(n + 1)
                for t in range(QT):
                    dve.wait_ge(z_ready, t + 1)
                    nc.vector.tensor_tensor(x[:, t, :], x[:, t, :], bank[t][:], ALU.add).then_inc(x2_ready, 1)
                dve.wait_ge(x2_ready, QT)


def experts(nc, a, keep, out, x):
    with ExitStack() as ctx:
        sb = lambda name, shape, dt=F32: ctx.enter_context(nc.sbuf_tensor(name, shape, dt))
        sem = lambda name: ctx.enter_context(nc.semaphore(name))
        HT = H // P
        ident = keep.ident
        xn = sb("xn_e", [P, QT, D])
        xT = sb("xT_e", [P, DT, T])
        w_in, w_out = sb("w_in", [P, 2, DT, H]), sb("w_out", [P, 2, HT, D])
        hT = sb("hT", [P, 2, HT, T])
        b_in = sb("b_in", [P, E * HT])
        b_out = sb("b_out", [E, D])
        router = sb("router", [P, DT, E])
        logits, probs = sb("logits", [P, QT, E]), sb("probs", [P, QT, E])
        top, left, gate = sb("top", [P, QT, 8]), sb("left", [P, QT, E]), sb("gate", [P, QT, E])
        lmax, lneg, lsum, lrec = (sb(n, [P, QT]) for n in ("lmax", "lneg", "lsum", "lrec"))
        gateT = sb("gateT", [E, T])
        stats, mv = sb("stats_e", [P, QT, 6]), sb("mv_e", [P, QT, 2])
        rs = sb("rs_e", [P, 7, QT])
        up = [ctx.enter_context(nc.psum_tensor(f"up{i}", [P, 512], F32)) for i in range(4)]
        down = [ctx.enter_context(nc.psum_tensor(f"down{i}", [P, 512], F32)) for i in range(4)]
        small_loaded = sem("small_loaded")
        in_loaded = [sem("in_loaded0"), sem("in_loaded1")]
        out_loaded = [sem("out_loaded0"), sem("out_loaded1")]
        ln_step, root = sem("ln_step2"), sem("root2")
        turned, turned_out = sem("turned2"), sem("turned2_out")
        lg_ready, lg_out, lg_step, lg_exp = sem("lg_ready"), sem("lg_out"), sem("lg_step"), sem("lg_exp")
        gates_ready, gates_turned, gates_out = sem("gates_ready"), sem("gates_turned"), sem("gates_out")
        up_ready, up_out, down_ready, down_out = sem("up_ready"), sem("up_out"), sem("down_ready"), sem("down_out")
        bias_ready, stored = sem("bias_ready"), sem("stored")

        with nc.Block() as block:

            @block.sync
            def _(sp):
                def load(e, b, wait):
                    if wait:
                        sp.wait_ge(up_ready, HT * (e - 1))
                    sp.dma_start(w_in[:, b], a["L0_ffn_w_in"][one_of(e)].rearrange("e (k p) n -> p (e k) n", p=P)
                                 ).then_inc(in_loaded[b], 16)
                    if wait:
                        sp.wait_ge(down_ready, QT * (e - 1))
                    sp.dma_start(w_out[:, b], a["L0_ffn_w_out"][one_of(e)].rearrange("e (k p) n -> p (e k) n", p=P)
                                 ).then_inc(out_loaded[b], 16)

                for t, s in ((router, a["L0_ffn_router_w"].rearrange("(k p) n -> p k n", p=P)),
                             (b_in, a["b_in_columns"]), (b_out, a["L0_ffn_b_out"])):
                    sp.dma_start(t[:], s).then_inc(small_loaded, 16)
                load(0, 0, False)
                load(1, 1, False)
                with sp.Fori(1, E // 2) as e2:
                    load(e2 * 2, 0, True)
                    load(e2 * 2 + 1, 1, True)
                sp.wait_ge(down_out, QT * (E + 1))
                sp.dma_start(out[0].rearrange("(t p) d -> p t d", p=P), x[:]).then_inc(stored, 16)
                sp.wait_ge(stored, 16)

            @block.tensor
            def _(pe):
                pe.wait_ge(ln_step, LN_DONE)
                for d in range(DT):
                    for t in range(QT):
                        i = nc.tensor.transpose(up[d][:, t * P:(t + 1) * P], xn[:, t, d * P:(d + 1) * P], ident[:])
                    i.then_inc(turned, 1)
                pe.wait_ge(small_loaded, 48)
                pe.wait_ge(turned_out, DT)
                for t in range(QT):
                    for k in range(DT):
                        i = nc.tensor.matmul(down[0][:, t * E:(t + 1) * E], xT[:, k, t * P:(t + 1) * P], router[:, k, :],
                                             start=(k == 0), stop=(k == DT - 1))
                i.then_inc(lg_ready, 1)

                def up_one(e, b, first=False):
                    for m in range(HT):
                        if not first:
                            pe.wait_ge(up_out, HT * (e - 1) + m + 1)
                        for k in range(DT):
                            i = nc.tensor.matmul(up[m][:], w_in[:, b, k, m * P:(m + 1) * P], xT[:, k, :],
                                                 start=(k == 0), stop=(k == DT - 1))
                        i.then_inc(up_ready, 1)

                pe.wait_ge(in_loaded[0], 16)
                up_one(0, 0, first=True)
                pe.wait_ge(gates_ready, 1)
                for t in range(QT):
                    i = nc.tensor.transpose(down[0][0:E, t * P:(t + 1) * P], gate[:, t, :], ident[:])
                i.then_inc(gates_turned, 1)
                pe.wait_ge(gates_out, 1)
                for t in range(QT):
                    nc.tensor.matmul(down[t][:], gateT[:, t * P:(t + 1) * P], b_out[:], start=True,
                                     stop=True).then_inc(bias_ready, 1)

                def down_one(e, b):
                    pe.wait_ge(up_out, HT * (e + 1))
                    for t in range(QT):
                        pe.wait_ge(down_out, QT * e + t + 1)
                        for k in range(HT):
                            i = nc.tensor.matmul(down[t][:], hT[:, b, k, t * P:(t + 1) * P], w_out[:, b, k, :],
                                                 start=(k == 0), stop=(k == HT - 1))
                        i.then_inc(down_ready, 1)

                def two(e2, last):
                    e = e2 * 2
                    pe.wait_ge(in_loaded[1], 16 * e2 + 16)
                    up_one(e + 1, 1)
                    pe.wait_ge(out_loaded[0], 16 * e2 + 16)
                    down_one(e, 0)
                    if not last:
                        pe.wait_ge(in_loaded[0], 16 * e2 + 32)
                        up_one(e + 2, 0)
                    pe.wait_ge(out_loaded[1], 16 * e2 + 16)
                    down_one(e + 1, 1)

                with pe.Fori(0, E // 2 - 1) as e2:
                    two(e2, False)
                two(E // 2 - 1, True)

            @block.scalar
            def _(act):
                act.wait_ge(ln_step, LN_VAR)
                nc.scalar.activation(rs[:, 1, :], rs[:, 0, :], ACT.Sqrt).then_inc(root, 1)
                act.wait_ge(lg_step, 3)
                for t in range(QT):
                    i = nc.scalar.activation(probs[:, t, :], logits[:, t, :], ACT.Exp, bias=lneg[:, t:t + 1], scale=1.0,
                                             accum_out=lsum[:, t:t + 1])
                i.then_inc(lg_exp, 1)

                def gelu(e, b, first):
                    for m in range(HT):
                        act.wait_ge(up_ready, HT * e + m + 1)
                        if not first:
                            act.wait_ge(down_ready, QT * (e - 1))
                        nc.scalar.activation(hT[:, b, m, :], up[m][:], ACT.Gelu_apprx_tanh,
                                             bias=b_in[:, e * HT + m:e * HT + m + 1] if isinstance(e, int)
                                             else b_in[:, bass.ds(e * HT + m, 1)]).then_inc(up_out, 1)

                act.wait_ge(small_loaded, 48)
                gelu(0, 0, True)
                gelu(1, 1, True)
                with act.Fori(1, E // 2) as e2:
                    gelu(e2 * 2, 0, False)
                    gelu(e2 * 2 + 1, 1, False)

            @block.vector
            def _(dve):
                layer_norm_rows(nc, dve, x, xn, stats, mv, rs, ln_step, root)
                for d in range(DT):
                    dve.wait_ge(turned, d + 1)
                    nc.vector.tensor_copy(xT[:, d, :], up[d][:]).then_inc(turned_out, 1)
                dve.wait_ge(lg_ready, 1)
                nc.vector.tensor_copy(logits[:], down[0][:, 0:QT * E].rearrange("p (t e) -> p t e", e=E)
                                      ).then_inc(lg_step, 1)
                dve.wait_ge(lg_step, 1)
                nc.vector.tensor_reduce(lmax[:], logits[:], X_AXIS, ALU.max).then_inc(lg_step, 1)
                dve.wait_ge(lg_step, 2)
                nc.vector.tensor_scalar(lneg[:], lmax[:], -1.0, None, ALU.mult).then_inc(lg_step, 1)
                dve.wait_ge(lg_exp, 1)
                nc.vector.reciprocal(lrec[:], lsum[:]).then_inc(lg_step, 1)
                dve.wait_ge(lg_step, 4)
                for t in range(QT):
                    i = nc.vector.tensor_scalar(probs[:, t, :], probs[:, t, :], lrec[:, t:t + 1], None, ALU.mult)
                i.then_inc(lg_step, 1)
                dve.wait_ge(lg_step, 5)
                for t in range(QT):
                    i = nc.vector.max(top[:, t, :], probs[:, t, :])
                i.then_inc(lg_step, 1)
                dve.wait_ge(lg_step, 6)
                nc.vector.memset(top[:, :, 2:8], -1.0).then_inc(lg_step, 1)
                dve.wait_ge(lg_step, 7)
                for t in range(QT):
                    i = nc.vector.match_replace(left[:, t, :], top[:, t, :], probs[:, t, :], 0.0)
                i.then_inc(lg_step, 1)
                dve.wait_ge(lg_step, 8)
                nc.vector.tensor_tensor(gate[:], probs[:], left[:], ALU.subtract).then_inc(gates_ready, 1)
                dve.wait_ge(gates_turned, 1)
                nc.vector.tensor_copy(gateT[:], down[0][0:E, :]).then_inc(gates_out, 1)
                for t in range(QT):
                    dve.wait_ge(bias_ready, t + 1)
                    nc.vector.tensor_tensor(x[:, t, :], x[:, t, :], down[t][:], ALU.add).then_inc(down_out, 1)

                def add(e, column):
                    for t in range(QT):
                        dve.wait_ge(down_ready, QT * e + t + 1)
                        dve.wait_ge(down_out, QT * e + t + 1)
                        nc.vector.scalar_tensor_tensor(out=x[:, t, :], in0=down[t][:], scalar=gate[:, t, column],
                                                       in1=x[:, t, :], op0=ALU.mult, op1=ALU.add).then_inc(down_out, 1)

                with dve.Fori(0, E) as e:
                    add(e, bass.ds(e, 1))


class Kept:
    pass


def build(nc, a, out):
    dram, keep = Kept(), Kept()
    dram.q = nc.dram_tensor("q_by_pair", (PAIRS, P, T), F32).ap()
    dram.o = nc.dram_tensor("o_by_pair", (PAIRS, P, QT * P), F32).ap()
    with ExitStack() as ctx:
        keep.ident = ctx.enter_context(nc.sbuf_tensor("ident", [P, P], F32))
        keep.ident16 = ctx.enter_context(nc.sbuf_tensor("ident16", [P, P], F16))
        with nc.sbuf_tensor("ctx_halves", [P, 2, CT, NKEY], F16) as keep.ctx:
            prologue(nc, a, dram, keep)
            cross_attention(nc, a, dram, keep)
        with nc.sbuf_tensor("x", [P, QT, D], F32) as x:
            self_attention(nc, a, dram, keep, x)
            experts(nc, a, keep, out, x)


def kernel(**inputs):
    import concourse.bacc as bacc
    from concourse.bass_utils import run_bass_kernel_spmd

    arrays = {}
    for name in ("x", "L0_xattn_Wq", "L0_xattn_Wo", "L0_xattn_bo", "L0_ffn_router_w", "L0_ffn_w_in", "L0_ffn_w_out",
                 "L0_ffn_b_out"):
        arrays[name] = np.ascontiguousarray(inputs[name])
    arrays["ctxT"] = np.ascontiguousarray(np.asarray(inputs["ctx_768"])[0].T)
    for name in ("Wk", "Wv"):
        w = np.asarray(inputs[f"L0_xattn_{name}"]).reshape(CT, P, PAIRS, P)
        arrays[f"{name.lower()}_pairs"] = np.ascontiguousarray(w.transpose(2, 1, 0, 3)).reshape(PAIRS, P, CT * P)
    for name in ("Wq", "Wk", "Wv", "Wo"):
        arrays[f"attn_{name}T"] = np.ascontiguousarray(np.asarray(inputs[f"L0_attn_{name}"]).T)
    b_in = np.asarray(inputs["L0_ffn_b_in"]).reshape(E, H // P, P)
    arrays["b_in_columns"] = np.ascontiguousarray(b_in.transpose(2, 0, 1)).reshape(P, E * (H // P))
    arrays["rope_cos"], arrays["rope_sin"], arrays["rope_turn"] = rope_constants()
    arrays["causal"] = np.where(np.arange(P)[None, :] > np.arange(P)[:, None], np.finfo(np.float32).min,
                                np.float32(0.0)).astype(np.float32)

    nc = bacc.Bacc("TRN2", target_bir_lowering=False, num_devices=1)
    a = {n: nc.dram_tensor(f"in_{n}", v.shape, mybir.dt.from_np(v.dtype), kind="ExternalInput").ap()
         for n, v in arrays.items()}
    out = nc.dram_tensor("out_0", (1, T, D), F32, kind="ExternalOutput").ap()
    build(nc, a, out)
    r = run_bass_kernel_spmd(nc, [{f"in_{n}": v for n, v in arrays.items()}], core_ids=[0])
    return r.results[0]["out_0"]
```

```python
import math
from contextlib import ExitStack

import concourse.bass as bass
import numpy as np
from concourse import mybir

F32 = mybir.dt.float32
F16 = mybir.dt.float16
ALU = mybir.AluOpType
ACT = mybir.ActivationFunctionType
X_AXIS = mybir.AxisListType.X

P = 128
D = 512
T = 512
QT = T // P
DT = D // P
EPS = 1e-5

NKEY = 8192
CTX = 384
CT = CTX // P
HX = 16
DH = 64
PAIRS = HX // 2
CHUNK = 2048
NCHUNK = NKEY // CHUNK
KB = CHUNK // P
DUOS = KB // 2
STEPS = 2 * DUOS
KT = CHUNK // 512
VW = 2 * DH + 1

CTX_SCALE = 16.0
W_SCALE = 256.0
KV_SCALE = 16.0
Q_SCALE = 16.0
P_SCALE = 256.0
M_UNIT = 64.0
KV_EVAC = KV_SCALE / (CTX_SCALE * W_SCALE)
EXP_SCALE = 1.0 / (Q_SCALE * KV_SCALE * math.sqrt(DH))

HS = 16
DS = D // HS

E = 8
H = 512

RING = 4
HEAD = 4

PSTEPS = NCHUNK * STEPS
KV_KEYS = 256
KV_JOBS = CHUNK // KV_KEYS
LAG = 2


def job_plan():
    steps = [[] for _ in range(STEPS)]
    k_at = [3 * (n // 2) + n % 2 for n in range(KV_JOBS)]
    v_at = [s for s in range(STEPS) if s not in k_at]
    for n in range(KV_JOBS):
        steps[k_at[n]].append((("K", n), False))
        steps[v_at[n]].append((("V", n), False))
    free = [s for s in range(2, STEPS + 2) for _ in range(2)]
    for h in range(2):
        for t in range(KT):
            for q in range(QT):
                s = next(s for s in free if s > k_at[2 * t + 1])
                free.remove(s)
                steps[s % STEPS].append((("M", h, q, t), s >= STEPS))
    steps[STEPS - 2].append((("R", 0), False))
    steps[2].append((("R", 1), True))
    for s in steps:
        s.sort(key=lambda j: j[0][0] not in "KV")
    return steps


PLAN = job_plan()
BANKS = 3
JOBS = sum(map(len, PLAN)) + 1
EARLY = [job for step in PLAN for job, late in step if not late]
LATE = sum(late for step in PLAN for _, late in step)
NUMBER = {job: n for n, (job, late) in enumerate(j for step in PLAN for j in step)}
FIRST_NUMBER = {job: LATE + n for n, job in enumerate(EARLY)}
LAST_NUMBER = {job: n for n, job in enumerate(j for step in PLAN for j, late in step if late)}
KV_ORDER = {job: n for n, job in enumerate(j for j in EARLY if j[0] in "KV")}
LAST_MAX = [("M", h, QT - 1, KT - 1) for h in range(2)]
WK_STEP = STEPS - 4
assert JOBS % BANKS == 0 and max(NUMBER, key=NUMBER.get) == EARLY[-1]
RING_S = 3
POOL_COLS = 384
def one_of(n):
    return slice(n, n + 1) if isinstance(n, int) else bass.ds(n, 1)


def layer_norm_rows(nc, dve, x, xn, stats, mv, rs, ln_step, root):
    for t in range(QT):
        i = nc.vector.bn_stats(stats[:, t, :], x[:, t, :])
    i.then_inc(ln_step, 1)
    dve.wait_ge(ln_step, 1)
    for t in range(QT):
        i = nc.vector.bn_aggr(mv[:, t, :], stats[:, t, :])
    i.then_inc(ln_step, 1)
    dve.wait_ge(ln_step, 2)
    nc.vector.tensor_scalar(rs[:, 0, :], mv[:, :, 1], EPS, None, ALU.add).then_inc(ln_step, 1)
    dve.wait_ge(root, 1)
    nc.vector.reciprocal(rs[:, 2, :], rs[:, 1, :]).then_inc(ln_step, 1)
    dve.wait_ge(ln_step, 4)
    nc.vector.tensor_tensor(rs[:, 3, :], rs[:, 2, :], rs[:, 2, :], ALU.mult).then_inc(ln_step, 1)
    dve.wait_ge(ln_step, 5)
    nc.vector.tensor_tensor(rs[:, 4, :], rs[:, 3, :], rs[:, 0, :], ALU.mult).then_inc(ln_step, 1)
    dve.wait_ge(ln_step, 6)
    nc.vector.tensor_scalar(rs[:, 5, :], rs[:, 4, :], -0.5, 1.5, ALU.mult, ALU.add).then_inc(ln_step, 1)
    dve.wait_ge(ln_step, 7)
    nc.vector.tensor_tensor(rs[:, 6, :], rs[:, 5, :], rs[:, 2, :], ALU.mult).then_inc(ln_step, 1)
    dve.wait_ge(ln_step, 8)
    for t in range(QT):
        i = nc.vector.tensor_scalar(xn[:, t, :], x[:, t, :], mv[:, t, 0:1], rs[:, 6, t:t + 1],
                                    ALU.subtract, ALU.mult)
    i.then_inc(ln_step, 1)


LN_VAR = 3
LN_DONE = 9


def prologue(nc, a, dram, keep):
    with ExitStack() as ctx:
        sb = lambda name, shape, dt=F32: ctx.enter_context(nc.sbuf_tensor(name, shape, dt))
        sem = lambda name: ctx.enter_context(nc.semaphore(name))
        PIECE = 512
        NPIECE = NKEY // PIECE
        raw = sb("ctx_raw", [P, 2, CT, PIECE])
        x = sb("x_in", [P, QT, D])
        xn = sb("xn", [P, QT, D])
        xnT = sb("xnT", [P, DT, T])
        wq = sb("wq", [P, DT, HX * DH])
        qout = sb("qout", [P, 2, T])
        stats = sb("stats", [P, QT, 6])
        mv = sb("mv", [P, QT, 2])
        rs = sb("rs", [P, 7, QT])
        ps = [ctx.enter_context(nc.psum_tensor(f"pp{i}", [P, 512], F32)) for i in range(4)]
        x_loaded, wq_loaded = sem("x_loaded"), sem("wq_loaded")
        q_stored = [sem("q_stored0"), sem("q_stored1")]
        raw_loaded = [sem("raw_loaded0"), sem("raw_loaded1")]
        ctx_hi, ctx_lo = sem("ctx_hi"), sem("ctx_lo")
        ln_step, root = sem("ln_step"), sem("root")
        turned, turned_out = sem("turned"), sem("turned_out")
        q_ready, q_out = sem("q_ready"), sem("q_out")
        ident_set = sem("ident_set")
        with nc.Block() as block:

            @block.sync
            def _(sp):
                sp.dma_start(x[:], a["x"][0].rearrange("(t p) d -> p t d", p=P)).then_inc(x_loaded, 16)
                sp.dma_start(wq[:], a["L0_xattn_Wq"].rearrange("(k p) n -> p k n", p=P)).then_inc(wq_loaded, 16)
                for n in range(NPIECE):
                    if n >= 2:
                        sp.wait_ge(ctx_lo, n - 1)
                    sp.dma_start(raw[:, n % 2], a["ctxT"].rearrange("(k p) n -> p k n", p=P)[
                        :, :, n * PIECE:(n + 1) * PIECE]).then_inc(raw_loaded[n % 2], 16)

            @block.gpsimd
            def _(pool):
                nc.gpsimd.memset(keep.ident[:], 0.0).then_inc(ident_set, 1)
                nc.gpsimd.memset(keep.ident16[:], 0.0).then_inc(ident_set, 1)
                pool.wait_ge(ident_set, 2)
                for m in (keep.ident, keep.ident16):
                    nc.gpsimd.affine_select(out=m[:], in_=m[:], compare_op=ALU.not_equal, fill=1.0, base=0,
                                            pattern=[[-1, P]], channel_multiplier=1).then_inc(ident_set, 1)

            @block.scalar
            def _(act):
                act.wait_ge(ln_step, LN_VAR)
                nc.scalar.activation(rs[:, 1, :], rs[:, 0, :], ACT.Sqrt).then_inc(root, 1)
                for n in range(NPIECE):
                    act.wait_ge(raw_loaded[n % 2], 16 * (n // 2 + 1))
                    nc.scalar.activation(keep.ctx[:, 0, :, n * PIECE:(n + 1) * PIECE], raw[:, n % 2], ACT.Copy,
                                         scale=CTX_SCALE).then_inc(ctx_hi, 1)
                for n in range(PAIRS):
                    act.wait_ge(q_ready, n + 1)
                    if n >= 2:
                        act.wait_ge(q_stored[n % 2], 16 * (n // 2))
                    nc.scalar.activation(qout[:, n % 2, :], ps[n % 4][:], ACT.Copy).then_inc(q_out, 1)
                    act.wait_ge(q_out, n + 1)
                    act.dma_start(dram.q[n], qout[:, n % 2, :]).then_inc(q_stored[n % 2], 16)
                for s in q_stored:
                    act.wait_ge(s, 16 * PAIRS // 2)

            @block.vector
            def _(dve):
                dve.wait_ge(x_loaded, 16)
                layer_norm_rows(nc, dve, x, xn, stats, mv, rs, ln_step, root)
                for t in range(DT):
                    dve.wait_ge(turned, t + 1)
                    nc.vector.tensor_copy(xnT[:, t, :], ps[t][:]).then_inc(turned_out, 1)
                for n in range(NPIECE):
                    dve.wait_ge(ctx_hi, n + 1)
                    nc.vector.scalar_tensor_tensor(
                        out=keep.ctx[:, 1, :, n * PIECE:(n + 1) * PIECE], in0=raw[:, n % 2], scalar=CTX_SCALE,
                        in1=keep.ctx[:, 0, :, n * PIECE:(n + 1) * PIECE], op0=ALU.mult,
                        op1=ALU.subtract).then_inc(ctx_lo, 1)

            @block.tensor
            def _(pe):
                pe.wait_ge(ident_set, 4)
                pe.wait_ge(ln_step, LN_DONE)
                for d in range(DT):
                    for t in range(QT):
                        i = nc.tensor.transpose(ps[d][:, t * P:(t + 1) * P], xn[:, t, d * P:(d + 1) * P],
                                                keep.ident[:])
                    i.then_inc(turned, 1)
                pe.wait_ge(wq_loaded, 16)
                pe.wait_ge(turned_out, DT)
                for n in range(PAIRS):
                    if n >= 4:
                        pe.wait_ge(q_out, n - 3)
                    for k in range(DT):
                        i = nc.tensor.matmul(ps[n % 4][:], wq[:, k, n * P:(n + 1) * P], xnT[:, k, :],
                                             start=(k == 0), stop=(k == DT - 1))
                    i.then_inc(q_ready, 1)


def cross_attention(nc, a, dram, keep):
    with ExitStack() as ctx:
        sb = lambda name, shape, dt=F32: ctx.enter_context(nc.sbuf_tensor(name, shape, dt))
        sem = lambda name: ctx.enter_context(nc.semaphore(name))
        C = keep.ctx
        SA = sb("sa", [P, 2, 2, CHUNK], F16)
        SB = sb("sb", [P, 2, 2, CHUNK], F16)
        VT = sb("vt", [P, 2, KB, 2, VW], F16)
        QA = sb("qa", [P, 2, 2, T], F16)
        MB = sb("mb", [P, 2, 2, T], F16)
        w_raw = sb("w_raw", [P, 2, CT, P])
        w_hl = sb("w_hl", [P, 2, 2, CT, P], F16)
        q_raw = sb("q_raw", [P, T])
        p32 = sb("p32", [P, 2, 1024])
        ph = sb("ph", [P, RING, 1024], F16)
        pl = sb("pl", [P, RING, 1024], F16)
        acc = sb("acc", [P, 2, 2, 2, DH + 1])
        out = sb("out", [P, QT, 2, DH])
        rec = sb("rec", [P, 2, 2, 2])
        cmx = sb("cmx", [P, 2, QT, KT])
        cm = sb("cm", [P, 2, QT])
        m16 = sb("m16", [P, 2, 2, QT], F16)
        md = sb("md", [P, 2, QT])
        corr = sb("corr", [P, 2, 2, QT])
        ln_p = sb("ln_p", [P, 1])
        ones = sb("ones", [P, 1], F16)
        scored = [ctx.enter_context(nc.psum_tensor(f"scores{i}", [P, 512], F32)) for i in range(RING_S)]
        work = [ctx.enter_context(nc.psum_tensor(f"work{i}", [P, 512], F32)) for i in range(BANKS)]
        O = ctx.enter_context(nc.psum_tensor("pv", [P, 2, 512], F32))
        O_view = O[:, :, 0:2 * VW].rearrange("p b (t n) -> p b t n", n=VW)

        scores_ready, exp_done, ph_ready = sem("scores_ready"), sem("exp_done"), sem("ph_ready")
        pl_ready, av_done, o_free = sem("pl_ready"), sem("av_done"), sem("o_free")
        pl_pool, copied = sem("pl_pool"), sem("copied")
        job_filled, job_free, out_stored = sem("job_filled"), sem("job_free"), sem("out_stored")
        hi_ready, corr_ready = sem("hi_ready"), sem("corr_ready")
        cm_ready, m_ready, md_ready = sem("cm_ready"), sem("m_ready"), sem("md_ready")
        w_loaded, w_hi, w_split = sem("w_loaded"), [sem("wk_hi"), sem("wv_hi")], [sem("wk_split"), sem("wv_split")]
        q_loaded, q_hi, q_set = sem("q_loaded"), sem("q_hi"), sem("q_set")
        o_part, out_rec, out_norm = sem("o_part"), sem("out_rec"), sem("out_norm")
        consts_set = sem("consts_set")

        def after(n):
            return n + 1 + HEAD

        def count_of(job):
            return 2 if job == EARLY[-1] else 1

        def score_bank(i):
            k = i % (2 * PSTEPS)
            return scored[k % RING_S], RING_S if k >= 2 * PSTEPS % RING_S else 2 * PSTEPS % RING_S

        def early(item, job):
            return item * JOBS + NUMBER[job]

        def where(p, s, last):
            c, d = divmod(s % PSTEPS, STEPS)
            pair = p + s // PSTEPS
            return pair, c, d, pair * NCHUNK + c, None if last and c == NCHUNK - 1 else (c + 1) % NCHUNK

        def corr_count(pair, c, h):
            return (pair * (NCHUNK - 1) + c - 1) * 2 + h + 1

        def jobs_of(p, s, last):
            pair, c, d, item, nxt = where(p, s, last)
            number = NUMBER if nxt is not None else LAST_NUMBER
            for job, late in PLAN[d]:
                if late or nxt is not None:
                    n = number[job]
                    of = (pair, item, c) if late else (pair + 1 if nxt == 0 else pair, item + 1, nxt)
                    yield ((item + 1) * JOBS + n, n % BANKS, job) + of

        def run_pairs(eng, step, finish):
            for s in range(LAG):
                step(0, s, False)
            with eng.Fori(0, PAIRS - 1) as p:
                for s in range(LAG, PSTEPS + LAG):
                    step(p, s, False)
            for s in range(LAG, PSTEPS):
                step(PAIRS - 1, s, True)
            finish()

        with nc.Block() as block:

            @block.sync
            def _(sp):
                def load_w(p):
                    for n, w in enumerate(("wk_pairs", "wv_pairs")):
                        sp.dma_start(w_raw[:, n].rearrange("p k n -> p (k n)"),
                                     a[w][one_of(p)].rearrange("a p n -> (a p) n")).then_inc(w_loaded, 16)

                def load_q(p):
                    sp.dma_start(q_raw[:], dram.q[one_of(p)].rearrange("a p n -> (a p) n")).then_inc(q_loaded, 16)

                def pair(p, last):
                    if not last:
                        for s in w_split:
                            sp.wait_ge(s, p + 1)
                        load_w(p + 1)
                        sp.wait_ge(q_set, 2 * p + 2)
                        load_q(p + 1)
                    sp.wait_ge(out_norm, after(p))
                    sp.dma_start(dram.o[one_of(p)].rearrange("a p n -> (a p) n"),
                                 out[:].rearrange("p t h d -> p (t h d)")).then_inc(out_stored, 16)

                sp.sem_inc(out_stored, HEAD)
                load_w(0)
                load_q(0)
                with sp.Fori(0, PAIRS - 1) as p:
                    pair(p, False)
                pair(PAIRS - 1, True)
                sp.wait_ge(out_stored, 16 * PAIRS + HEAD)

            @block.gpsimd
            def _(pool):
                nc.gpsimd.memset(ln_p[:], math.log(P_SCALE)).then_inc(consts_set, 1)
                nc.gpsimd.memset(ones[:], 1.0).then_inc(consts_set, 1)
                nc.gpsimd.memset(VT[:, :, :, :, DH:DH + 1], KV_SCALE).then_inc(consts_set, 1)
                pool.wait_ge(consts_set, 3)
                nc.gpsimd.memset(SB[DH:DH + 1], M_UNIT).then_inc(consts_set, 1)

                def low(item, c, d):
                    g = item * STEPS + d
                    cols = slice(2 * T - POOL_COLS, 2 * T)
                    pool.wait_ge(ph_ready, after(g))
                    pool.wait_ge(pl_pool, after(g - 1))
                    pool.wait_ge(copied, copies(item, c, d))
                    nc.gpsimd.tensor_tensor(pl[:, d % RING, cols], p32[:, d % 2, cols], ph[:, d % RING, cols],
                                            ALU.subtract).then_inc(pl_pool, 1)

                def copies(item, c, d):
                    k_jobs = sum(job[0] == "K" for step in PLAN[:d + 1] for job, _ in step)
                    ahead = 0 if c is None else k_jobs
                    return 2 * (KV_JOBS * (item + 1) + ahead)

                def copy(n, bank, job, pair, item, c, low_done=None):
                    if job[0] == "K":
                        if low_done is not None:
                            pool.wait_ge(pl_pool, after(low_done))
                        par, keys = c % 2, slice(job[1] * KV_KEYS, (job[1] + 1) * KV_KEYS)
                        for h in range(2):
                            pool.wait_ge(hi_ready, (item * len(KV_ORDER) + KV_ORDER[job]) * 2 + h + 1)
                            rows = slice(h * DH, (h + 1) * DH)
                            before = (item * KV_JOBS + job[1]) * 2 + h
                            if job[1] + h > 0 or low_done is not None:
                                pool.wait_ge(copied, before)
                            nc.gpsimd.tensor_tensor(SB[0:DH, par, h, keys], SA[rows, par, h, keys],
                                                    ones[rows, :].to_broadcast([DH, KV_KEYS]),
                                                    ALU.mult).then_inc(copied, 1)

                def step(p, s, last):
                    _, _, d, item, nxt = where(p, s, last)
                    if s >= 1:
                        _, _, d1, item1, nxt1 = where(p, s - 1, last)
                        low(item1, nxt1, d1)
                    for j in jobs_of(p, s, last):
                        copy(*j, low_done=item * STEPS + d - 1)
                    if s == PSTEPS + LAG - 1:
                        normalise(p, copies(item, nxt, d))

                def normalise(pair, copies_before):
                    pool.wait_ge(copied, copies_before)
                    pool.wait_ge(out_rec, pair + 1)
                    pool.wait_ge(out_stored, 16 * pair + HEAD)
                    for h in range(2):
                        i = nc.gpsimd.tensor_tensor(
                            out[:, :, h, :], acc[:, h, :, :, 0:DH].rearrange("p b t d -> p (b t) d"),
                            rec[:, h].rearrange("p b t -> p (b t)").unsqueeze(2).to_broadcast([P, QT, DH]), ALU.mult)
                    i.then_inc(out_norm, 1)

                def finish():
                    low(PAIRS * NCHUNK - 1, None, STEPS - 1)
                    normalise(PAIRS - 1, 2 * KV_JOBS * PAIRS * NCHUNK)

                pool.sem_inc(pl_pool, HEAD)
                pool.sem_inc(out_norm, HEAD)
                for job in EARLY:
                    copy(0, 0, job, 0, 0, 0)
                run_pairs(pool, step, finish)

            @block.tensor
            def _(pe):
                def fill(n, bank, job, item, c, k_done):
                    W, par = work[bank], c % 2
                    pe.wait_ge(job_free, after(n - BANKS))
                    if job[0] == "K":
                        keys = slice(c * CHUNK + job[1] * KV_KEYS, c * CHUNK + (job[1] + 1) * KV_KEYS)
                        for k in range(CT):
                            for w, x in [(0, 0), (0, 1), (1, 0)]:
                                i = nc.tensor.matmul(W[:, 0:KV_KEYS], w_hl[:, 0, w, k, :], C[:, x, k, keys],
                                                     start=(k == 0 and (w, x) == (0, 0)),
                                                     stop=(k == CT - 1 and (w, x) == (1, 0)))
                    elif job[0] == "V":
                        for b in range(KV_KEYS // P):
                            k0 = c * CHUNK + job[1] * KV_KEYS + b * P
                            for k in range(CT):
                                for x, w in [(0, 0), (0, 1), (1, 0)]:
                                    i = nc.tensor.matmul(W[:, b * P:(b + 1) * P], C[:, x, k, k0:k0 + P],
                                                         w_hl[:, 1, w, k, :],
                                                         start=(k == 0 and (x, w) == (0, 0)),
                                                         stop=(k == CT - 1 and (x, w) == (1, 0)))
                    elif job[0] == "M":
                        _, h, q, kt = job
                        if h == 0:
                            pe.wait_ge(job_free, after(k_done(("K", 2 * kt + 1))))
                        i = nc.tensor.matmul(W[:], QA[:, par, h, q * P:(q + 1) * P],
                                             SA[:, par, h, kt * 512:(kt + 1) * 512], start=True, stop=True)
                    else:
                        h = job[1]
                        pe.wait_ge(m_ready, 2 * item + h + 1)
                        for q in range(QT):
                            i = nc.tensor.matmul(W[0:1, q * P:(q + 1) * P], m16[:, par, h, q:q + 1],
                                                 keep.ident16[:], start=True, stop=True)
                    i.then_inc(job_filled, count_of(job))

                def scores(item, c, d, b, nxt):
                    n = 2 * (item * STEPS + d) + b
                    bank, ago = score_bank(2 * (c * STEPS + d) + b)
                    h, par = d // DUOS, c % 2
                    if b == 0:
                        if d == 0:
                            pe.wait_ge(job_free, after(early(item, ("R", 0))))
                            pe.wait_ge(copied, (item + 1) * 2 * KV_JOBS)
                        if d == DUOS:
                            late = NUMBER if nxt is not None else LAST_NUMBER
                            pe.wait_ge(job_free, after((item + 1) * JOBS + late[("R", 1)]))
                    pe.wait_ge(exp_done, after(n - ago))
                    kb = (d % DUOS) * 2 + b
                    nc.tensor.matmul(bank[:], SA[:, par, h, kb * P:(kb + 1) * P],
                                     QA[:, par, h, :], start=True, stop=False)
                    i = nc.tensor.matmul(bank[:], SB[0:DH + 1, par, h, kb * P:(kb + 1) * P],
                                         MB[0:DH + 1, par, h, :], start=False, stop=True)
                    i.then_inc(scores_ready, 1)

                def weigh(item, c, d, b):
                    g = item * STEPS + d
                    h, par, at = d // DUOS, c % 2, d % RING
                    if b == 0:
                        if d == 0:
                            pe.wait_ge(job_free, after(early(item, EARLY[-1]) + 1))
                        if d % DUOS == 0:
                            pe.wait_ge(o_free, after(2 * item + h - 1))
                        pe.wait_ge(pl_ready, after(g))
                    if b == 1:
                        pe.wait_ge(pl_pool, after(g))
                    kb = (d % DUOS) * 2 + b
                    for q in range(QT):
                        o = (q % 2) * VW
                        cols = slice(b * T + q * P, b * T + (q + 1) * P)
                        nc.tensor.matmul(O[:, q // 2, o:o + VW], ph[:, at, cols], VT[:, par, kb, h, :],
                                         start=(kb == 0 and q % 2 == 0), stop=False, skip_group_check=True)
                        i = nc.tensor.matmul(O[:, q // 2, o:o + DH + 1], pl[:, at, cols],
                                             VT[:, par, kb, h, 0:DH + 1], start=False,
                                             stop=(kb == KB - 1), skip_group_check=True)
                    if b == 1:
                        i.then_inc(av_done, 1)

                def step(p, s, last):
                    pair, c, d, item, nxt = where(p, s, last)
                    jobs = [(n, bank, job, it, ch, lambda k: (item + 1) * JOBS + NUMBER[k])
                            for n, bank, job, _, it, ch in jobs_of(p, s, last)]
                    if nxt == 0:
                        if d < 3 and d % 2 == 0:
                            pe.wait_ge(w_split[d // 2], pair + 2)
                    if nxt is not None and nxt < 2 and d == 2:
                        pe.wait_ge(q_set, 2 * pair + (3 if nxt == 0 else 2))
                    scores(item, c, d, 0, nxt)
                    for j in jobs[0:1]:
                        fill(*j)
                    scores(item, c, d, 1, nxt)
                    for j in jobs[1:2]:
                        fill(*j)
                    lagging = None
                    if s >= LAG:
                        _, c2, d2, item2, _ = where(p, s - LAG, last)
                        weigh(item2, c2, d2, 0)
                    for j in jobs[2:3]:
                        fill(*j)
                    if s >= LAG:
                        weigh(item2, c2, d2, 1)
                    for j in jobs[3:]:
                        fill(*j)

                def finish():
                    for d in range(STEPS - LAG, STEPS):
                        for b in range(2):
                            weigh(PAIRS * NCHUNK - 1, NCHUNK - 1, d, b)

                for s, n in ((scores_ready, 0), (av_done, 0), (job_filled, LATE)):
                    pe.sem_inc(s, HEAD + n)
                pe.wait_ge(consts_set, 4)
                for s in w_split:
                    pe.wait_ge(s, 1)
                pe.wait_ge(q_set, 1)
                for job in EARLY:
                    n = FIRST_NUMBER[job]
                    fill(n, n % BANKS, job, 0, 0, FIRST_NUMBER.__getitem__)
                run_pairs(pe, step, finish)

            @block.scalar
            def _(act):
                def w_high(n, p, job_number=None):
                    act.wait_ge(w_loaded, 32 * p + 32)
                    if job_number is not None:
                        act.wait_ge(job_filled, after(job_number))
                    nc.scalar.activation(w_hl[:, n, 0], w_raw[:, n], ACT.Copy, scale=W_SCALE).then_inc(w_hi[n], 1)

                def q_high(p, par):
                    act.wait_ge(q_loaded, 16 * p + 16)
                    for h in range(2):
                        for rows in (slice(0, DH), slice(DH, P)):
                            i = nc.scalar.activation(QA[rows, par, h, :], q_raw[h * DH:(h + 1) * DH, :], ACT.Copy,
                                                     scale=Q_SCALE)
                    i.then_inc(q_hi, 1)

                def drain(n, bank, job, pair, item, c):
                    W, par = work[bank], c % 2
                    if job[0] == "K":
                        keys = slice(job[1] * KV_KEYS, (job[1] + 1) * KV_KEYS)
                        act.wait_ge(job_filled, after(n))
                        for h in range(2):
                            rows = slice(h * DH, (h + 1) * DH)
                            nc.scalar.activation(SA[rows, par, h, keys], W[rows, 0:KV_KEYS], ACT.Copy,
                                                 scale=KV_EVAC).then_inc(hi_ready, 1)
                    elif job[0] == "V":
                        act.wait_ge(job_filled, after(n))
                        v = VT[:, par, job[1] * 2:(job[1] + 1) * 2].rearrange("p k h n -> p (k h) n")
                        nc.scalar.activation(v[:, :, 0:DH], W[:, 0:KV_KEYS].rearrange("p (k n) -> p k n", n=DH),
                                             ACT.Copy, scale=KV_EVAC).then_inc(hi_ready, 2)
                    elif job[0] == "R" and c > 0:
                        h = job[1]
                        act.wait_ge(md_ready, corr_count(pair, c, h))
                        nc.scalar.activation(corr[:, par, h, :], md[:, h, :], ACT.Exp,
                                             scale=M_UNIT * EXP_SCALE).then_inc(corr_ready, 1)

                def exp(item, c, d, b):
                    g = item * STEPS + d
                    bank, _ = score_bank(2 * (c * STEPS + d) + b)
                    act.wait_ge(scores_ready, after(2 * g + b))
                    if b == 0:
                        act.wait_ge(pl_ready, after(g - 2))
                        act.wait_ge(pl_pool, after(g - 2))
                    nc.scalar.activation(p32[:, d % 2, b * T:(b + 1) * T], bank[:], ACT.Exp,
                                         bias=ln_p[:], scale=EXP_SCALE).then_inc(exp_done, 1)

                def step(p, s, last):
                    pair, c, d, item, nxt = where(p, s, last)
                    g = item * STEPS + d
                    jobs = list(jobs_of(p, s, last))
                    exp(item, c, d, 0)
                    for j in jobs[:1]:
                        drain(*j)
                    exp(item, c, d, 1)
                    if nxt is not None and nxt < 2 and d == 0:
                        act.wait_ge(scores_ready, after(2 * item * STEPS - 1))
                        q_high(pair + 1 if nxt == 0 else pair, nxt)
                    if nxt == 0 and d == 0:
                        w_high(1, pair + 1, early(item, ("V", KV_JOBS - 1)))
                    for j in jobs[1:]:
                        drain(*j)
                    if nxt == NCHUNK - 1 and d == WK_STEP and not last:
                        w_high(0, pair + 1, early(item + 1, ("K", KV_JOBS - 1)))
                    act.wait_ge(av_done, after(g - RING))
                    act.wait_ge(exp_done, after(2 * g + 1))
                    nc.scalar.activation(ph[:, d % RING, :], p32[:, d % 2, :], ACT.Copy).then_inc(ph_ready, 1)

                for s in (exp_done, ph_ready):
                    act.sem_inc(s, HEAD)
                act.wait_ge(consts_set, 4)
                w_high(0, 0)
                w_high(1, 0)
                q_high(0, 0)
                for job in EARLY:
                    n = FIRST_NUMBER[job]
                    drain(n, n % BANKS, job, 0, 0, 0)
                run_pairs(act, step, lambda: None)

            @block.vector
            def _(dve):
                def w_low(n, p):
                    dve.wait_ge(w_hi[n], p + 1)
                    nc.vector.scalar_tensor_tensor(out=w_hl[:, n, 1], in0=w_raw[:, n], scalar=W_SCALE,
                                                   in1=w_hl[:, n, 0], op0=ALU.mult,
                                                   op1=ALU.subtract).then_inc(w_split[n], 1)

                def q_low(n, par):
                    dve.wait_ge(q_hi, n)
                    for h in range(2):
                        rows = slice(h * DH, (h + 1) * DH)
                        i = nc.vector.scalar_tensor_tensor(out=MB[0:DH, par, h, :], in0=q_raw[rows, :], scalar=Q_SCALE,
                                                           in1=QA[rows, par, h, :], op0=ALU.mult, op1=ALU.subtract)
                    i.then_inc(q_set, 1)

                def new_maximum(n, pair, item, c, h):
                    par = c % 2
                    dve.wait_ge(job_free, after(n))
                    nc.vector.tensor_reduce(cm[:, h, :], cmx[:, h], X_AXIS, ALU.max).then_inc(cm_ready, 1)
                    dve.wait_ge(cm_ready, 2 * item + h + 1)
                    if c == 0:
                        nc.vector.tensor_scalar(m16[:, par, h, :], cm[:, h, :], 1.0 / M_UNIT, None,
                                                ALU.mult).then_inc(m_ready, 1)
                        return
                    nc.vector.scalar_tensor_tensor(out=m16[:, par, h, :], in0=cm[:, h, :], scalar=1.0 / M_UNIT,
                                                   in1=m16[:, 1 - par, h, :], op0=ALU.mult,
                                                   op1=ALU.max).then_inc(m_ready, 1)
                    dve.wait_ge(m_ready, 2 * item + h + 1)
                    nc.vector.tensor_tensor(md[:, h, :], m16[:, 1 - par, h, :], m16[:, par, h, :],
                                            ALU.subtract).then_inc(md_ready, 1)

                def drain(n, bank, job, pair, item, c):
                    W, par = work[bank], c % 2
                    if job[0] in "KV":
                        hi_count = (item * len(KV_ORDER) + KV_ORDER[job]) * 2
                    if job[0] == "K":
                        keys = slice(job[1] * KV_KEYS, (job[1] + 1) * KV_KEYS)
                        for h in range(2):
                            hi, lo = (slice(0, DH), slice(DH, P)) if h == 0 else (slice(DH, P), slice(0, DH))
                            dve.wait_ge(hi_ready, hi_count + h + 1)
                            i = nc.vector.scalar_tensor_tensor(
                                out=SA[lo, par, h, keys], in0=W[hi, 0:KV_KEYS], scalar=KV_EVAC,
                                in1=SA[hi, par, h, keys], op0=ALU.mult, op1=ALU.subtract)
                        i.then_inc(job_free, 1)
                    elif job[0] == "V":
                        dve.wait_ge(hi_ready, hi_count + 2)
                        v = VT[:, par, job[1] * 2:(job[1] + 1) * 2].rearrange("p k h n -> p (k h) n")
                        nc.vector.scalar_tensor_tensor(
                            out=v[:, :, DH + 1:VW], in0=W[:, 0:KV_KEYS].rearrange("p (k n) -> p k n", n=DH),
                            scalar=KV_EVAC, in1=v[:, :, 0:DH], op0=ALU.mult,
                            op1=ALU.subtract).then_inc(job_free, count_of(job))
                    elif job[0] == "M":
                        _, h, q, kt = job
                        dve.wait_ge(job_filled, after(n))
                        nc.vector.tensor_reduce(cmx[:, h, q, kt:kt + 1], W[:], X_AXIS,
                                                ALU.max).then_inc(job_free, count_of(job))
                        if job == LAST_MAX[h]:
                            new_maximum(n, pair, item, c, h)
                    else:
                        h = job[1]
                        dve.wait_ge(job_filled, after(n))
                        nc.vector.tensor_scalar(MB[DH:DH + 1, par, h, :], W[0:1, :], -1.0, None,
                                                ALU.mult).then_inc(job_free, count_of(job))

                def low(item, d):
                    g = item * STEPS + d
                    dve.wait_ge(ph_ready, after(g))
                    cols = slice(0, 2 * T - POOL_COLS)
                    nc.vector.tensor_tensor(pl[:, d % RING, cols], p32[:, d % 2, cols], ph[:, d % RING, cols],
                                            ALU.subtract).then_inc(pl_ready, 1)

                def gather(pair, item, c, h):
                    unit = 2 * item + h
                    par = c % 2
                    dve.wait_ge(av_done, after(unit * DUOS + DUOS - 1))
                    if c == 0:
                        if h == 0:
                            dve.wait_ge(out_norm, after(pair - 1))
                        for b in range(2):
                            i = nc.vector.tensor_copy(acc[:, h, b], O_view[:, b, :, 0:DH + 1])
                    else:
                        dve.wait_ge(corr_ready, corr_count(pair, c, h))
                        for q in range(QT):
                            i = nc.vector.scalar_tensor_tensor(
                                out=acc[:, h, q // 2, q % 2, :], in0=acc[:, h, q // 2, q % 2, :],
                                scalar=corr[:, par, h, q:q + 1], in1=O_view[:, q // 2, q % 2, 0:DH + 1],
                                op0=ALU.mult, op1=ALU.add)
                    i.then_inc(o_part, 1)
                    dve.wait_ge(o_part, unit + 1)
                    for b in range(2):
                        i = nc.vector.tensor_tensor(acc[:, h, b, :, 0:DH], acc[:, h, b, :, 0:DH],
                                                    O_view[:, b, :, DH + 1:VW], ALU.add)
                    i.then_inc(o_free, 1)

                def finish_pair(pair, item):
                    dve.wait_ge(o_free, after(2 * item + 1))
                    nc.vector.reciprocal(rec[:], acc[:, :, :, :, DH]).then_inc(out_rec, 1)

                def step(p, s, last):
                    pair, c, d, item, nxt = where(p, s, last)
                    if s >= 1:
                        _, _, d1, item1, _ = where(p, s - 1, last)
                        low(item1, d1)
                    if nxt is not None and nxt < 2 and d == 0:
                        q_low(2 * pair + (3 if nxt == 0 else 2), nxt)
                    if nxt == 0 and d == 0:
                        w_low(1, pair + 1)
                    for j in jobs_of(p, s, last):
                        drain(*j)
                    if nxt == NCHUNK - 1 and d == WK_STEP and not last:
                        w_low(0, pair + 1)
                    if d == DUOS + LAG - 1:
                        gather(pair, item, c, 0)
                    if d == LAG - 1 and s >= STEPS:
                        pair0, c0, _, item0, _ = where(p, s - STEPS, last)
                        gather(pair0, item0, c0, 1)
                        if c0 == NCHUNK - 1:
                            finish_pair(pair0, item0)

                def finish():
                    item = PAIRS * NCHUNK - 1
                    low(item, STEPS - 1)
                    gather(PAIRS - 1, item, NCHUNK - 1, 1)
                    finish_pair(PAIRS - 1, item)

                for s, n in ((pl_ready, 0), (o_free, 0), (job_free, LATE)):
                    dve.sem_inc(s, HEAD + n)
                w_low(0, 0)
                w_low(1, 0)
                q_low(1, 0)
                for job in EARLY:
                    n = FIRST_NUMBER[job]
                    drain(n, n % BANKS, job, 0, 0, 0)
                run_pairs(dve, step, finish)


def rope_constants():
    inv = (np.float32(1.0) / np.float32(10000.0) ** (np.arange(0, DS, 2, dtype=np.float32) / np.float32(DS)))
    angle = np.outer(np.arange(T, dtype=np.float32), inv.astype(np.float32)).astype(np.float32)
    angle = np.concatenate([angle, angle], axis=-1).T
    turn = np.zeros((P, P), np.float32)
    for n in range(P):
        d = n % DS
        if d < DS // 2:
            turn[n + DS // 2, n] = -1.0
        else:
            turn[n - DS // 2, n] = 1.0
    tile4 = lambda t: np.ascontiguousarray(np.tile(t, (P // DS, 1)).astype(np.float32))
    return tile4(np.cos(angle)), tile4(np.sin(angle)), turn


def self_attention(nc, a, dram, keep, x):
    with ExitStack() as ctx:
        sb = lambda name, shape, dt=F32: ctx.enter_context(nc.sbuf_tensor(name, shape, dt))
        sem = lambda name: ctx.enter_context(nc.semaphore(name))
        ident = keep.ident
        big = sb("big", [P, PAIRS, T])
        o_all = sb("o_all", [P, PAIRS, QT, P])
        wo_x = sb("wo_x", [P, PAIRS, D])
        bo = sb("bo", [P, D])
        xn = sb("xn_t", [P, QT, D])
        xT = sb("xT", [P, DT, T])
        w_at = {n: sb(f"w_{n}", [P, DT, D]) for n in ("Wq", "Wk", "Wv", "Wo")}
        cos, sin, turn, causal = sb("cos", [P, T]), sb("sin", [P, T]), sb("turn", [P, P]), sb("causal", [P, P])
        qk = sb("qk", [P, 2 * DT, T])
        v = sb("v", [P, QT, D])
        r0, r1, r2 = sb("r0", [P, T]), sb("r1", [P, T]), sb("r2", [P, T])
        pr = sb("pr", [P, 2, QT, T])
        pT = sb("pT", [P, 2, QT, T])
        mx, nb = sb("mx", [P, HS, QT]), sb("nb", [P, HS, QT])
        rsum, rrec = sb("rsum", [P, HS, QT]), sb("rrec", [P, HS, QT])
        stats, mv = sb("stats_t", [P, QT, 6]), sb("mv_t", [P, QT, 2])
        rs = sb("rs_t", [P, 7, QT])
        bank = [ctx.enter_context(nc.psum_tensor(f"bank{i}", [P, 512], F32)) for i in range(8)]
        oT = big

        loaded = {n: sem(f"loaded_{n}") for n in ("o", "wo_x", "x", "bo", "Wq", "Wk", "Wv", "Wo", "rope")}
        o_turned, o_turned_out, y_ready, x1_ready = sem("o_turned"), sem("o_turned_out"), sem("y_ready"), sem("x1_ready")
        ln_step, root = sem("ln_step1"), sem("root1")
        x_turned, x_turned_out = sem("x_turned"), sem("x_turned_out")
        proj, proj_out, rotated, rope_step, rope_done = (sem("proj"), sem("proj_out"), sem("rotated"),
                                                         sem("rope_step"), sem("rope_done"))
        v_ready, v_out = sem("v_ready"), sem("v_out")
        s_ready, s_masked, s_max, s_bias, s_exp, s_rec, s_norm = (sem("s_ready"), sem("s_masked"), sem("s_max"), sem(
            "s_bias"), sem("s_exp"), sem("s_rec"), sem("s_norm"))
        p_turned, p_turned_out, av_ready, av_out = sem("p_turned"), sem("p_turned_out"), sem("av_ready"), sem("av_out")
        z_ready, x2_ready = sem("z_ready"), sem("x2_ready")

        S_AT = {3: (0, 0), 2: (1, 0), 0: (1, 384), 1: (2, 0)}
        T_AT = {0: (3, 0), 1: (4, 0), 3: (4, 384), 2: (5, 0)}

        with nc.Block() as block:

            @block.sync
            def _(sp):
                for t in range(QT):
                    sp.dma_start(o_all[:, :, t, :], dram.o.rearrange("a p (t n) -> p a t n", t=QT)[:, :, t, :]
                                 ).then_inc(loaded["o"], 16)
                sp.dma_start(wo_x[:], a["L0_xattn_Wo"].rearrange("(k p) n -> p k n", p=P)).then_inc(loaded["wo_x"], 16)
                sp.dma_start(x[:], a["x"][0].rearrange("(t p) d -> p t d", p=P)).then_inc(loaded["x"], 16)
                sp.dma_start(bo[:], a["L0_xattn_bo"].rearrange("(o n) -> o n", o=1).broadcast_to([P, D])
                             ).then_inc(loaded["bo"], 16)
                for n in ("Wq", "Wk", "Wv", "Wo"):
                    sp.dma_start(w_at[n][:], a[f"attn_{n}T"].rearrange("(k p) n -> p k n", p=P)).then_inc(loaded[n], 16)
                for t, n in ((cos, "rope_cos"), (sin, "rope_sin"), (turn, "rope_turn"), (causal, "causal")):
                    sp.dma_start(t[:], a[n]).then_inc(loaded["rope"], 16)

            @block.tensor
            def _(pe):
                pe.wait_ge(loaded["o"], 16 * QT)
                for n in range(PAIRS):
                    if n >= 4:
                        pe.wait_ge(o_turned_out, n - 3)
                    for t in range(QT):
                        i = nc.tensor.transpose(bank[n % 4][:, t * P:(t + 1) * P], o_all[:, n, t, :], ident[:])
                    i.then_inc(o_turned, 1)
                pe.wait_ge(loaded["wo_x"], 16)
                pe.wait_ge(o_turned_out, PAIRS)
                for t in range(QT):
                    for k in range(PAIRS):
                        i = nc.tensor.matmul(bank[4 + t][:], oT[:, k, t * P:(t + 1) * P], wo_x[:, k, :],
                                             start=(k == 0), stop=(k == PAIRS - 1))
                    i.then_inc(y_ready, 1)
                pe.wait_ge(ln_step, LN_DONE)
                for d in range(DT):
                    for t in range(QT):
                        i = nc.tensor.transpose(bank[d][:, t * P:(t + 1) * P], xn[:, t, d * P:(d + 1) * P], ident[:])
                    i.then_inc(x_turned, 1)
                pe.wait_ge(x_turned_out, DT)
                for n in range(2 * DT):
                    name, m = ("Wq", n) if n < DT else ("Wk", n - DT)
                    if m == 0:
                        pe.wait_ge(loaded[name], 16)
                        pe.wait_ge(loaded["rope"], 64)
                    if n >= 4:
                        pe.wait_ge(rope_done, n - 3)
                    for k in range(DT):
                        i = nc.tensor.matmul(bank[4 + n % 4][:], w_at[name][:, k, m * P:(m + 1) * P], xT[:, k, :],
                                             start=(k == 0), stop=(k == DT - 1))
                    i.then_inc(proj, 1)
                    if n >= 1:
                        pe.wait_ge(proj_out, n)
                        nc.tensor.matmul(bank[(n - 1) % 4][:], turn[:], qk[:, n - 1, :], start=True,
                                         stop=True).then_inc(rotated, 1)
                pe.wait_ge(proj_out, 2 * DT)
                nc.tensor.matmul(bank[(2 * DT - 1) % 4][:], turn[:], qk[:, 2 * DT - 1, :], start=True,
                                 stop=True).then_inc(rotated, 1)
                pe.wait_ge(loaded["Wv"], 16)
                pe.wait_ge(rope_done, 2 * DT)
                for t in range(QT):
                    for k in range(DT):
                        i = nc.tensor.matmul(bank[4 + t][:], xT[:, k, t * P:(t + 1) * P], w_at["Wv"][:, k, :],
                                             start=(k == 0), stop=(k == DT - 1))
                    i.then_inc(v_ready, 1)
                pe.wait_ge(v_out, QT)

                def head_scores(n):
                    rows, tile = slice(n % 4 * DS, n % 4 * DS + DS), n // 4
                    if n >= 1:
                        pe.wait_ge(s_exp, n)
                    for t in (3, 2, 0, 1):
                        b, o = S_AT[t]
                        i = nc.tensor.matmul(bank[b][:, o:o + (t + 1) * P], qk[rows, tile, t * P:(t + 1) * P],
                                             qk[rows, DT + tile, 0:(t + 1) * P], start=True, stop=True)
                    i.then_inc(s_ready, 1)

                head_scores(0)
                for n in range(HS):
                    if n + 1 < HS:
                        head_scores(n + 1)
                    pe.wait_ge(s_norm, n + 1)
                    if n >= 1:
                        pe.wait_ge(p_turned_out, n)
                    for k in (0, 1, 3, 2):
                        b, o = T_AT[k]
                        for t in range(k, QT):
                            i = nc.tensor.transpose(bank[b][:, o + (t - k) * P:o + (t - k + 1) * P],
                                                    pr[:, n % 2, t, k * P:(k + 1) * P], ident[:])
                    i.then_inc(p_turned, 1)
                    pe.wait_ge(p_turned_out, n + 1)
                    rows, out_bank = slice(n % 4 * DS, n % 4 * DS + DS), bank[6 + n // 4 % 2]
                    if n % 4 == 0 and n >= 8:
                        pe.wait_ge(av_out, n // 4 - 1)
                    for k in range(QT):
                        i = nc.tensor.matmul(out_bank[rows, k * P:T], v[:, k, n * DS:(n + 1) * DS],
                                             pT[:, n % 2, k, k * P:T], start=(k == 0), stop=(k == QT - 1))
                    if n % 4 == 3:
                        i.then_inc(av_ready, 1)
                pe.wait_ge(loaded["Wo"], 16)
                pe.wait_ge(av_out, DT)
                for t in range(QT):
                    for k in range(DT):
                        i = nc.tensor.matmul(bank[t][:], oT[:, k, t * P:(t + 1) * P], w_at["Wo"][:, k, :],
                                             start=(k == 0), stop=(k == DT - 1))
                    i.then_inc(z_ready, 1)

            @block.scalar
            def _(act):
                act.wait_ge(ln_step, LN_VAR)
                nc.scalar.activation(rs[:, 1, :], rs[:, 0, :], ACT.Sqrt).then_inc(root, 1)
                for n in range(2 * DT):
                    act.wait_ge(proj, n + 1)
                    nc.scalar.activation(qk[:, n, :], bank[4 + n % 4][:], ACT.Copy).then_inc(proj_out, 1)
                for t in range(QT):
                    act.wait_ge(v_ready, t + 1)
                    nc.scalar.activation(v[:, t, :], bank[4 + t][:], ACT.Copy).then_inc(v_out, 1)

                def exps(n):
                    act.wait_ge(s_bias, n + 1)
                    if n >= 2:
                        act.wait_ge(p_turned, n - 1)
                    for t in range(QT):
                        b, o = S_AT[t]
                        i = nc.scalar.activation(pr[:, n % 2, t, 0:(t + 1) * P], bank[b][:, o:o + (t + 1) * P], ACT.Exp,
                                                 bias=nb[:, n, t:t + 1], scale=1.0 / math.sqrt(DS),
                                                 accum_out=rsum[:, n, t:t + 1])
                    i.then_inc(s_exp, 1)

                exps(0)
                for n in range(HS):
                    if n + 1 < HS:
                        exps(n + 1)
                    act.wait_ge(p_turned, n + 1)
                    for k in range(QT):
                        b, o = T_AT[k]
                        i = nc.scalar.activation(pT[:, n % 2, k, k * P:T], bank[b][:, o:o + (QT - k) * P], ACT.Copy)
                    i.then_inc(p_turned_out, 1)
                    if n % 4 == 3:
                        act.wait_ge(av_ready, n // 4 + 1)
                        nc.scalar.activation(oT[:, n // 4, :], bank[6 + n // 4 % 2][:], ACT.Copy).then_inc(av_out, 1)

            @block.vector
            def _(dve):
                for n in range(PAIRS):
                    dve.wait_ge(o_turned, n + 1)
                    nc.vector.tensor_copy(oT[:, n, :], bank[n % 4][:]).then_inc(o_turned_out, 1)
                dve.wait_ge(loaded["x"], 16)
                dve.wait_ge(loaded["bo"], 16)
                for t in range(QT):
                    i = nc.vector.tensor_tensor(x[:, t, :], x[:, t, :], bo[:], ALU.add)
                i.then_inc(x1_ready, 1)
                dve.wait_ge(x1_ready, 1)
                for t in range(QT):
                    dve.wait_ge(y_ready, t + 1)
                    nc.vector.tensor_tensor(x[:, t, :], x[:, t, :], bank[4 + t][:], ALU.add).then_inc(x1_ready, 1)
                dve.wait_ge(x1_ready, 1 + QT)
                layer_norm_rows(nc, dve, x, xn, stats, mv, rs, ln_step, root)
                for d in range(DT):
                    dve.wait_ge(x_turned, d + 1)
                    nc.vector.tensor_copy(xT[:, d, :], bank[d][:]).then_inc(x_turned_out, 1)
                for n in range(2 * DT):
                    dve.wait_ge(rotated, n + 1)
                    if n >= 1:
                        dve.wait_ge(rope_done, n)
                    nc.vector.tensor_tensor(r0[:], bank[n % 4][:], sin[:], ALU.mult).then_inc(rope_step, 1)
                    nc.vector.tensor_tensor(r1[:], qk[:, n, :], cos[:], ALU.mult).then_inc(rope_step, 1)
                    dve.wait_ge(rope_step, 2 * n + 2)
                    nc.vector.tensor_tensor(qk[:, n, :], r0[:], r1[:], ALU.add).then_inc(rope_done, 1)

                def soft(n):
                    dve.wait_ge(s_ready, n + 1)
                    for t in range(QT):
                        b, o = S_AT[t]
                        diag = bank[b][:, o + t * P:o + (t + 1) * P]
                        i = nc.vector.tensor_tensor(diag, diag, causal[:], ALU.add)
                    i.then_inc(s_masked, 1)
                    dve.wait_ge(s_masked, n + 1)
                    for t in range(QT):
                        b, o = S_AT[t]
                        i = nc.vector.tensor_reduce(mx[:, n, t:t + 1], bank[b][:, o:o + (t + 1) * P], X_AXIS, ALU.max)
                    i.then_inc(s_max, 1)
                    dve.wait_ge(s_max, n + 1)
                    nc.vector.tensor_scalar(nb[:, n, :], mx[:, n, :], -1.0 / math.sqrt(DS), None,
                                            ALU.mult).then_inc(s_bias, 1)

                def norm(n):
                    dve.wait_ge(s_exp, n + 1)
                    nc.vector.reciprocal(rrec[:, n, :], rsum[:, n, :]).then_inc(s_rec, 1)
                    dve.wait_ge(s_rec, n + 1)
                    for t in range(QT):
                        i = nc.vector.tensor_scalar(pr[:, n % 2, t, 0:(t + 1) * P], pr[:, n % 2, t, 0:(t + 1) * P],
                                                    rrec[:, n, t:t + 1], None, ALU.mult)
                    i.then_inc(s_norm, 1)

                soft(0)
                for n in range(HS):
                    norm(n)
                    if n + 1 < HS:
                        soft(n + 1)
                for t in range(QT):
                    dve.wait_ge(z_ready, t + 1)
                    nc.vector.tensor_tensor(x[:, t, :], x[:, t, :], bank[t][:], ALU.add).then_inc(x2_ready, 1)
                dve.wait_ge(x2_ready, QT)


def experts(nc, a, keep, out, x):
    with ExitStack() as ctx:
        sb = lambda name, shape, dt=F32: ctx.enter_context(nc.sbuf_tensor(name, shape, dt))
        sem = lambda name: ctx.enter_context(nc.semaphore(name))
        HT = H // P
        ident = keep.ident
        xn = sb("xn_e", [P, QT, D])
        xT = sb("xT_e", [P, DT, T])
        w_in, w_out = sb("w_in", [P, 2, DT, H]), sb("w_out", [P, 2, HT, D])
        hT = sb("hT", [P, 2, HT, T])
        b_in = sb("b_in", [P, E * HT])
        b_out = sb("b_out", [E, D])
        router = sb("router", [P, DT, E])
        logits, probs = sb("logits", [P, QT, E]), sb("probs", [P, QT, E])
        top, left, gate = sb("top", [P, QT, 8]), sb("left", [P, QT, E]), sb("gate", [P, QT, E])
        lmax, lneg, lsum, lrec = (sb(n, [P, QT]) for n in ("lmax", "lneg", "lsum", "lrec"))
        gateT = sb("gateT", [E, T])
        stats, mv = sb("stats_e", [P, QT, 6]), sb("mv_e", [P, QT, 2])
        rs = sb("rs_e", [P, 7, QT])
        up = [ctx.enter_context(nc.psum_tensor(f"up{i}", [P, 512], F32)) for i in range(4)]
        down = [ctx.enter_context(nc.psum_tensor(f"down{i}", [P, 512], F32)) for i in range(4)]
        small_loaded = sem("small_loaded")
        in_loaded = [sem("in_loaded0"), sem("in_loaded1")]
        out_loaded = [sem("out_loaded0"), sem("out_loaded1")]
        ln_step, root = sem("ln_step2"), sem("root2")
        turned, turned_out = sem("turned2"), sem("turned2_out")
        lg_ready, lg_out, lg_step, lg_exp = sem("lg_ready"), sem("lg_out"), sem("lg_step"), sem("lg_exp")
        gates_ready, gates_turned, gates_out = sem("gates_ready"), sem("gates_turned"), sem("gates_out")
        up_ready, up_out, down_ready, down_out = sem("up_ready"), sem("up_out"), sem("down_ready"), sem("down_out")
        bias_ready, stored = sem("bias_ready"), sem("stored")

        with nc.Block() as block:

            @block.sync
            def _(sp):
                def load(e, b, wait):
                    if wait:
                        sp.wait_ge(up_ready, HT * (e - 1))
                    sp.dma_start(w_in[:, b], a["L0_ffn_w_in"][one_of(e)].rearrange("e (k p) n -> p (e k) n", p=P)
                                 ).then_inc(in_loaded[b], 16)
                    if wait:
                        sp.wait_ge(down_ready, QT * (e - 1))
                    sp.dma_start(w_out[:, b], a["L0_ffn_w_out"][one_of(e)].rearrange("e (k p) n -> p (e k) n", p=P)
                                 ).then_inc(out_loaded[b], 16)

                for t, s in ((router, a["L0_ffn_router_w"].rearrange("(k p) n -> p k n", p=P)),
                             (b_in, a["b_in_columns"]), (b_out, a["L0_ffn_b_out"])):
                    sp.dma_start(t[:], s).then_inc(small_loaded, 16)
                load(0, 0, False)
                load(1, 1, False)
                with sp.Fori(1, E // 2) as e2:
                    load(e2 * 2, 0, True)
                    load(e2 * 2 + 1, 1, True)
                sp.wait_ge(down_out, QT * (E + 1))
                sp.dma_start(out[0].rearrange("(t p) d -> p t d", p=P), x[:]).then_inc(stored, 16)
                sp.wait_ge(stored, 16)

            @block.tensor
            def _(pe):
                pe.wait_ge(ln_step, LN_DONE)
                for d in range(DT):
                    for t in range(QT):
                        i = nc.tensor.transpose(up[d][:, t * P:(t + 1) * P], xn[:, t, d * P:(d + 1) * P], ident[:])
                    i.then_inc(turned, 1)
                pe.wait_ge(small_loaded, 48)
                pe.wait_ge(turned_out, DT)
                for t in range(QT):
                    for k in range(DT):
                        i = nc.tensor.matmul(down[0][:, t * E:(t + 1) * E], xT[:, k, t * P:(t + 1) * P], router[:, k, :],
                                             start=(k == 0), stop=(k == DT - 1))
                i.then_inc(lg_ready, 1)

                def up_one(e, b, first=False):
                    for m in range(HT):
                        if not first:
                            pe.wait_ge(up_out, HT * (e - 1) + m + 1)
                        for k in range(DT):
                            i = nc.tensor.matmul(up[m][:], w_in[:, b, k, m * P:(m + 1) * P], xT[:, k, :],
                                                 start=(k == 0), stop=(k == DT - 1))
                        i.then_inc(up_ready, 1)

                pe.wait_ge(in_loaded[0], 16)
                up_one(0, 0, first=True)
                pe.wait_ge(gates_ready, 1)
                for t in range(QT):
                    i = nc.tensor.transpose(down[0][0:E, t * P:(t + 1) * P], gate[:, t, :], ident[:])
                i.then_inc(gates_turned, 1)
                pe.wait_ge(gates_out, 1)
                for t in range(QT):
                    nc.tensor.matmul(down[t][:], gateT[:, t * P:(t + 1) * P], b_out[:], start=True,
                                     stop=True).then_inc(bias_ready, 1)

                def down_one(e, b):
                    pe.wait_ge(up_out, HT * (e + 1))
                    for t in range(QT):
                        pe.wait_ge(down_out, QT * e + t + 1)
                        for k in range(HT):
                            i = nc.tensor.matmul(down[t][:], hT[:, b, k, t * P:(t + 1) * P], w_out[:, b, k, :],
                                                 start=(k == 0), stop=(k == HT - 1))
                        i.then_inc(down_ready, 1)

                def two(e2, last):
                    e = e2 * 2
                    pe.wait_ge(in_loaded[1], 16 * e2 + 16)
                    up_one(e + 1, 1)
                    pe.wait_ge(out_loaded[0], 16 * e2 + 16)
                    down_one(e, 0)
                    if not last:
                        pe.wait_ge(in_loaded[0], 16 * e2 + 32)
                        up_one(e + 2, 0)
                    pe.wait_ge(out_loaded[1], 16 * e2 + 16)
                    down_one(e + 1, 1)

                with pe.Fori(0, E // 2 - 1) as e2:
                    two(e2, False)
                two(E // 2 - 1, True)

            @block.scalar
            def _(act):
                act.wait_ge(ln_step, LN_VAR)
                nc.scalar.activation(rs[:, 1, :], rs[:, 0, :], ACT.Sqrt).then_inc(root, 1)
                act.wait_ge(lg_step, 3)
                for t in range(QT):
                    i = nc.scalar.activation(probs[:, t, :], logits[:, t, :], ACT.Exp, bias=lneg[:, t:t + 1], scale=1.0,
                                             accum_out=lsum[:, t:t + 1])
                i.then_inc(lg_exp, 1)

                def gelu(e, b, first):
                    for m in range(HT):
                        act.wait_ge(up_ready, HT * e + m + 1)
                        if not first:
                            act.wait_ge(down_ready, QT * (e - 1))
                        nc.scalar.activation(hT[:, b, m, :], up[m][:], ACT.Gelu_apprx_tanh,
                                             bias=b_in[:, e * HT + m:e * HT + m + 1] if isinstance(e, int)
                                             else b_in[:, bass.ds(e * HT + m, 1)]).then_inc(up_out, 1)

                act.wait_ge(small_loaded, 48)
                gelu(0, 0, True)
                gelu(1, 1, True)
                with act.Fori(1, E // 2) as e2:
                    gelu(e2 * 2, 0, False)
                    gelu(e2 * 2 + 1, 1, False)

            @block.vector
            def _(dve):
                layer_norm_rows(nc, dve, x, xn, stats, mv, rs, ln_step, root)
                for d in range(DT):
                    dve.wait_ge(turned, d + 1)
                    nc.vector.tensor_copy(xT[:, d, :], up[d][:]).then_inc(turned_out, 1)
                dve.wait_ge(lg_ready, 1)
                nc.vector.tensor_copy(logits[:], down[0][:, 0:QT * E].rearrange("p (t e) -> p t e", e=E)
                                      ).then_inc(lg_step, 1)
                dve.wait_ge(lg_step, 1)
                nc.vector.tensor_reduce(lmax[:], logits[:], X_AXIS, ALU.max).then_inc(lg_step, 1)
                dve.wait_ge(lg_step, 2)
                nc.vector.tensor_scalar(lneg[:], lmax[:], -1.0, None, ALU.mult).then_inc(lg_step, 1)
                dve.wait_ge(lg_exp, 1)
                nc.vector.reciprocal(lrec[:], lsum[:]).then_inc(lg_step, 1)
                dve.wait_ge(lg_step, 4)
                for t in range(QT):
                    i = nc.vector.tensor_scalar(probs[:, t, :], probs[:, t, :], lrec[:, t:t + 1], None, ALU.mult)
                i.then_inc(lg_step, 1)
                dve.wait_ge(lg_step, 5)
                for t in range(QT):
                    i = nc.vector.max(top[:, t, :], probs[:, t, :])
                i.then_inc(lg_step, 1)
                dve.wait_ge(lg_step, 6)
                nc.vector.memset(top[:, :, 2:8], -1.0).then_inc(lg_step, 1)
                dve.wait_ge(lg_step, 7)
                for t in range(QT):
                    i = nc.vector.match_replace(left[:, t, :], top[:, t, :], probs[:, t, :], 0.0)
                i.then_inc(lg_step, 1)
                dve.wait_ge(lg_step, 8)
                nc.vector.tensor_tensor(gate[:], probs[:], left[:], ALU.subtract).then_inc(gates_ready, 1)
                dve.wait_ge(gates_turned, 1)
                nc.vector.tensor_copy(gateT[:], down[0][0:E, :]).then_inc(gates_out, 1)
                for t in range(QT):
                    dve.wait_ge(bias_ready, t + 1)
                    nc.vector.tensor_tensor(x[:, t, :], x[:, t, :], down[t][:], ALU.add).then_inc(down_out, 1)

                def add(e, column):
                    for t in range(QT):
                        dve.wait_ge(down_ready, QT * e + t + 1)
                        dve.wait_ge(down_out, QT * e + t + 1)
                        nc.vector.scalar_tensor_tensor(out=x[:, t, :], in0=down[t][:], scalar=gate[:, t, column],
                                                       in1=x[:, t, :], op0=ALU.mult, op1=ALU.add).then_inc(down_out, 1)

                with dve.Fori(0, E) as e:
                    add(e, bass.ds(e, 1))


class Kept:
    pass


def build(nc, a, out):
    dram, keep = Kept(), Kept()
    dram.q = nc.dram_tensor("q_by_pair", (PAIRS, P, T), F32).ap()
    dram.o = nc.dram_tensor("o_by_pair", (PAIRS, P, QT * P), F32).ap()
    with ExitStack() as ctx:
        keep.ident = ctx.enter_context(nc.sbuf_tensor("ident", [P, P], F32))
        keep.ident16 = ctx.enter_context(nc.sbuf_tensor("ident16", [P, P], F16))
        with nc.sbuf_tensor("ctx_halves", [P, 2, CT, NKEY], F16) as keep.ctx:
            prologue(nc, a, dram, keep)
            cross_attention(nc, a, dram, keep)
        with nc.sbuf_tensor("x", [P, QT, D], F32) as x:
            self_attention(nc, a, dram, keep, x)
            experts(nc, a, keep, out, x)


def kernel(**inputs):
    import concourse.bacc as bacc
    from concourse.bass_utils import run_bass_kernel_spmd

    arrays = {}
    for name in ("x", "L0_xattn_Wq", "L0_xattn_Wo", "L0_xattn_bo", "L0_ffn_router_w", "L0_ffn_w_in", "L0_ffn_w_out",
                 "L0_ffn_b_out"):
        arrays[name] = np.ascontiguousarray(inputs[name])
    arrays["ctxT"] = np.ascontiguousarray(np.asarray(inputs["ctx_768"])[0].T)
    for name in ("Wk", "Wv"):
        w = np.asarray(inputs[f"L0_xattn_{name}"]).reshape(CT, P, PAIRS, P)
        arrays[f"{name.lower()}_pairs"] = np.ascontiguousarray(w.transpose(2, 1, 0, 3)).reshape(PAIRS, P, CT * P)
    for name in ("Wq", "Wk", "Wv", "Wo"):
        arrays[f"attn_{name}T"] = np.ascontiguousarray(np.asarray(inputs[f"L0_attn_{name}"]).T)
    b_in = np.asarray(inputs["L0_ffn_b_in"]).reshape(E, H // P, P)
    arrays["b_in_columns"] = np.ascontiguousarray(b_in.transpose(2, 0, 1)).reshape(P, E * (H // P))
    arrays["rope_cos"], arrays["rope_sin"], arrays["rope_turn"] = rope_constants()
    arrays["causal"] = np.where(np.arange(P)[None, :] > np.arange(P)[:, None], np.finfo(np.float32).min,
                                np.float32(0.0)).astype(np.float32)

    nc = bacc.Bacc("TRN2", target_bir_lowering=False, num_devices=1)
    a = {n: nc.dram_tensor(f"in_{n}", v.shape, mybir.dt.from_np(v.dtype), kind="ExternalInput").ap()
         for n, v in arrays.items()}
    out = nc.dram_tensor("out_0", (1, T, D), F32, kind="ExternalOutput").ap()
    build(nc, a, out)
    r = run_bass_kernel_spmd(nc, [{f"in_{n}": v for n, v in arrays.items()}], core_ids=[0])
    return r.results[0]["out_0"]
```

```python
import math
from contextlib import ExitStack

import concourse.bass as bass
import numpy as np
from concourse import mybir

F32 = mybir.dt.float32
F16 = mybir.dt.float16
ALU = mybir.AluOpType
ACT = mybir.ActivationFunctionType
X_AXIS = mybir.AxisListType.X

P = 128
D = 512
T = 512
QT = T // P
DT = D // P
EPS = 1e-5

NKEY = 8192
CTX = 384
CT = CTX // P
HX = 16
DH = 64
PAIRS = HX // 2
CHUNK = 2048
NCHUNK = NKEY // CHUNK
KB = CHUNK // P
DUOS = KB // 2
STEPS = 2 * DUOS
KT = CHUNK // 512
VW = 2 * DH + 1

CTX_SCALE = 16.0
W_SCALE = 256.0
KV_SCALE = 16.0
Q_SCALE = 16.0
P_SCALE = 256.0
M_UNIT = 64.0
KV_EVAC = KV_SCALE / (CTX_SCALE * W_SCALE)
EXP_SCALE = 1.0 / (Q_SCALE * KV_SCALE * math.sqrt(DH))

HS = 16
DS = D // HS
P_COLS = P * QT * (QT + 1) // 2
MASKED = 60000.0

E = 8
H = 512
H_SCALE = 16.0

RING = 4
HEAD = 4

PSTEPS = NCHUNK * STEPS
KV_KEYS = 256
KV_JOBS = CHUNK // KV_KEYS
LAG = 2


def job_plan():
    steps = [[] for _ in range(STEPS)]
    k_at = [3 * (n // 2) + n % 2 for n in range(KV_JOBS)]
    v_at = [s for s in range(STEPS) if s not in k_at]
    for n in range(KV_JOBS):
        steps[k_at[n]].append((("K", n), False))
        steps[v_at[n]].append((("V", n), False))
    free = [s for s in range(2, STEPS + 2) for _ in range(2)]
    for h in range(2):
        for t in range(KT):
            for q in range(QT):
                s = next(s for s in free if s > k_at[2 * t + 1])
                free.remove(s)
                steps[s % STEPS].append((("M", h, q, t), s >= STEPS))
    steps[STEPS - 2].append((("R", 0), False))
    steps[4].append((("R", 1), True))
    for s in steps:
        s.sort(key=lambda j: j[0][0] not in "KV")
    return steps


PLAN = job_plan()
BANKS = 3
JOBS = sum(map(len, PLAN)) + 1
EARLY = [job for step in PLAN for job, late in step if not late]
LATE = sum(late for step in PLAN for _, late in step)
NUMBER = {job: n for n, (job, late) in enumerate(j for step in PLAN for j in step)}
FIRST_NUMBER = {job: LATE + n for n, job in enumerate(EARLY)}
LAST_NUMBER = {job: n for n, job in enumerate(j for step in PLAN for j, late in step if late)}
KV_ORDER = {job: n for n, job in enumerate(j for j in EARLY if j[0] in "KV")}
LAST_MAX = [("M", h, QT - 1, KT - 1) for h in range(2)]
WK_STEP = STEPS - 4
assert JOBS % BANKS == 0 and max(NUMBER, key=NUMBER.get) == EARLY[-1]
RING_S = 3
FIRST_BANKS = BANKS + RING_S
POOL_COLS = 512
def one_of(n):
    return slice(n, n + 1) if isinstance(n, int) else bass.ds(n, 1)


def layer_norm_rows(nc, dve, x, xn, stats, mv, rs, ln_step, root, ready=None):
    for t in range(QT):
        if ready is not None:
            dve.wait_ge(*ready(t))
        i = nc.vector.bn_stats(stats[:, t, :], x[:, t, :])
    i.then_inc(ln_step, 1)
    dve.wait_ge(ln_step, 1)
    for t in range(QT):
        i = nc.vector.bn_aggr(mv[:, t, :], stats[:, t, :])
    i.then_inc(ln_step, 1)
    dve.wait_ge(ln_step, 2)
    nc.vector.tensor_scalar(rs[:, 0, :], mv[:, :, 1], EPS, None, ALU.add).then_inc(ln_step, 1)
    dve.wait_ge(root, 1)
    nc.vector.reciprocal(rs[:, 2, :], rs[:, 1, :]).then_inc(ln_step, 1)
    dve.wait_ge(ln_step, 4)
    nc.vector.tensor_tensor(rs[:, 3, :], rs[:, 2, :], rs[:, 2, :], ALU.mult).then_inc(ln_step, 1)
    dve.wait_ge(ln_step, 5)
    nc.vector.tensor_tensor(rs[:, 4, :], rs[:, 3, :], rs[:, 0, :], ALU.mult).then_inc(ln_step, 1)
    dve.wait_ge(ln_step, 6)
    nc.vector.tensor_scalar(rs[:, 5, :], rs[:, 4, :], -0.5, 1.5, ALU.mult, ALU.add).then_inc(ln_step, 1)
    dve.wait_ge(ln_step, 7)
    nc.vector.tensor_tensor(rs[:, 6, :], rs[:, 5, :], rs[:, 2, :], ALU.mult).then_inc(ln_step, 1)
    dve.wait_ge(ln_step, 8)
    for t in range(QT):
        i = nc.vector.tensor_scalar(xn[:, t, :], x[:, t, :], mv[:, t, 0:1], rs[:, 6, t:t + 1],
                                    ALU.subtract, ALU.mult)
    i.then_inc(ln_step, 1)


LN_VAR = 3
LN_DONE = 9


def prologue(nc, a, dram, keep):
    with ExitStack() as ctx:
        sb = lambda name, shape, dt=F32: ctx.enter_context(nc.sbuf_tensor(name, shape, dt))
        sem = lambda name: ctx.enter_context(nc.semaphore(name))
        PIECE = 512
        NPIECE = NKEY // PIECE
        RAWS = 4
        raw = sb("ctx_raw", [P, RAWS, CT, PIECE])
        x = sb("x_in", [P, QT, D])
        xn = sb("xn", [P, QT, D])
        xnT = sb("xnT", [P, DT, T])
        wq = sb("wq", [P, DT, HX * DH])
        qout = sb("qout", [P, 2, T])
        stats = sb("stats", [P, QT, 6])
        mv = sb("mv", [P, QT, 2])
        rs = sb("rs", [P, 7, QT])
        ps = [ctx.enter_context(nc.psum_tensor(f"pp{i}", [P, 512], F32)) for i in range(4)]
        x_loaded, wq_loaded = sem("x_loaded"), sem("wq_loaded")
        q_stored = [sem("q_stored0"), sem("q_stored1")]
        raw_loaded = [sem(f"raw_loaded{i}") for i in range(RAWS)]
        ctx_hi, ctx_lo = sem("ctx_hi"), sem("ctx_lo")
        ln_step, root = sem("ln_step"), sem("root")
        turned, turned_out = sem("turned"), sem("turned_out")
        q_ready, q_out = sem("q_ready"), sem("q_out")
        ident_set = sem("ident_set")
        with nc.Block() as block:

            @block.sync
            def _(sp):
                sp.dma_start(x[:], a["x"][0].rearrange("(t p) d -> p t d", p=P)).then_inc(x_loaded, 16)
                sp.dma_start(wq[:], a["L0_xattn_Wq"].rearrange("(k p) n -> p k n", p=P)).then_inc(wq_loaded, 16)
                for n in range(NPIECE):
                    if n >= RAWS:
                        sp.wait_ge(ctx_lo, n - RAWS + 1)
                    sp.dma_start(raw[:, n % RAWS], a["ctxT"].rearrange("(k p) n -> p k n", p=P)[
                        :, :, n * PIECE:(n + 1) * PIECE]).then_inc(raw_loaded[n % RAWS], 16)

            @block.gpsimd
            def _(pool):
                nc.gpsimd.memset(keep.ident[:], 0.0).then_inc(ident_set, 1)
                nc.gpsimd.memset(keep.ident16[:], 0.0).then_inc(ident_set, 1)
                pool.wait_ge(ident_set, 2)
                for m in (keep.ident, keep.ident16):
                    nc.gpsimd.affine_select(out=m[:], in_=m[:], compare_op=ALU.not_equal, fill=1.0, base=0,
                                            pattern=[[-1, P]], channel_multiplier=1).then_inc(ident_set, 1)

            @block.scalar
            def _(act):
                act.wait_ge(ln_step, LN_VAR)
                nc.scalar.activation(rs[:, 1, :], rs[:, 0, :], ACT.Sqrt).then_inc(root, 1)

                def q_leaves(n):
                    act.wait_ge(q_ready, n + 1)
                    if n >= 2:
                        act.wait_ge(q_stored[n % 2], 16 * (n // 2))
                    nc.scalar.activation(qout[:, n % 2, :], ps[n % 4][:], ACT.Copy).then_inc(q_out, 1)
                    act.wait_ge(q_out, n + 1)
                    act.dma_start(dram.q[n], qout[:, n % 2, :]).then_inc(q_stored[n % 2], 16)

                for n in range(NPIECE):
                    act.wait_ge(raw_loaded[n % RAWS], 16 * (n // RAWS + 1))
                    nc.scalar.activation(keep.ctx[:, 0, :, n * PIECE:(n + 1) * PIECE], raw[:, n % RAWS], ACT.Copy,
                                         scale=CTX_SCALE).then_inc(ctx_hi, 1)
                    if n >= NPIECE - PAIRS:
                        q_leaves(n - NPIECE + PAIRS)
                for s in q_stored:
                    act.wait_ge(s, 16 * PAIRS // 2)

            @block.vector
            def _(dve):
                dve.wait_ge(x_loaded, 16)
                layer_norm_rows(nc, dve, x, xn, stats, mv, rs, ln_step, root)
                for t in range(DT):
                    dve.wait_ge(turned, t + 1)
                    nc.vector.tensor_copy(xnT[:, t, :], ps[t][:]).then_inc(turned_out, 1)
                for n in range(NPIECE):
                    dve.wait_ge(ctx_hi, n + 1)
                    nc.vector.scalar_tensor_tensor(
                        out=keep.ctx[:, 1, :, n * PIECE:(n + 1) * PIECE], in0=raw[:, n % RAWS], scalar=CTX_SCALE,
                        in1=keep.ctx[:, 0, :, n * PIECE:(n + 1) * PIECE], op0=ALU.mult,
                        op1=ALU.subtract).then_inc(ctx_lo, 1)

            @block.tensor
            def _(pe):
                pe.wait_ge(ident_set, 4)
                pe.wait_ge(ln_step, LN_DONE)
                for d in range(DT):
                    for t in range(QT):
                        i = nc.tensor.transpose(ps[d][:, t * P:(t + 1) * P], xn[:, t, d * P:(d + 1) * P],
                                                keep.ident[:])
                    i.then_inc(turned, 1)
                pe.wait_ge(wq_loaded, 16)
                pe.wait_ge(turned_out, DT)
                for n in range(PAIRS):
                    if n >= 4:
                        pe.wait_ge(q_out, n - 3)
                    for k in range(DT):
                        i = nc.tensor.matmul(ps[n % 4][:], wq[:, k, n * P:(n + 1) * P], xnT[:, k, :],
                                             start=(k == 0), stop=(k == DT - 1))
                    i.then_inc(q_ready, 1)


def cross_attention(nc, a, dram, keep):
    with ExitStack() as ctx:
        sb = lambda name, shape, dt=F32: ctx.enter_context(nc.sbuf_tensor(name, shape, dt))
        sem = lambda name: ctx.enter_context(nc.semaphore(name))
        C = keep.ctx
        SA = sb("sa", [P, 2, 2, CHUNK], F16)
        SB = sb("sb", [P, 2, 2, CHUNK], F16)
        VT = sb("vt", [P, 2, KB, 2, VW], F16)
        QA = sb("qa", [P, 2, 2, T], F16)
        MB = sb("mb", [P, 2, 2, T], F16)
        w_raw = sb("w_raw", [P, 2, CT, P])
        w_hl = sb("w_hl", [P, 2, 2, CT, P], F16)
        q_raw = sb("q_raw", [P, T])
        p32 = sb("p32", [P, 2, 1024])
        ph = sb("ph", [P, RING, 1024], F16)
        pl = sb("pl", [P, RING, 1024], F16)
        acc = sb("acc", [P, 2, 2, 2, DH + 1])
        out = sb("out", [P, QT, 2, DH])
        rec = sb("rec", [P, 2, 2, 2])
        cmx = sb("cmx", [P, 2, QT, KT])
        cm = sb("cm", [P, 2, QT])
        m16 = sb("m16", [P, 2, 2, QT], F16)
        md = sb("md", [P, 2, QT])
        corr = sb("corr", [P, 2, 2, QT])
        ln_p = sb("ln_p", [P, 1])
        ones = sb("ones", [P, 1], F16)
        scored = [ctx.enter_context(nc.psum_tensor(f"scores{i}", [P, 512], F32)) for i in range(RING_S)]
        work = [ctx.enter_context(nc.psum_tensor(f"work{i}", [P, 512], F32)) for i in range(BANKS)]
        job_bank = work + scored
        O = ctx.enter_context(nc.psum_tensor("pv", [P, 2, 512], F32))
        O_view = O[:, :, 0:2 * VW].rearrange("p b (t n) -> p b t n", n=VW)

        scores_ready, exp_done, ph_ready = sem("scores_ready"), sem("exp_done"), sem("ph_ready")
        pl_ready, av_done, o_free = sem("pl_ready"), sem("av_done"), sem("o_free")
        pl_pool, copied = sem("pl_pool"), sem("copied")
        job_filled, job_free, out_stored = sem("job_filled"), sem("job_free"), sem("out_stored")
        hi_ready, corr_ready = sem("hi_ready"), sem("corr_ready")
        cm_ready, m_ready, md_ready = sem("cm_ready"), sem("m_ready"), sem("md_ready")
        w_loaded, w_hi, w_split = sem("w_loaded"), [sem("wk_hi"), sem("wv_hi")], [sem("wk_split"), sem("wv_split")]
        q_loaded, q_hi, q_set = sem("q_loaded"), sem("q_hi"), sem("q_set")
        o_part, out_rec, out_norm = sem("o_part"), sem("out_rec"), sem("out_norm")
        consts_set = sem("consts_set")

        Q_BEFORE = EARLY[2]

        def after(n):
            return n + 1 + HEAD

        def count_of(job):
            return 2 if job == EARLY[-1] else 1

        def score_bank(i):
            k = i % (2 * PSTEPS)
            return scored[k % RING_S], RING_S if k >= 2 * PSTEPS % RING_S else 2 * PSTEPS % RING_S

        def early(item, job):
            return item * JOBS + NUMBER[job]

        def where(p, s, last):
            c, d = divmod(s % PSTEPS, STEPS)
            pair = p + s // PSTEPS
            return pair, c, d, pair * NCHUNK + c, None if last and c == NCHUNK - 1 else (c + 1) % NCHUNK

        def corr_count(pair, c, h):
            return (pair * (NCHUNK - 1) + c - 1) * 2 + h + 1

        def jobs_of(p, s, last):
            pair, c, d, item, nxt = where(p, s, last)
            number = NUMBER if nxt is not None else LAST_NUMBER
            for job, late in PLAN[d]:
                if late or nxt is not None:
                    n = number[job]
                    of = (pair, item, c) if late else (pair + 1 if nxt == 0 else pair, item + 1, nxt)
                    yield ((item + 1) * JOBS + n, n % BANKS, job) + of

        def run_pairs(eng, step, finish):
            for s in range(LAG):
                step(0, s, False)
            with eng.Fori(0, PAIRS - 1) as p:
                for s in range(LAG, PSTEPS + LAG):
                    step(p, s, False)
            for s in range(LAG, PSTEPS):
                step(PAIRS - 1, s, True)
            finish()

        with nc.Block() as block:

            @block.sync
            def _(sp):
                def load_w(p):
                    for n, w in enumerate(("wk_pairs", "wv_pairs")):
                        sp.dma_start(w_raw[:, n].rearrange("p k n -> p (k n)"),
                                     a[w][one_of(p)].rearrange("a p n -> (a p) n")).then_inc(w_loaded, 16)

                def load_q(p):
                    sp.dma_start(q_raw[:], dram.q[one_of(p)].rearrange("a p n -> (a p) n")).then_inc(q_loaded, 16)

                def load_next_stage():
                    sp.wait_ge(job_filled, after(PAIRS * NCHUNK * JOBS - 1))
                    k, into = keep, keep.loaded
                    sp.dma_start(k.wo_x, a["L0_xattn_Wo"].rearrange("(k p) n -> p k n", p=P)).then_inc(into["wo_x"], 16)
                    sp.dma_start(k.x, a["x"][0].rearrange("(t p) d -> p t d", p=P)).then_inc(into["x"], 16)
                    sp.dma_start(k.bo, a["L0_xattn_bo"].rearrange("(o n) -> o n", o=1).broadcast_to([P, D])
                                 ).then_inc(into["bo"], 16)
                    for n, w in (("Wq", k.w_q), ("Wk", k.w_k), ("Wv", k.w_v), ("Wo", k.w_o)):
                        sp.dma_start(w, a[f"attn_{n}T"].rearrange("(k p) n -> p k n", p=P)).then_inc(into[n], 16)
                    for t, n in ((k.cos, "rope_cos"), (k.sin, "rope_sin"), (k.turn, "rope_turn")):
                        sp.dma_start(t, a[n]).then_inc(into["rope"], 16)
                    sp.wait_ge(out_stored, 16 * (PAIRS - 1) + HEAD)
                    for n in range(PAIRS - 1):
                        load_o(n)

                def load_o(n):
                    sp.dma_start(keep.o_all[:, n].rearrange("p t n -> p (t n)"), dram.o[n]).then_inc(keep.o_loaded[n], 16)

                def pair(p, last):
                    if not last:
                        for s in w_split:
                            sp.wait_ge(s, p + 1)
                        load_w(p + 1)
                        sp.wait_ge(q_set, 2 * p + 2)
                        load_q(p + 1)
                    if last:
                        load_next_stage()
                    sp.wait_ge(out_norm, after(p))
                    sp.dma_start(dram.o[one_of(p)].rearrange("a p n -> (a p) n"),
                                 out[:].rearrange("p t h d -> p (t h d)")).then_inc(out_stored, 16)

                sp.sem_inc(out_stored, HEAD)
                load_w(0)
                load_q(0)
                with sp.Fori(0, PAIRS - 1) as p:
                    pair(p, False)
                pair(PAIRS - 1, True)
                sp.wait_ge(out_stored, 16 * PAIRS + HEAD)
                load_o(PAIRS - 1)

            @block.gpsimd
            def _(pool):
                nc.gpsimd.memset(ln_p[:], math.log(P_SCALE)).then_inc(consts_set, 1)
                nc.gpsimd.memset(ones[:], 1.0).then_inc(consts_set, 1)
                nc.gpsimd.memset(VT[:, :, :, :, DH:DH + 1], KV_SCALE).then_inc(consts_set, 1)
                pool.wait_ge(consts_set, 3)
                nc.gpsimd.memset(SB[DH:DH + 1], M_UNIT).then_inc(consts_set, 1)

                def low(item, c, d):
                    g = item * STEPS + d
                    cols = slice(2 * T - POOL_COLS, 2 * T)
                    pool.wait_ge(ph_ready, after(g))
                    pool.wait_ge(pl_pool, after(g - 1))
                    pool.wait_ge(copied, copies(item, c, d))
                    nc.gpsimd.tensor_tensor(pl[:, d % RING, cols], p32[:, d % 2, cols], ph[:, d % RING, cols],
                                            ALU.subtract).then_inc(pl_pool, 1)

                def copies(item, c, d):
                    k_jobs = sum(job[0] == "K" for step in PLAN[:d + 1] for job, _ in step)
                    ahead = 0 if c is None else k_jobs
                    return 2 * (KV_JOBS * (item + 1) + ahead)

                def copy(n, bank, job, pair, item, c, low_done=None):
                    if job[0] == "K":
                        if low_done is not None:
                            pool.wait_ge(pl_pool, after(low_done))
                        par, keys = c % 2, slice(job[1] * KV_KEYS, (job[1] + 1) * KV_KEYS)
                        for h in range(2):
                            pool.wait_ge(hi_ready, (item * len(KV_ORDER) + KV_ORDER[job]) * 2 + h + 1)
                            rows = slice(h * DH, (h + 1) * DH)
                            before = (item * KV_JOBS + job[1]) * 2 + h
                            if job[1] + h > 0 or low_done is not None:
                                pool.wait_ge(copied, before)
                            nc.gpsimd.tensor_tensor(SB[0:DH, par, h, keys], SA[rows, par, h, keys],
                                                    ones[rows, :].to_broadcast([DH, KV_KEYS]),
                                                    ALU.mult).then_inc(copied, 1)

                def step(p, s, last):
                    _, _, d, item, nxt = where(p, s, last)
                    if s >= 1:
                        _, _, d1, item1, nxt1 = where(p, s - 1, last)
                        low(item1, nxt1, d1)
                    for j in jobs_of(p, s, last):
                        copy(*j, low_done=item * STEPS + d - 1)
                    if s == PSTEPS + LAG - 1:
                        normalise(p, copies(item, nxt, d))

                def normalise(pair, copies_before):
                    pool.wait_ge(copied, copies_before)
                    pool.wait_ge(out_rec, pair + 1)
                    pool.wait_ge(out_stored, 16 * pair + HEAD)
                    for h in range(2):
                        i = nc.gpsimd.tensor_tensor(
                            out[:, :, h, :], acc[:, h, :, :, 0:DH].rearrange("p b t d -> p (b t) d"),
                            rec[:, h].rearrange("p b t -> p (b t)").unsqueeze(2).to_broadcast([P, QT, DH]), ALU.mult)
                    i.then_inc(out_norm, 1)

                def finish():
                    low(PAIRS * NCHUNK - 1, None, STEPS - 1)
                    normalise(PAIRS - 1, 2 * KV_JOBS * PAIRS * NCHUNK)

                pool.sem_inc(pl_pool, HEAD)
                pool.sem_inc(out_norm, HEAD)
                for job in EARLY:
                    copy(0, 0, job, 0, 0, 0)
                run_pairs(pool, step, finish)

            @block.tensor
            def _(pe):
                def fill(n, bank, job, item, c, k_done, banks=BANKS):
                    W, par = job_bank[bank], c % 2
                    pe.wait_ge(job_free, after(n - banks))
                    if job[0] == "K":
                        keys = slice(c * CHUNK + job[1] * KV_KEYS, c * CHUNK + (job[1] + 1) * KV_KEYS)
                        for k in range(CT):
                            for w, x in [(0, 0), (0, 1), (1, 0)]:
                                i = nc.tensor.matmul(W[:, 0:KV_KEYS], w_hl[:, 0, w, k, :], C[:, x, k, keys],
                                                     start=(k == 0 and (w, x) == (0, 0)),
                                                     stop=(k == CT - 1 and (w, x) == (1, 0)))
                    elif job[0] == "V":
                        for b in range(KV_KEYS // P):
                            k0 = c * CHUNK + job[1] * KV_KEYS + b * P
                            for k in range(CT):
                                for x, w in [(0, 0), (0, 1), (1, 0)]:
                                    i = nc.tensor.matmul(W[:, b * P:(b + 1) * P], C[:, x, k, k0:k0 + P],
                                                         w_hl[:, 1, w, k, :],
                                                         start=(k == 0 and (x, w) == (0, 0)),
                                                         stop=(k == CT - 1 and (x, w) == (1, 0)))
                    elif job[0] == "M":
                        _, h, q, kt = job
                        if h == 0:
                            pe.wait_ge(job_free, after(k_done(("K", 2 * kt + 1))))
                        i = nc.tensor.matmul(W[:], QA[:, par, h, q * P:(q + 1) * P],
                                             SA[:, par, h, kt * 512:(kt + 1) * 512], start=True, stop=True)
                    else:
                        h = job[1]
                        pe.wait_ge(m_ready, 2 * item + h + 1)
                        for q in range(QT):
                            i = nc.tensor.matmul(W[0:1, q * P:(q + 1) * P], m16[:, par, h, q:q + 1],
                                                 keep.ident16[:], start=True, stop=True)
                    i.then_inc(job_filled, count_of(job))

                def scores(item, c, d, b, nxt):
                    n = 2 * (item * STEPS + d) + b
                    bank, ago = score_bank(2 * (c * STEPS + d) + b)
                    h, par = d // DUOS, c % 2
                    if b == 0:
                        if d == 0:
                            pe.wait_ge(job_free, after(early(item, ("R", 0))))
                            pe.wait_ge(copied, (item + 1) * 2 * KV_JOBS)
                        if d == DUOS:
                            late = NUMBER if nxt is not None else LAST_NUMBER
                            pe.wait_ge(job_free, after((item + 1) * JOBS + late[("R", 1)]))
                    pe.wait_ge(exp_done, after(n - ago))
                    kb = (d % DUOS) * 2 + b
                    nc.tensor.matmul(bank[:], SA[:, par, h, kb * P:(kb + 1) * P],
                                     QA[:, par, h, :], start=True, stop=False)
                    i = nc.tensor.matmul(bank[:], SB[0:DH + 1, par, h, kb * P:(kb + 1) * P],
                                         MB[0:DH + 1, par, h, :], start=False, stop=True)
                    i.then_inc(scores_ready, 1)

                def weigh(item, c, d, b):
                    g = item * STEPS + d
                    h, par, at = d // DUOS, c % 2, d % RING
                    if b == 0:
                        if d == 0:
                            pe.wait_ge(job_free, after(early(item, EARLY[-1]) + 1))
                        if d % DUOS == 0:
                            pe.wait_ge(o_free, after(2 * item + h - 1))
                        pe.wait_ge(pl_ready, after(g))
                    if b == 1:
                        pe.wait_ge(pl_pool, after(g))
                    kb = (d % DUOS) * 2 + b
                    for q in range(QT):
                        o = (q % 2) * VW
                        cols = slice(b * T + q * P, b * T + (q + 1) * P)
                        nc.tensor.matmul(O[:, q // 2, o:o + VW], ph[:, at, cols], VT[:, par, kb, h, :],
                                         start=(kb == 0 and q % 2 == 0), stop=False, skip_group_check=True)
                        i = nc.tensor.matmul(O[:, q // 2, o:o + DH + 1], pl[:, at, cols],
                                             VT[:, par, kb, h, 0:DH + 1], start=False,
                                             stop=(kb == KB - 1), skip_group_check=True)
                    if b == 1:
                        i.then_inc(av_done, 1)

                def step(p, s, last):
                    pair, c, d, item, nxt = where(p, s, last)
                    jobs = [(n, bank, job, it, ch, lambda k: (item + 1) * JOBS + NUMBER[k])
                            for n, bank, job, _, it, ch in jobs_of(p, s, last)]
                    if nxt == 0:
                        if d < 3 and d % 2 == 0:
                            pe.wait_ge(w_split[d // 2], pair + 2)
                    if nxt is not None and nxt < 2 and d == 2:
                        pe.wait_ge(q_set, 2 * pair + (3 if nxt == 0 else 2))
                    scores(item, c, d, 0, nxt)
                    for j in jobs[0:1]:
                        fill(*j)
                    scores(item, c, d, 1, nxt)
                    for j in jobs[1:2]:
                        fill(*j)
                    lagging = None
                    if s >= LAG:
                        _, c2, d2, item2, _ = where(p, s - LAG, last)
                        weigh(item2, c2, d2, 0)
                    for j in jobs[2:3]:
                        fill(*j)
                    if s >= LAG:
                        weigh(item2, c2, d2, 1)
                    for j in jobs[3:]:
                        fill(*j)

                def finish():
                    for d in range(STEPS - LAG, STEPS):
                        for b in range(2):
                            weigh(PAIRS * NCHUNK - 1, NCHUNK - 1, d, b)

                for s, n in ((scores_ready, 0), (av_done, 0), (job_filled, LATE)):
                    pe.sem_inc(s, HEAD + n)
                pe.wait_ge(consts_set, 4)
                for s in w_split:
                    pe.wait_ge(s, 1)
                for job in EARLY:
                    if job == ("M", 0, 0, 0):
                        pe.wait_ge(q_set, 1)
                    n = FIRST_NUMBER[job]
                    fill(n, n % FIRST_BANKS, job, 0, 0, FIRST_NUMBER.__getitem__, FIRST_BANKS)
                pe.wait_ge(job_free, after(JOBS - 1 - BANKS))
                run_pairs(pe, step, finish)

            @block.scalar
            def _(act):
                def w_high(n, p, job_number=None):
                    act.wait_ge(w_loaded, 32 * p + 32)
                    if job_number is not None:
                        act.wait_ge(job_filled, after(job_number))
                    nc.scalar.activation(w_hl[:, n, 0], w_raw[:, n], ACT.Copy, scale=W_SCALE).then_inc(w_hi[n], 1)

                def q_high(p, par):
                    act.wait_ge(q_loaded, 16 * p + 16)
                    for h in range(2):
                        for rows in (slice(0, DH), slice(DH, P)):
                            i = nc.scalar.activation(QA[rows, par, h, :], q_raw[h * DH:(h + 1) * DH, :], ACT.Copy,
                                                     scale=Q_SCALE)
                    i.then_inc(q_hi, 1)

                def drain(n, bank, job, pair, item, c):
                    W, par = job_bank[bank], c % 2
                    if job[0] == "K":
                        keys = slice(job[1] * KV_KEYS, (job[1] + 1) * KV_KEYS)
                        act.wait_ge(job_filled, after(n))
                        for h in range(2):
                            rows = slice(h * DH, (h + 1) * DH)
                            nc.scalar.activation(SA[rows, par, h, keys], W[rows, 0:KV_KEYS], ACT.Copy,
                                                 scale=KV_EVAC).then_inc(hi_ready, 1)
                    elif job[0] == "V":
                        act.wait_ge(job_filled, after(n))
                        v = VT[:, par, job[1] * 2:(job[1] + 1) * 2].rearrange("p k h n -> p (k h) n")
                        nc.scalar.activation(v[:, :, 0:DH], W[:, 0:KV_KEYS].rearrange("p (k n) -> p k n", n=DH),
                                             ACT.Copy, scale=KV_EVAC).then_inc(hi_ready, 2)
                    elif job[0] == "R" and c > 0:
                        h = job[1]
                        act.wait_ge(md_ready, corr_count(pair, c, h))
                        nc.scalar.activation(corr[:, par, h, :], md[:, h, :], ACT.Exp,
                                             scale=M_UNIT * EXP_SCALE).then_inc(corr_ready, 1)

                def exp(item, c, d, b):
                    g = item * STEPS + d
                    bank, _ = score_bank(2 * (c * STEPS + d) + b)
                    act.wait_ge(scores_ready, after(2 * g + b))
                    if b == 0:
                        act.wait_ge(pl_ready, after(g - 2))
                        act.wait_ge(pl_pool, after(g - 2))
                    nc.scalar.activation(p32[:, d % 2, b * T:(b + 1) * T], bank[:], ACT.Exp,
                                         bias=ln_p[:], scale=EXP_SCALE).then_inc(exp_done, 1)

                def step(p, s, last):
                    pair, c, d, item, nxt = where(p, s, last)
                    g = item * STEPS + d
                    jobs = list(jobs_of(p, s, last))
                    exp(item, c, d, 0)
                    for j in jobs[:1]:
                        drain(*j)
                    exp(item, c, d, 1)
                    if nxt is not None and nxt < 2 and d == 0:
                        act.wait_ge(scores_ready, after(2 * item * STEPS - 1))
                        q_high(pair + 1 if nxt == 0 else pair, nxt)
                    if nxt == 0 and d == 0:
                        w_high(1, pair + 1, early(item, ("V", KV_JOBS - 1)))
                    for j in jobs[1:]:
                        drain(*j)
                    if nxt == NCHUNK - 1 and d == WK_STEP and not last:
                        w_high(0, pair + 1, early(item + 1, ("K", KV_JOBS - 1)))
                    act.wait_ge(av_done, after(g - RING))
                    act.wait_ge(exp_done, after(2 * g + 1))
                    nc.scalar.activation(ph[:, d % RING, :], p32[:, d % 2, :], ACT.Copy).then_inc(ph_ready, 1)

                for s in (exp_done, ph_ready):
                    act.sem_inc(s, HEAD)
                act.wait_ge(consts_set, 4)
                w_high(0, 0)
                w_high(1, 0)
                for job in EARLY:
                    if job == Q_BEFORE:
                        q_high(0, 0)
                    n = FIRST_NUMBER[job]
                    drain(n, n % FIRST_BANKS, job, 0, 0, 0)
                run_pairs(act, step, lambda: None)

            @block.vector
            def _(dve):
                def w_low(n, p):
                    dve.wait_ge(w_hi[n], p + 1)
                    nc.vector.scalar_tensor_tensor(out=w_hl[:, n, 1], in0=w_raw[:, n], scalar=W_SCALE,
                                                   in1=w_hl[:, n, 0], op0=ALU.mult,
                                                   op1=ALU.subtract).then_inc(w_split[n], 1)

                def q_low(n, par):
                    dve.wait_ge(q_hi, n)
                    for h in range(2):
                        rows = slice(h * DH, (h + 1) * DH)
                        i = nc.vector.scalar_tensor_tensor(out=MB[0:DH, par, h, :], in0=q_raw[rows, :], scalar=Q_SCALE,
                                                           in1=QA[rows, par, h, :], op0=ALU.mult, op1=ALU.subtract)
                    i.then_inc(q_set, 1)

                def new_maximum(n, pair, item, c, h):
                    par = c % 2
                    dve.wait_ge(job_free, after(n))
                    nc.vector.tensor_reduce(cm[:, h, :], cmx[:, h], X_AXIS, ALU.max).then_inc(cm_ready, 1)
                    dve.wait_ge(cm_ready, 2 * item + h + 1)
                    if c == 0:
                        nc.vector.tensor_scalar(m16[:, par, h, :], cm[:, h, :], 1.0 / M_UNIT, None,
                                                ALU.mult).then_inc(m_ready, 1)
                        return
                    nc.vector.scalar_tensor_tensor(out=m16[:, par, h, :], in0=cm[:, h, :], scalar=1.0 / M_UNIT,
                                                   in1=m16[:, 1 - par, h, :], op0=ALU.mult,
                                                   op1=ALU.max).then_inc(m_ready, 1)
                    dve.wait_ge(m_ready, 2 * item + h + 1)
                    nc.vector.tensor_tensor(md[:, h, :], m16[:, 1 - par, h, :], m16[:, par, h, :],
                                            ALU.subtract).then_inc(md_ready, 1)

                def drain(n, bank, job, pair, item, c):
                    W, par = job_bank[bank], c % 2
                    if job[0] in "KV":
                        hi_count = (item * len(KV_ORDER) + KV_ORDER[job]) * 2
                    if job[0] == "K":
                        keys = slice(job[1] * KV_KEYS, (job[1] + 1) * KV_KEYS)
                        for h in range(2):
                            hi, lo = (slice(0, DH), slice(DH, P)) if h == 0 else (slice(DH, P), slice(0, DH))
                            dve.wait_ge(hi_ready, hi_count + h + 1)
                            i = nc.vector.scalar_tensor_tensor(
                                out=SA[lo, par, h, keys], in0=W[hi, 0:KV_KEYS], scalar=KV_EVAC,
                                in1=SA[hi, par, h, keys], op0=ALU.mult, op1=ALU.subtract)
                        i.then_inc(job_free, 1)
                    elif job[0] == "V":
                        dve.wait_ge(hi_ready, hi_count + 2)
                        v = VT[:, par, job[1] * 2:(job[1] + 1) * 2].rearrange("p k h n -> p (k h) n")
                        nc.vector.scalar_tensor_tensor(
                            out=v[:, :, DH + 1:VW], in0=W[:, 0:KV_KEYS].rearrange("p (k n) -> p k n", n=DH),
                            scalar=KV_EVAC, in1=v[:, :, 0:DH], op0=ALU.mult,
                            op1=ALU.subtract).then_inc(job_free, count_of(job))
                    elif job[0] == "M":
                        _, h, q, kt = job
                        dve.wait_ge(job_filled, after(n))
                        nc.vector.tensor_reduce(cmx[:, h, q, kt:kt + 1], W[:], X_AXIS,
                                                ALU.max).then_inc(job_free, count_of(job))
                        if job == LAST_MAX[h]:
                            new_maximum(n, pair, item, c, h)
                    else:
                        h = job[1]
                        dve.wait_ge(job_filled, after(n))
                        nc.vector.tensor_scalar(MB[DH:DH + 1, par, h, :], W[0:1, :], -1.0, None,
                                                ALU.mult).then_inc(job_free, count_of(job))

                def low(item, d):
                    g = item * STEPS + d
                    dve.wait_ge(ph_ready, after(g))
                    cols = slice(0, 2 * T - POOL_COLS)
                    nc.vector.tensor_tensor(pl[:, d % RING, cols], p32[:, d % 2, cols], ph[:, d % RING, cols],
                                            ALU.subtract).then_inc(pl_ready, 1)

                def gather(pair, item, c, h):
                    unit = 2 * item + h
                    par = c % 2
                    dve.wait_ge(av_done, after(unit * DUOS + DUOS - 1))
                    if c == 0:
                        if h == 0:
                            dve.wait_ge(out_norm, after(pair - 1))
                        for b in range(2):
                            i = nc.vector.tensor_copy(acc[:, h, b], O_view[:, b, :, 0:DH + 1])
                    else:
                        dve.wait_ge(corr_ready, corr_count(pair, c, h))
                        for q in range(QT):
                            i = nc.vector.scalar_tensor_tensor(
                                out=acc[:, h, q // 2, q % 2, :], in0=acc[:, h, q // 2, q % 2, :],
                                scalar=corr[:, par, h, q:q + 1], in1=O_view[:, q // 2, q % 2, 0:DH + 1],
                                op0=ALU.mult, op1=ALU.add)
                    i.then_inc(o_part, 1)
                    dve.wait_ge(o_part, unit + 1)
                    for b in range(2):
                        i = nc.vector.tensor_tensor(acc[:, h, b, :, 0:DH], acc[:, h, b, :, 0:DH],
                                                    O_view[:, b, :, DH + 1:VW], ALU.add)
                    i.then_inc(o_free, 1)

                def finish_pair(pair, item):
                    dve.wait_ge(o_free, after(2 * item + 1))
                    nc.vector.reciprocal(rec[:], acc[:, :, :, :, DH]).then_inc(out_rec, 1)

                def step(p, s, last):
                    pair, c, d, item, nxt = where(p, s, last)
                    if s >= 1:
                        _, _, d1, item1, _ = where(p, s - 1, last)
                        low(item1, d1)
                    if nxt is not None and nxt < 2 and d == 0:
                        q_low(2 * pair + (3 if nxt == 0 else 2), nxt)
                    if nxt == 0 and d == 0:
                        w_low(1, pair + 1)
                    jobs = list(jobs_of(p, s, last))
                    lead = 2 if jobs and jobs[0][2][0] in "KV" else 1
                    for j in jobs[:lead]:
                        drain(*j)
                    if d == DUOS + LAG - 1:
                        gather(pair, item, c, 0)
                    if d == LAG - 1 and s >= STEPS:
                        pair0, c0, _, item0, _ = where(p, s - STEPS, last)
                        gather(pair0, item0, c0, 1)
                        if c0 == NCHUNK - 1:
                            finish_pair(pair0, item0)
                    for j in jobs[lead:]:
                        drain(*j)
                    if nxt == NCHUNK - 1 and d == WK_STEP and not last:
                        w_low(0, pair + 1)

                def finish():
                    item = PAIRS * NCHUNK - 1
                    low(item, STEPS - 1)
                    gather(PAIRS - 1, item, NCHUNK - 1, 1)
                    finish_pair(PAIRS - 1, item)

                for s, n in ((pl_ready, 0), (o_free, 0), (job_free, LATE)):
                    dve.sem_inc(s, HEAD + n)
                w_low(0, 0)
                w_low(1, 0)
                for job in EARLY:
                    if job == Q_BEFORE:
                        q_low(1, 0)
                    n = FIRST_NUMBER[job]
                    drain(n, n % FIRST_BANKS, job, 0, 0, 0)
                run_pairs(dve, step, finish)


def rope_constants():
    inv = (np.float32(1.0) / np.float32(10000.0) ** (np.arange(0, DS, 2, dtype=np.float32) / np.float32(DS)))
    angle = np.outer(np.arange(T, dtype=np.float32), inv.astype(np.float32)).astype(np.float32)
    angle = np.concatenate([angle, angle], axis=-1).T
    turn = np.zeros((P, P), np.float32)
    for n in range(P):
        d = n % DS
        if d < DS // 2:
            turn[n + DS // 2, n] = -1.0
        else:
            turn[n - DS // 2, n] = 1.0
    tile4 = lambda t: np.ascontiguousarray(np.tile(t, (P // DS, 1)).astype(np.float32))
    return tile4(np.cos(angle)), tile4(np.sin(angle)), turn


def self_attention(nc, a, keep):
    with ExitStack() as ctx:
        sb = lambda name, shape, dt=F32: ctx.enter_context(nc.sbuf_tensor(name, shape, dt))
        sem = lambda name: ctx.enter_context(nc.semaphore(name))
        ident = keep.ident
        o_all, wo_x, bo, x, xn = keep.o_all, keep.wo_x, keep.bo, keep.x, keep.xn
        xT = sb("xT", [P, DT, T])
        w_at = {"Wq": keep.w_q, "Wk": keep.w_k, "Wv": keep.w_v, "Wo": keep.w_o}
        cos, sin, turn = keep.cos, keep.sin, keep.turn
        causal, big_ident = sb("causal", [P, P], F16), sb("big_ident", [P, P], F16)
        qk = sb("qk", [P, 2 * DT, T])
        r0, r1 = sb("r0", [P, T]), sb("r1", [P, T])
        halves = sb("qk_halves", [P, 2, 2, T], F16)
        QS = sb("qs", [P, HS, T], F16)
        KS = sb("ks", [P, HS, T], F16)
        V = sb("v_halves", [P, QT, HS, 2 * DS + 1], F16)
        p32 = sb("p32_s", [P, 2, P_COLS])
        ph, pl = sb("ph_s", [P, 2, P_COLS], F16), sb("pl_s", [P, 2, P_COLS], F16)
        ln_p = sb("ln_p_s", [P, 1])
        mx, m16 = sb("mx", [P, HS, QT]), sb("m16_s", [P, HS, QT], F16)
        orec = sb("orec", [P, 2, QT])
        stats, mv = sb("stats_t", [P, QT, 6]), sb("mv_t", [P, QT, 2])
        rs = sb("rs_t", [P, 7, QT])
        bank = [ctx.enter_context(nc.psum_tensor(f"bank{i}", [P, 512], F32)) for i in range(8)]
        oT = o_all.rearrange("p a t n -> p a (t n)")
        o_att = xn

        loaded, o_loaded = keep.loaded, keep.o_loaded
        masks_loaded = sem("masks_loaded")
        o_turned, o_turned_out, y_ready, x1_ready = sem("o_turned"), sem("o_turned_out"), sem("y_ready"), sem("x1_ready")
        ln_step, root = sem("ln_step1"), sem("root1")
        x_turned, x_turned_out = sem("x_turned"), sem("x_turned_out")
        proj, proj_out, rotated, rope_step, rope_done = (sem("proj"), sem("proj_out"), sem("rotated"),
                                                         sem("rope_step"), sem("rope_done"))
        act_spread, dve_spread = sem("act_spread"), sem("dve_spread")
        hi_made, lo_made, spread_out = sem("hi_made"), sem("lo_made"), [sem("q_spread"), sem("k_spread")]
        SPREAD = 16 * (P // DS)
        v_ready, v_hi, v_out, small_set = sem("v_ready"), sem("v_hi"), sem("v_out"), sem("small_set")
        s_ready, s_max, m_ready, r_ready, row_set = (sem("s_ready"), sem("s_max"), sem("m_ready_s"), sem("r_ready"),
                                                     sem("row_set"))
        st_ready, s_exp, s_high, s_low, s_low_pool = (sem("st_ready"), sem("s_exp"), sem("s_high"), sem("s_low"),
                                                      sem("s_low_pool"))
        av_ready, s_rec, s_norm = sem("av_ready"), sem("s_rec"), sem("s_norm")
        a_turned, a_turned_out = sem("a_turned"), sem("a_turned_out")
        z_ready, x2_ready = sem("z_ready"), sem("x2_ready")

        S_AT = {3: (0, 0), 2: (1, 0), 0: (1, 384), 1: (2, 0)}
        T_AT = {0: (3, 0), 1: (4, 0), 3: (4, 384), 2: (5, 0)}
        P_AT = {k: (b - 3) * 512 + o for k, (b, o) in T_AT.items()}
        POOL_AT = P_COLS - 512

        def stacked(w):
            return QS if w == "Wq" else KS

        HI_ROW, LO_ROW = {"Wq": 1, "Wk": 2}, {"Wq": 2, "Wk": 1}
        TILES = [(w, m, m + (DT if w == "Wk" else 0)) for m in range(DT) for w in ("Wq", "Wk")]

        with nc.Block() as block:

            @block.sync
            def _(sp):
                for t, n in ((causal, "causal"), (big_ident, "big_ident")):
                    sp.dma_start(t[:], a[n]).then_inc(masks_loaded, 16)
                for n, (w, m, _) in enumerate(TILES):
                    sp.wait_ge(hi_made, n + 1)
                    for j in range(P // DS):
                        sp.dma_start(stacked(w)[0:DS, m * (P // DS) + j, :],
                                     halves[j * DS:(j + 1) * DS, n % 2, 0, :]).then_inc(spread_out[n % 2], 16)

            @block.gpsimd
            def _(pool):
                nc.gpsimd.memset(ln_p[:], math.log(P_SCALE)).then_inc(small_set, 1)
                nc.gpsimd.memset(V[:, :, :, DS:DS + 1], KV_SCALE).then_inc(small_set, 1)
                pool.wait_ge(small_set, 2)
                nc.gpsimd.memset(KS[3 * DS:3 * DS + 1], M_UNIT).then_inc(small_set, 1)
                pool.wait_ge(small_set, 3)
                for n in range(HS):
                    pool.wait_ge(s_high, n + 1)
                    if n >= 2:
                        pool.wait_ge(av_ready, n - 1)
                    nc.gpsimd.tensor_tensor(pl[:, n % 2, POOL_AT:], p32[:, n % 2, POOL_AT:], ph[:, n % 2, POOL_AT:],
                                            ALU.subtract).then_inc(s_low_pool, 1)

            @block.tensor
            def _(pe):
                for n in range(PAIRS):
                    pe.wait_ge(o_loaded[n], 16)
                    if n >= 4:
                        pe.wait_ge(o_turned_out, n - 3)
                    for t in range(QT):
                        i = nc.tensor.transpose(bank[n % 4][:, t * P:(t + 1) * P], o_all[:, n, t, :], ident[:])
                    i.then_inc(o_turned, 1)
                pe.wait_ge(loaded["wo_x"], 16)
                pe.wait_ge(o_turned_out, PAIRS)
                for t in range(QT):
                    for k in range(PAIRS):
                        i = nc.tensor.matmul(bank[4 + t][:], oT[:, k, t * P:(t + 1) * P], wo_x[:, k, :],
                                             start=(k == 0), stop=(k == PAIRS - 1))
                    i.then_inc(y_ready, 1)
                pe.wait_ge(ln_step, LN_DONE)
                for d in range(DT):
                    for t in range(QT):
                        i = nc.tensor.transpose(bank[d][:, t * P:(t + 1) * P], xn[:, t, d * P:(d + 1) * P], ident[:])
                    i.then_inc(x_turned, 1)
                pe.wait_ge(x_turned_out, DT)
                for n, (name, m, _) in enumerate(TILES):
                    if m == 0:
                        pe.wait_ge(loaded[name], 16)
                        pe.wait_ge(loaded["rope"], 48)
                    if n >= 4:
                        pe.wait_ge(rope_done, n - 3)
                    for k in range(DT):
                        i = nc.tensor.matmul(bank[4 + n % 4][:], w_at[name][:, k, m * P:(m + 1) * P], xT[:, k, :],
                                             start=(k == 0), stop=(k == DT - 1))
                    i.then_inc(proj, 1)
                    if n >= 1:
                        pe.wait_ge(proj_out, n)
                        nc.tensor.matmul(bank[(n - 1) % 4][:], turn[:], qk[:, TILES[n - 1][2], :], start=True,
                                         stop=True).then_inc(rotated, 1)
                pe.wait_ge(proj_out, 2 * DT)
                nc.tensor.matmul(bank[(2 * DT - 1) % 4][:], turn[:], qk[:, 2 * DT - 1, :], start=True,
                                 stop=True).then_inc(rotated, 1)
                pe.wait_ge(loaded["Wv"], 16)
                pe.wait_ge(rope_done, 2 * DT)
                for t in range(QT):
                    for k in range(DT):
                        i = nc.tensor.matmul(bank[4 + t][:], xT[:, k, t * P:(t + 1) * P], w_at["Wv"][:, k, :],
                                             start=(k == 0), stop=(k == DT - 1))
                    i.then_inc(v_ready, 1)
                pe.wait_ge(v_out, QT)

                def add(out, left, right, start, stop):
                    return nc.tensor.matmul(out, left, right, start=start, stop=stop, skip_group_check=True)

                def head_scores(n):
                    if n % (P // DS) == 0:
                        for s in spread_out:
                            pe.wait_ge(s, SPREAD * (n // (P // DS) + 1))
                        pe.wait_ge(act_spread, 2 * (n // (P // DS) + 1))
                        pe.wait_ge(dve_spread, 2 * (n // (P // DS) + 1))
                    if n >= 1:
                        pe.wait_ge(s_max, n)
                    for t in (3, 2, 0, 1):
                        b, o = S_AT[t]
                        add(bank[b][:, o:o + (t + 1) * P], QS[0:3 * DS, n, t * P:(t + 1) * P],
                            KS[0:3 * DS, n, 0:(t + 1) * P], o == 0, False)
                        i = add(bank[b][:, o + t * P:o + (t + 1) * P], big_ident[:], causal[:], False, True)
                    i.then_inc(s_ready, 1)

                def maximum_row(n):
                    pe.wait_ge(m_ready, n + 1)
                    if n >= 1:
                        pe.wait_ge(s_exp, n)
                    for t in range(QT):
                        i = add(bank[5][0:1, t * P:(t + 1) * P], m16[:, n, t:t + 1], keep.ident16[:], t == 0, True)
                    i.then_inc(r_ready, 1)

                def head_scores_turned(n):
                    pe.wait_ge(row_set, n + 1)
                    for k in (0, 1, 3, 2):
                        b, o = T_AT[k]
                        add(bank[b][:, o:o + T - k * P], KS[0:3 * DS + 1, n, k * P:(k + 1) * P],
                            QS[0:3 * DS + 1, n, k * P:T], o == 0, False)
                        i = add(bank[b][:, o:o + P], causal[:], big_ident[:], False, True)
                    i.then_inc(st_ready, 1)

                def weigh(n):
                    at = bank[6 + n % 2][:, 0:QT * (DS + 1)].rearrange("p (t n) -> p t n", n=DS + 1)
                    pe.wait_ge(s_low, n + 1)
                    pe.wait_ge(s_low_pool, n + 1)
                    if n >= 2:
                        pe.wait_ge(s_norm, n - 1)
                    for t in range(QT):
                        for k in range(t + 1):
                            cols = slice(P_AT[k] + (t - k) * P, P_AT[k] + (t - k + 1) * P)
                            first, final = t == 0 and k == 0, k == t
                            add(at[:, t, :], ph[:, n % 2, cols], V[:, k, n, 0:DS + 1], first, False)
                            add(at[:, t, 0:DS], ph[:, n % 2, cols], V[:, k, n, DS + 1:], False, False)
                            i = add(at[:, t, :], pl[:, n % 2, cols], V[:, k, n, 0:DS + 1], False, final)
                    i.then_inc(av_ready, 1)

                pe.wait_ge(small_set, 3)
                pe.wait_ge(masks_loaded, 32)
                head_scores(0)
                head_scores(1)
                maximum_row(0)
                head_scores_turned(0)
                for n in range(HS):
                    if n + 1 < HS:
                        maximum_row(n + 1)
                    if n + 2 < HS:
                        head_scores(n + 2)
                    if n + 1 < HS:
                        head_scores_turned(n + 1)
                    if n >= 1:
                        weigh(n - 1)
                weigh(HS - 1)
                pe.wait_ge(s_norm, HS)
                for k in range(DT):
                    for t in range(QT):
                        i = nc.tensor.transpose(bank[k][:, t * P:(t + 1) * P], o_att[:, t, k * P:(k + 1) * P],
                                                ident[:])
                    i.then_inc(a_turned, 1)
                pe.wait_ge(loaded["Wo"], 16)
                pe.wait_ge(a_turned_out, DT)
                for t in range(QT):
                    for k in range(DT):
                        i = nc.tensor.matmul(bank[4 + t][:], oT[:, k, t * P:(t + 1) * P], w_at["Wo"][:, k, :],
                                             start=(k == 0), stop=(k == DT - 1))
                    i.then_inc(z_ready, 1)

            @block.scalar
            def _(act):
                act.wait_ge(ln_step, LN_VAR)
                nc.scalar.activation(rs[:, 1, :], rs[:, 0, :], ACT.Sqrt).then_inc(root, 1)
                def high(n):
                    act.wait_ge(rope_done, n + 1)
                    if n >= 2:
                        act.wait_ge(spread_out[n % 2], SPREAD * (n // 2))
                        act.wait_ge(act_spread, n - 1)
                    nc.scalar.activation(halves[:, n % 2, 0, :], qk[:, TILES[n][2], :], ACT.Copy,
                                         scale=Q_SCALE).then_inc(hi_made, 1)
                    act.wait_ge(hi_made, n + 1)
                    w, m, _ = TILES[n]
                    for j in range(P // DS):
                        i = nc.scalar.activation(stacked(w)[HI_ROW[w] * DS:(HI_ROW[w] + 1) * DS, m * (P // DS) + j, :],
                                                 halves[j * DS:(j + 1) * DS, n % 2, 0, :], ACT.Copy)
                    i.then_inc(act_spread, 1)

                for n, (_, _, slot) in enumerate(TILES):
                    act.wait_ge(proj, n + 1)
                    nc.scalar.activation(qk[:, slot, :], bank[4 + n % 4][:], ACT.Copy).then_inc(proj_out, 1)
                    if n >= 1:
                        high(n - 1)
                high(2 * DT - 1)
                for t in range(QT):
                    act.wait_ge(v_ready, t + 1)
                    nc.scalar.activation(V[:, t, :, 0:DS], bank[4 + t].rearrange("p (h d) -> p h d", d=DS), ACT.Copy,
                                         scale=KV_SCALE).then_inc(v_hi, 1)

                def row(n):
                    act.wait_ge(r_ready, n + 1)
                    nc.scalar.activation(QS[3 * DS:3 * DS + 1, n, :], bank[5][0:1, :], ACT.Copy,
                                         scale=-1.0).then_inc(row_set, 1)

                def exps(n):
                    act.wait_ge(st_ready, n + 1)
                    if n >= 2:
                        act.wait_ge(s_low, n - 1)
                        act.wait_ge(s_low_pool, n - 1)
                    for b in range(3):
                        cols = slice(b * 512, min((b + 1) * 512, P_COLS))
                        i = nc.scalar.activation(p32[:, n % 2, cols], bank[3 + b][:, 0:cols.stop - cols.start], ACT.Exp,
                                                 bias=ln_p[:], scale=1.0 / (Q_SCALE * Q_SCALE * math.sqrt(DS)))
                    i.then_inc(s_exp, 1)

                act.wait_ge(small_set, 3)
                row(0)
                exps(0)
                for n in range(HS):
                    if n + 1 < HS:
                        row(n + 1)
                    if n >= 2:
                        act.wait_ge(av_ready, n - 1)
                    act.wait_ge(s_exp, n + 1)
                    nc.scalar.activation(ph[:, n % 2, :], p32[:, n % 2, :], ACT.Copy).then_inc(s_high, 1)
                    if n + 1 < HS:
                        exps(n + 1)

            @block.vector
            def _(dve):
                for n in range(PAIRS):
                    dve.wait_ge(o_turned, n + 1)
                    nc.vector.tensor_copy(oT[:, n, :], bank[n % 4][:]).then_inc(o_turned_out, 1)
                dve.wait_ge(loaded["x"], 16)
                dve.wait_ge(loaded["bo"], 16)
                for t in range(QT):
                    i = nc.vector.tensor_tensor(x[:, t, :], x[:, t, :], bo[:], ALU.add)
                i.then_inc(x1_ready, 1)
                dve.wait_ge(x1_ready, 1)
                for t in range(QT):
                    dve.wait_ge(y_ready, t + 1)
                    nc.vector.tensor_tensor(x[:, t, :], x[:, t, :], bank[4 + t][:], ALU.add).then_inc(x1_ready, 1)
                layer_norm_rows(nc, dve, x, xn, stats, mv, rs, ln_step, root, lambda t: (x1_ready, t + 2))
                for d in range(DT):
                    dve.wait_ge(x_turned, d + 1)
                    nc.vector.tensor_copy(xT[:, d, :], bank[d][:]).then_inc(x_turned_out, 1)
                def low(n):
                    dve.wait_ge(hi_made, n + 1)
                    nc.vector.scalar_tensor_tensor(out=halves[:, n % 2, 1, :], in0=qk[:, TILES[n][2], :],
                                                   scalar=Q_SCALE, in1=halves[:, n % 2, 0, :], op0=ALU.mult,
                                                   op1=ALU.subtract).then_inc(lo_made, 1)
                    dve.wait_ge(lo_made, n + 1)
                    w, m, _ = TILES[n]
                    for j in range(P // DS):
                        i = nc.vector.tensor_copy(stacked(w)[LO_ROW[w] * DS:(LO_ROW[w] + 1) * DS, m * (P // DS) + j, :],
                                                  halves[j * DS:(j + 1) * DS, n % 2, 1, :])
                    i.then_inc(dve_spread, 1)

                for n, (_, _, slot) in enumerate(TILES):
                    dve.wait_ge(rotated, n + 1)
                    if n >= 1:
                        dve.wait_ge(rope_done, n)
                    nc.vector.tensor_tensor(r0[:], bank[n % 4][:], sin[:], ALU.mult).then_inc(rope_step, 1)
                    nc.vector.tensor_tensor(r1[:], qk[:, slot, :], cos[:], ALU.mult).then_inc(rope_step, 1)
                    dve.wait_ge(rope_step, 2 * n + 2)
                    nc.vector.tensor_tensor(qk[:, slot, :], r0[:], r1[:], ALU.add).then_inc(rope_done, 1)
                    if n >= 1:
                        low(n - 1)
                low(2 * DT - 1)
                for t in range(QT):
                    dve.wait_ge(v_hi, t + 1)
                    nc.vector.scalar_tensor_tensor(
                        out=V[:, t, :, DS + 1:], in0=bank[4 + t].rearrange("p (h d) -> p h d", d=DS), scalar=KV_SCALE,
                        in1=V[:, t, :, 0:DS], op0=ALU.mult, op1=ALU.subtract).then_inc(v_out, 1)

                def maxima(n):
                    dve.wait_ge(s_ready, n + 1)
                    for t in range(QT):
                        b, o = S_AT[t]
                        i = nc.vector.tensor_reduce(mx[:, n, t:t + 1], bank[b][:, o:o + (t + 1) * P], X_AXIS, ALU.max)
                    i.then_inc(s_max, 1)
                    dve.wait_ge(s_max, n + 1)
                    nc.vector.tensor_scalar(m16[:, n, :], mx[:, n, :], 1.0 / M_UNIT, None, ALU.mult).then_inc(m_ready, 1)

                def norm(n):
                    at = bank[6 + n % 2][:, 0:QT * (DS + 1)].rearrange("p (t n) -> p t n", n=DS + 1)
                    dve.wait_ge(av_ready, n + 1)
                    nc.vector.reciprocal(orec[:, n % 2, :], at[:, :, DS]).then_inc(s_rec, 1)
                    dve.wait_ge(s_rec, n + 1)
                    nc.vector.tensor_tensor(o_att[:, :, n * DS:(n + 1) * DS], at[:, :, 0:DS],
                                            orec[:, n % 2, :].unsqueeze(2).to_broadcast([P, QT, DS]),
                                            ALU.mult).then_inc(s_norm, 1)

                maxima(0)
                maxima(1)
                for n in range(HS):
                    if n + 2 < HS:
                        maxima(n + 2)
                    dve.wait_ge(s_high, n + 1)
                    nc.vector.tensor_tensor(pl[:, n % 2, 0:POOL_AT], p32[:, n % 2, 0:POOL_AT], ph[:, n % 2, 0:POOL_AT],
                                            ALU.subtract).then_inc(s_low, 1)
                    if n >= 1:
                        norm(n - 1)
                norm(HS - 1)
                for k in range(DT):
                    dve.wait_ge(a_turned, k + 1)
                    nc.vector.tensor_copy(oT[:, k, :], bank[k][:]).then_inc(a_turned_out, 1)
                for t in range(QT):
                    dve.wait_ge(z_ready, t + 1)
                    nc.vector.tensor_tensor(x[:, t, :], x[:, t, :], bank[4 + t][:], ALU.add).then_inc(x2_ready, 1)
                dve.wait_ge(x2_ready, QT)


def experts(nc, a, keep, out):
    with ExitStack() as ctx:
        sb = lambda name, shape, dt=F32: ctx.enter_context(nc.sbuf_tensor(name, shape, dt))
        sem = lambda name: ctx.enter_context(nc.semaphore(name))
        HT = H // P
        ident = keep.ident
        x, xn, xT = keep.x, keep.xn, keep.xT
        w_raw = [keep.w_in, keep.w_out]
        w_in, w_out = (sb(n, [P, 2, 2, DT, H], F16) for n in ("w_in_halves", "w_out_halves"))
        halves = [w_in, w_out]
        xh = sb("xT_halves", [P, 2, DT, T], F16)
        hT = sb("hT", [P, HT, T])
        hh = sb("hT_halves", [P, 2, 2, HT, T], F16)
        gate_s = sb("gate_s", [P, QT, E])
        b_in = sb("b_in", [P, E * HT])
        b_out = sb("b_out", [E, D])
        router = sb("router", [P, DT, E])
        logits, probs = sb("logits", [P, QT, E]), sb("probs", [P, QT, E])
        top, left, gate = sb("top", [P, QT, 8]), sb("left", [P, QT, E]), sb("gate", [P, QT, E])
        lmax, lneg, lsum, lrec = (sb(n, [P, QT]) for n in ("lmax", "lneg", "lsum", "lrec"))
        gateT = sb("gateT", [E, T])
        stats, mv = sb("stats_e", [P, QT, 6]), sb("mv_e", [P, QT, 2])
        rs = sb("rs_e", [P, 7, QT])
        up = [ctx.enter_context(nc.psum_tensor(f"up{i}", [P, 512], F32)) for i in range(4)]
        down = [ctx.enter_context(nc.psum_tensor(f"down{i}", [P, 512], F32)) for i in range(4)]
        small_loaded = sem("small_loaded")
        in_loaded = [sem("in_loaded0"), sem("in_loaded1")]
        out_loaded = [sem("out_loaded0"), sem("out_loaded1")]
        ln_step, root = sem("ln_step2"), sem("root2")
        turned, turned_out = sem("turned2"), sem("turned2_out")
        lg_ready, lg_out, lg_step, lg_exp = sem("lg_ready"), sem("lg_out"), sem("lg_step"), sem("lg_exp")
        gates_ready, gates_turned, gates_out = sem("gates_ready"), sem("gates_turned"), sem("gates_out")
        up_ready, up_out, down_ready, down_out = sem("up_ready"), sem("up_out"), sem("down_ready"), sem("down_out")
        x_hi, x_split, h_made, h_hi, h_split = sem("x_hi"), sem("x_split"), sem("h_made"), sem("h_hi"), sem("h_split")
        w_hi, w_split = [sem("w_in_hi"), sem("w_out_hi")], [sem("w_in_split"), sem("w_out_split")]
        bias_ready, stored = sem("bias_ready"), sem("stored")

        with nc.Block() as block:

            @block.sync
            def _(sp):
                def load(e, b, wait):
                    for n, (w, s) in enumerate((("L0_ffn_w_in", in_loaded), ("L0_ffn_w_out", out_loaded))):
                        if wait:
                            sp.wait_ge(w_split[n], e - 1)
                        sp.dma_start(w_raw[n][:, b], a[w][one_of(e)].rearrange("e (k p) n -> p (e k) n", p=P)
                                     ).then_inc(s[b], 16)

                for t, s in ((router, a["L0_ffn_router_w"].rearrange("(k p) n -> p k n", p=P)),
                             (b_in, a["b_in_columns"]), (b_out, a["L0_ffn_b_out"])):
                    sp.dma_start(t[:], s).then_inc(small_loaded, 16)
                load(0, 0, False)
                load(1, 1, False)
                with sp.Fori(1, E // 2) as e2:
                    load(e2 * 2, 0, True)
                    load(e2 * 2 + 1, 1, True)
                sp.wait_ge(down_out, QT * (E + 1))
                sp.dma_start(out[0].rearrange("(t p) d -> p t d", p=P), x[:]).then_inc(stored, 16)
                sp.wait_ge(stored, 16)

            @block.tensor
            def _(pe):
                pe.wait_ge(ln_step, LN_DONE)
                for d in range(DT):
                    for t in range(QT):
                        i = nc.tensor.transpose(up[d][:, t * P:(t + 1) * P], xn[:, t, d * P:(d + 1) * P], ident[:])
                    i.then_inc(turned, 1)
                pe.wait_ge(small_loaded, 48)
                pe.wait_ge(turned_out, DT)
                for t in range(QT):
                    for k in range(DT):
                        i = nc.tensor.matmul(down[0][:, t * E:(t + 1) * E], xT[:, k, t * P:(t + 1) * P], router[:, k, :],
                                             start=(k == 0), stop=(k == DT - 1))
                i.then_inc(lg_ready, 1)

                PARTS = ((0, 0), (0, 1), (1, 0))

                def up_one(e, b, first=False):
                    pe.wait_ge(w_split[0], e + 1)
                    for m in range(HT):
                        if not first:
                            pe.wait_ge(up_out, HT * (e - 1) + m + 1)
                        for k in range(DT):
                            for w, z in PARTS:
                                i = nc.tensor.matmul(up[m][:], w_in[:, b, w, k, m * P:(m + 1) * P], xh[:, z, k, :],
                                                     start=(k == 0 and (w, z) == PARTS[0]),
                                                     stop=(k == DT - 1 and (w, z) == PARTS[-1]))
                        i.then_inc(up_ready, 1)

                pe.wait_ge(x_split, DT)
                up_one(0, 0, first=True)
                pe.wait_ge(gates_ready, 1)
                for t in range(QT):
                    i = nc.tensor.transpose(down[0][0:E, t * P:(t + 1) * P], gate[:, t, :], ident[:])
                i.then_inc(gates_turned, 1)
                pe.wait_ge(gates_out, 1)
                for t in range(QT):
                    nc.tensor.matmul(down[t][:], gateT[:, t * P:(t + 1) * P], b_out[:], start=True,
                                     stop=True).then_inc(bias_ready, 1)

                def down_one(e, b):
                    pe.wait_ge(h_split, HT * (e + 1))
                    pe.wait_ge(w_split[1], e + 1)
                    for t in range(QT):
                        pe.wait_ge(down_out, QT * e + t + 1)
                        for k in range(HT):
                            for z, w in PARTS:
                                i = nc.tensor.matmul(down[t][:], hh[:, b, z, k, t * P:(t + 1) * P],
                                                     w_out[:, b, w, k, :], start=(k == 0 and (z, w) == PARTS[0]),
                                                     stop=(k == HT - 1 and (z, w) == PARTS[-1]))
                        i.then_inc(down_ready, 1)

                def two(e2, last):
                    e = e2 * 2
                    up_one(e + 1, 1)
                    down_one(e, 0)
                    if not last:
                        up_one(e + 2, 0)
                    down_one(e + 1, 1)

                with pe.Fori(0, E // 2 - 1) as e2:
                    two(e2, False)
                two(E // 2 - 1, True)

            @block.scalar
            def _(act):
                def w_high(n, e, b, wait):
                    act.wait_ge((in_loaded, out_loaded)[n][b], 8 * (e - b) + 16)
                    if wait:
                        act.wait_ge((up_ready, down_ready)[n], HT * (e - 1))
                    nc.scalar.activation(halves[n][:, b, 0], w_raw[n][:, b], ACT.Copy, scale=W_SCALE).then_inc(w_hi[n], 1)

                act.wait_ge(ln_step, LN_VAR)
                nc.scalar.activation(rs[:, 1, :], rs[:, 0, :], ACT.Sqrt).then_inc(root, 1)
                w_high(0, 0, 0, False)
                for d in range(DT):
                    act.wait_ge(turned_out, d + 1)
                    nc.scalar.activation(xh[:, 0, d, :], xT[:, d, :], ACT.Copy, scale=CTX_SCALE).then_inc(x_hi, 1)
                act.wait_ge(lg_step, 3)
                for t in range(QT):
                    i = nc.scalar.activation(probs[:, t, :], logits[:, t, :], ACT.Exp, bias=lneg[:, t:t + 1], scale=1.0,
                                             accum_out=lsum[:, t:t + 1])
                i.then_inc(lg_exp, 1)
                w_high(0, 1, 1, False)
                w_high(1, 0, 0, False)

                def gelu(e, b, first):
                    for m in range(HT):
                        act.wait_ge(up_ready, HT * e + m + 1)
                        if not (isinstance(e, int) and e == 0):
                            act.wait_ge(h_split, HT * (e - 1) + m + 1)
                        nc.scalar.activation(hT[:, m, :], up[m][:], ACT.Gelu_apprx_tanh,
                                             bias=b_in[:, e * HT + m:e * HT + m + 1] if isinstance(e, int)
                                             else b_in[:, bass.ds(e * HT + m, 1)],
                                             scale=1.0 / (CTX_SCALE * W_SCALE)).then_inc(up_out, 1)
                        if not first:
                            act.wait_ge(down_ready, QT * (e - 1))
                        act.wait_ge(up_out, HT * e + m + 1)
                        nc.scalar.activation(hh[:, b, 0, m, :], hT[:, m, :], ACT.Copy, scale=H_SCALE).then_inc(h_hi, 1)

                def expert(e, b, first=False, has=(True, True)):
                    gelu(e, b, first)
                    if has[0]:
                        w_high(0, e + 2, b, True)
                    if has[1]:
                        w_high(1, e + 1, 1 - b, not (isinstance(e, int) and e == 0))

                act.wait_ge(small_loaded, 48)
                expert(0, 0, True)
                expert(1, 1, True)
                with act.Fori(1, E // 2 - 1) as e2:
                    expert(e2 * 2, 0)
                    expert(e2 * 2 + 1, 1)
                expert(E - 2, 0, has=(False, True))
                expert(E - 1, 1, has=(False, False))

            @block.vector
            def _(dve):
                def w_low(n, e, b):
                    dve.wait_ge(w_hi[n], e + 1)
                    nc.vector.scalar_tensor_tensor(out=halves[n][:, b, 1], in0=w_raw[n][:, b], scalar=W_SCALE,
                                                   in1=halves[n][:, b, 0], op0=ALU.mult,
                                                   op1=ALU.subtract).then_inc(w_split[n], 1)

                layer_norm_rows(nc, dve, x, xn, stats, mv, rs, ln_step, root)
                for d in range(DT):
                    dve.wait_ge(turned, d + 1)
                    nc.vector.tensor_copy(xT[:, d, :], up[d][:]).then_inc(turned_out, 1)
                w_low(0, 0, 0)
                for d in range(DT):
                    dve.wait_ge(x_hi, d + 1)
                    nc.vector.scalar_tensor_tensor(out=xh[:, 1, d, :], in0=xT[:, d, :], scalar=CTX_SCALE,
                                                   in1=xh[:, 0, d, :], op0=ALU.mult,
                                                   op1=ALU.subtract).then_inc(x_split, 1)
                dve.wait_ge(lg_ready, 1)
                nc.vector.tensor_copy(logits[:], down[0][:, 0:QT * E].rearrange("p (t e) -> p t e", e=E)
                                      ).then_inc(lg_step, 1)
                dve.wait_ge(lg_step, 1)
                nc.vector.tensor_reduce(lmax[:], logits[:], X_AXIS, ALU.max).then_inc(lg_step, 1)
                dve.wait_ge(lg_step, 2)
                nc.vector.tensor_scalar(lneg[:], lmax[:], -1.0, None, ALU.mult).then_inc(lg_step, 1)
                dve.wait_ge(lg_exp, 1)
                nc.vector.reciprocal(lrec[:], lsum[:]).then_inc(lg_step, 1)
                dve.wait_ge(lg_step, 4)
                for t in range(QT):
                    i = nc.vector.tensor_scalar(probs[:, t, :], probs[:, t, :], lrec[:, t:t + 1], None, ALU.mult)
                i.then_inc(lg_step, 1)
                dve.wait_ge(lg_step, 5)
                for t in range(QT):
                    i = nc.vector.max(top[:, t, :], probs[:, t, :])
                i.then_inc(lg_step, 1)
                dve.wait_ge(lg_step, 6)
                nc.vector.memset(top[:, :, 2:8], -1.0).then_inc(lg_step, 1)
                dve.wait_ge(lg_step, 7)
                for t in range(QT):
                    i = nc.vector.match_replace(left[:, t, :], top[:, t, :], probs[:, t, :], 0.0)
                i.then_inc(lg_step, 1)
                dve.wait_ge(lg_step, 8)
                nc.vector.tensor_tensor(gate[:], probs[:], left[:], ALU.subtract).then_inc(gates_ready, 1)
                dve.wait_ge(gates_ready, 1)
                nc.vector.tensor_scalar(gate_s[:], gate[:], 1.0 / (H_SCALE * W_SCALE), None,
                                        ALU.mult).then_inc(gates_ready, 1)
                w_low(0, 1, 1)
                w_low(1, 0, 0)
                dve.wait_ge(gates_turned, 1)
                nc.vector.tensor_copy(gateT[:], down[0][0:E, :]).then_inc(gates_out, 1)
                for t in range(QT):
                    dve.wait_ge(bias_ready, t + 1)
                    nc.vector.tensor_tensor(x[:, t, :], x[:, t, :], down[t][:], ALU.add).then_inc(down_out, 1)

                def add(e):
                    column = slice(e, e + 1) if isinstance(e, int) else bass.ds(e, 1)
                    for t in range(QT):
                        dve.wait_ge(down_ready, QT * e + t + 1)
                        dve.wait_ge(down_out, QT * e + t + 1)
                        nc.vector.scalar_tensor_tensor(out=x[:, t, :], in0=down[t][:], scalar=gate_s[:, t, column],
                                                       in1=x[:, t, :], op0=ALU.mult, op1=ALU.add).then_inc(down_out, 1)

                def expert(e, b, has=(True, True)):
                    for m in range(HT):
                        dve.wait_ge(h_hi, HT * e + m + 1)
                        nc.vector.scalar_tensor_tensor(out=hh[:, b, 1, m, :], in0=hT[:, m, :], scalar=H_SCALE,
                                                       in1=hh[:, b, 0, m, :], op0=ALU.mult,
                                                       op1=ALU.subtract).then_inc(h_split, 1)
                    if has[0]:
                        w_low(0, e + 2, b)
                    if not (isinstance(e, int) and e == 0):
                        add(e - 1)
                    if has[1]:
                        w_low(1, e + 1, 1 - b)

                expert(0, 0)
                expert(1, 1)
                with dve.Fori(1, E // 2 - 1) as e2:
                    expert(e2 * 2, 0)
                    expert(e2 * 2 + 1, 1)
                expert(E - 2, 0, has=(False, True))
                expert(E - 1, 1, has=(False, False))
                add(E - 1)


class Kept:
    pass


def carve(store, *shapes):
    views, at = [], 0
    for shape in shapes:
        size = math.prod(shape)
        axes = "abc"[:len(shape)]
        view = store[:, at:at + size].rearrange(f"p ({' '.join(axes)}) -> p {' '.join(axes)}",
                                                **dict(zip(axes[1:], shape[1:])))
        views.append(view)
        at += size
    return views


def build(nc, a, out):
    dram, keep = Kept(), Kept()
    dram.q = nc.dram_tensor("q_by_pair", (PAIRS, P, T), F32).ap()
    dram.o = nc.dram_tensor("o_by_pair", (PAIRS, P, QT * P), F32).ap()
    with ExitStack() as ctx:
        keep.ident = ctx.enter_context(nc.sbuf_tensor("ident", [P, P], F32))
        keep.ident16 = ctx.enter_context(nc.sbuf_tensor("ident16", [P, P], F16))
        store = ctx.enter_context(nc.sbuf_tensor("store", [P, CT * NKEY], F32))
        keep.ctx = store[:].bitcast(F16).rearrange("p (s k n) -> p s k n", s=2, k=CT)
        keep.x, keep.wo_x, keep.w_q, keep.w_k, keep.w_v, keep.w_o, keep.bo, keep.cos, keep.sin, keep.turn, keep.o_all, \
            keep.xn = carve(store, (QT, D), (PAIRS, D), *[(DT, D)] * 4, (D,), (T,), (T,), (P,), (PAIRS, QT, P), (QT, D))
        _, keep.w_in, keep.w_out, keep.xT = carve(store, (QT + PAIRS, D), (2, DT, H), (2, H // P, D), (DT, T))
        names = ("wo_x", "x", "bo", "Wq", "Wk", "Wv", "Wo", "rope")
        keep.loaded = {n: ctx.enter_context(nc.semaphore(f"loaded_{n}")) for n in names}
        keep.o_loaded = [ctx.enter_context(nc.semaphore(f"o_loaded{n}")) for n in range(PAIRS)]
        prologue(nc, a, dram, keep)
        cross_attention(nc, a, dram, keep)
        self_attention(nc, a, keep)
        experts(nc, a, keep, out)


def kernel(**inputs):
    import concourse.bacc as bacc
    from concourse.bass_utils import run_bass_kernel_spmd

    arrays = {}
    for name in ("x", "L0_xattn_Wq", "L0_xattn_Wo", "L0_xattn_bo", "L0_ffn_router_w", "L0_ffn_w_in", "L0_ffn_w_out",
                 "L0_ffn_b_out"):
        arrays[name] = np.ascontiguousarray(inputs[name])
    arrays["ctxT"] = np.ascontiguousarray(np.asarray(inputs["ctx_768"])[0].T)
    for name in ("Wk", "Wv"):
        w = np.asarray(inputs[f"L0_xattn_{name}"]).reshape(CT, P, PAIRS, P)
        arrays[f"{name.lower()}_pairs"] = np.ascontiguousarray(w.transpose(2, 1, 0, 3)).reshape(PAIRS, P, CT * P)
    for name in ("Wq", "Wk", "Wv", "Wo"):
        arrays[f"attn_{name}T"] = np.ascontiguousarray(np.asarray(inputs[f"L0_attn_{name}"]).T)
    b_in = np.asarray(inputs["L0_ffn_b_in"]).reshape(E, H // P, P)
    arrays["b_in_columns"] = np.ascontiguousarray(b_in.transpose(2, 0, 1)).reshape(P, E * (H // P))
    arrays["rope_cos"], arrays["rope_sin"], arrays["rope_turn"] = rope_constants()
    arrays["causal"] = np.where(np.arange(P)[None, :] > np.arange(P)[:, None], -MASKED, 0.0).astype(np.float16)
    arrays["big_ident"] = (np.eye(P) * MASKED).astype(np.float16)

    nc = bacc.Bacc("TRN2", target_bir_lowering=False, num_devices=1)
    a = {n: nc.dram_tensor(f"in_{n}", v.shape, mybir.dt.from_np(v.dtype), kind="ExternalInput").ap()
         for n, v in arrays.items()}
    out = nc.dram_tensor("out_0", (1, T, D), F32, kind="ExternalOutput").ap()
    build(nc, a, out)
    r = run_bass_kernel_spmd(nc, [{f"in_{n}": v for n, v in arrays.items()}], core_ids=[0])
    return r.results[0]["out_0"]
```
